# Optimizing a Trainium2 kernel written in Bass

```python
import numpy as np
import jax
import jax.numpy as jnp

def _softmax(x, axis=-1):
    return jax.nn.softmax(x, axis=axis)

def _gelu(x):
    return jax.nn.gelu(x, approximate=True)

def _silu(x):
    return jax.nn.silu(x)

def _sigmoid(x):
    return jax.nn.sigmoid(x)

def _layernorm(x, axis=-1, eps=1e-05):
    m = jnp.mean(x, axis=axis, keepdims=True)
    v = jnp.var(x, axis=axis, keepdims=True)
    return (x - m) / jnp.sqrt(v + eps)

def _scatter_add(tgt, idx, src, axis=0):
    return tgt.at[idx].add(src)

def _segment_sum(src, seg, n):
    return jax.ops.segment_sum(src, seg, n)
kernel_name = 'mk_gnn_ffn_d2_gnn_r8_a59c07'

def setup_inputs(seed: int=0):
    np.random.seed(seed)
    _w = jnp.asarray

    def _rec_inputs():
        import jax
        import jax.numpy as jnp
        _gk = jax.random.key(seed)
        x = -0.0003713 + 1 * jax.random.normal(jax.random.fold_in(_gk, 1), (6250, 256), jnp.float32)
        _s = jax.random.randint(jax.random.fold_in(_gk, 2), (100000,), 0, 6250, jnp.int32)
        _d = jax.random.randint(jax.random.fold_in(_gk, 3), (100000,), 0, 6250, jnp.int32)
        _loop = jnp.arange(6250, dtype=jnp.int32)
        src = jnp.concatenate([_s, _d, _loop])
        dst = jnp.concatenate([_d, _s, _loop])
        _o = jnp.argsort(dst, stable=True)
        src = src[_o]
        dst = dst[_o]
        return (x, src, dst)
    x, src, dst = _rec_inputs()

    def _L0_gnn_setup():
        import jax, jax.numpy as jnp
        import numpy as np
        N_NODES = 6250
        N_EDGES = 312500
        WIDTH = 256
        LN_EPS = 1e-05

        def gcn_conv(x, edge_index, W, b):
            n = x.shape[0]
            loops = jnp.arange(n, dtype=edge_index.dtype)
            src = jnp.concatenate([edge_index[0], loops])
            dst = jnp.concatenate([edge_index[1], loops])
            deg = jax.ops.segment_sum(jnp.ones_like(dst, dtype=x.dtype), dst, num_segments=n)
            dinv = jnp.where(deg > 0, jax.lax.rsqrt(deg), 0.0)
            norm = dinv[src] * dinv[dst]
            h = x @ W.T
            msgs = norm[:, None] * h[src]
            out = jax.ops.segment_sum(msgs, dst, num_segments=n)
            return out + b

        def layer_norm(x, gamma, beta):
            mu = jnp.mean(x, axis=-1, keepdims=True)
            var = jnp.mean(jnp.square(x - mu), axis=-1, keepdims=True)
            return (x - mu) * jax.lax.rsqrt(var + LN_EPS) * gamma + beta
        key = jax.random.key(seed)
        k1, k2, k3, k4 = jax.random.split(key, 4)
        x = jax.random.normal(k1, (N_NODES, WIDTH), dtype=jnp.float32)
        edge_index = jax.random.randint(k2, (2, N_EDGES), 0, N_NODES, dtype=jnp.int64)
        W = jax.random.normal(k3, (WIDTH, WIDTH), dtype=jnp.float32) / np.sqrt(WIDTH)
        b = jax.random.normal(k4, (WIDTH,), dtype=jnp.float32) * 0.01
        gamma = jnp.ones((WIDTH,), dtype=jnp.float32)
        beta = jnp.zeros((WIDTH,), dtype=jnp.float32)
        return {'x': x, 'edge_index': edge_index, 'W': W, 'b': b, 'gamma': gamma, 'beta': beta}
    _L0_gnn_all = _L0_gnn_setup()
    _L0_gnn_in = {k: v for k, v in _L0_gnn_all.items() if k in ('W', 'b', 'gamma', 'beta')}
    del _L0_gnn_all

    def _L0_ffn_setup():
        import jax, jax.numpy as jnp
        import numpy as np
        NUM_EXPERTS = 8
        TOP_K = 2
        B, S, D = (8, 1024, 256)

        def _moe(tokens, router_w, w1, b1, w2, b2):
            N = tokens.shape[0]
            E = router_w.shape[0]
            logits = tokens.astype(jnp.float32) @ router_w.astype(jnp.float32).T
            probs = jax.nn.softmax(logits, axis=-1)
            rw, re = jax.lax.top_k(probs, TOP_K)
            if TOP_K > 1:
                rw = rw / jnp.maximum(rw.sum(-1, keepdims=True), 1e-12)
            rw = rw.astype(tokens.dtype)
            combine = jnp.zeros((N, E), tokens.dtype).at[jnp.arange(N)[:, None], re].set(rw)
            out = tokens
            for e in range(E):
                h = jax.nn.gelu(tokens @ w1[e] + b1[e], approximate=False)
                y = h @ w2[e] + b2[e]
                out = out + combine[:, e:e + 1] * y
            return out
        key = jax.random.key(seed)
        ks = jax.random.split(key, 4)
        scale = 1.0 / np.sqrt(D).astype(np.float32)
        return {'input_embeddings': jax.random.normal(ks[0], (B, S, D), jnp.float32), 'router_w': jax.random.normal(ks[1], (NUM_EXPERTS, D), jnp.float32) * scale, 'w1': jax.random.normal(ks[2], (NUM_EXPERTS, D, D), jnp.float32) * scale, 'b1': jnp.zeros((NUM_EXPERTS, D), jnp.float32), 'w2': jax.random.normal(ks[3], (NUM_EXPERTS, D, D), jnp.float32) * scale, 'b2': jnp.zeros((NUM_EXPERTS, D), jnp.float32)}
    _L0_ffn_all = _L0_ffn_setup()
    _L0_ffn_in = {k: v for k, v in _L0_ffn_all.items() if k in ('router_w', 'w1', 'b1', 'w2', 'b2')}
    del _L0_ffn_all

    def _L1_gnn_setup():
        import jax, jax.numpy as jnp
        import numpy as np
        N, DIM, H, C, E = (6250, 256, 4, 64, 100000)
        NEG_SLOPE = 0.2
        LN_EPS = 1e-05
        key = jax.random.key(seed)
        ks = jax.random.split(key, 8)
        x = jax.random.normal(ks[0], (N, DIM), dtype=jnp.float32)
        edge_index = jax.random.randint(ks[1], (2, E), 0, N, dtype=jnp.int64)
        W = jax.random.normal(ks[2], (DIM, H * C), dtype=jnp.float32) * (1.0 / np.sqrt(DIM))
        a_src = jax.random.normal(ks[3], (H, C), dtype=jnp.float32) * (1.0 / np.sqrt(C))
        a_dst = jax.random.normal(ks[4], (H, C), dtype=jnp.float32) * (1.0 / np.sqrt(C))
        bias_gat = jnp.zeros((DIM,), dtype=jnp.float32)
        W_res = jax.random.normal(ks[5], (DIM, DIM), dtype=jnp.float32) * (1.0 / np.sqrt(DIM))
        b_res = jnp.zeros((DIM,), dtype=jnp.float32)
        gamma = jnp.ones((DIM,), dtype=jnp.float32)
        beta = jnp.zeros((DIM,), dtype=jnp.float32)
        return {'x': x, 'edge_index': edge_index, 'W': W, 'a_src': a_src, 'a_dst': a_dst, 'bias_gat': bias_gat, 'W_res': W_res, 'b_res': b_res, 'gamma': gamma, 'beta': beta}
    _L1_gnn_all = _L1_gnn_setup()
    _L1_gnn_in = {k: v for k, v in _L1_gnn_all.items() if k in ('W', 'a_src', 'a_dst', 'bias_gat', 'W_res', 'b_res', 'gamma', 'beta')}
    del _L1_gnn_all

    def _L1_ffn_setup():
        import math
        import jax, jax.numpy as jnp
        import numpy as np
        CAPACITY_FACTOR = 1.25
        key = jax.random.key(seed)
        ks = jax.random.split(key, 5)
        B, L, D, F, E = (8, 1024, 256, 1024, 8)
        h = jax.random.normal(ks[0], (B, L, D), dtype=jnp.float32)
        gate_w = jax.random.normal(ks[1], (D, E), dtype=jnp.float32) * 0.02
        gate_b = jnp.zeros((E,), dtype=jnp.float32)
        w1 = jax.random.normal(ks[2], (E, D, F), dtype=jnp.float32) * (1.0 / math.sqrt(D))
        b1 = jnp.zeros((E, F), dtype=jnp.float32)
        w2 = jax.random.normal(ks[3], (E, F, D), dtype=jnp.float32) * (1.0 / math.sqrt(F))
        b2 = jnp.zeros((E, D), dtype=jnp.float32)
        return {'h': h, 'gate_w': gate_w, 'gate_b': gate_b, 'w1': w1, 'b1': b1, 'w2': w2, 'b2': b2}
    _L1_ffn_all = _L1_ffn_setup()
    _L1_ffn_in = {k: v for k, v in _L1_ffn_all.items() if k in ('gate_w', 'gate_b', 'w1', 'b1', 'w2', 'b2')}
    del _L1_ffn_all
    return {'x': x, 'src': src, 'dst': dst, 'L0_gnn_W': _L0_gnn_in['W'], 'L0_gnn_b': _L0_gnn_in['b'], 'L0_gnn_gamma': _L0_gnn_in['gamma'], 'L0_gnn_beta': _L0_gnn_in['beta'], 'L0_ffn_router_w': _L0_ffn_in['router_w'], 'L0_ffn_w1': _L0_ffn_in['w1'], 'L0_ffn_b1': _L0_ffn_in['b1'], 'L0_ffn_w2': _L0_ffn_in['w2'], 'L0_ffn_b2': _L0_ffn_in['b2'], 'L1_gnn_W': _L1_gnn_in['W'], 'L1_gnn_a_src': _L1_gnn_in['a_src'], 'L1_gnn_a_dst': _L1_gnn_in['a_dst'], 'L1_gnn_bias_gat': _L1_gnn_in['bias_gat'], 'L1_gnn_W_res': _L1_gnn_in['W_res'], 'L1_gnn_b_res': _L1_gnn_in['b_res'], 'L1_gnn_gamma': _L1_gnn_in['gamma'], 'L1_gnn_beta': _L1_gnn_in['beta'], 'L1_ffn_gate_w': _L1_ffn_in['gate_w'], 'L1_ffn_gate_b': _L1_ffn_in['gate_b'], 'L1_ffn_w1': _L1_ffn_in['w1'], 'L1_ffn_b1': _L1_ffn_in['b1'], 'L1_ffn_w2': _L1_ffn_in['w2'], 'L1_ffn_b2': _L1_ffn_in['b2']}

def reference(x, src, dst, L0_gnn_W, L0_gnn_b, L0_gnn_gamma, L0_gnn_beta, L0_ffn_router_w, L0_ffn_w1, L0_ffn_b1, L0_ffn_w2, L0_ffn_b2, L1_gnn_W, L1_gnn_a_src, L1_gnn_a_dst, L1_gnn_bias_gat, L1_gnn_W_res, L1_gnn_b_res, L1_gnn_gamma, L1_gnn_beta, L1_ffn_gate_w, L1_ffn_gate_b, L1_ffn_w1, L1_ffn_b1, L1_ffn_w2, L1_ffn_b2):
    import jax
    import jax.numpy as jnp

    def _L0_gnn_ref(x, edge_index, W, b, gamma, beta):
        import jax, jax.numpy as jnp
        import numpy as np
        N_NODES = 6250
        N_EDGES = 312500
        WIDTH = 256
        LN_EPS = 1e-05

        def gcn_conv(x, edge_index, W, b):
            n = x.shape[0]
            loops = jnp.arange(n, dtype=edge_index.dtype)
            src = jnp.concatenate([edge_index[0], loops])
            dst = jnp.concatenate([edge_index[1], loops])
            deg = jax.ops.segment_sum(jnp.ones_like(dst, dtype=x.dtype), dst, num_segments=n)
            dinv = jnp.where(deg > 0, jax.lax.rsqrt(deg), 0.0)
            norm = dinv[src] * dinv[dst]
            h = x @ W.T
            msgs = norm[:, None] * h[src]
            out = jax.ops.segment_sum(msgs, dst, num_segments=n)
            return out + b

        def layer_norm(x, gamma, beta):
            mu = jnp.mean(x, axis=-1, keepdims=True)
            var = jnp.mean(jnp.square(x - mu), axis=-1, keepdims=True)
            return (x - mu) * jax.lax.rsqrt(var + LN_EPS) * gamma + beta
        h = gcn_conv(x, edge_index, W, b)
        h = layer_norm(h, gamma, beta)
        h = jax.nn.relu(h)
        return h

    def _L0_ffn_ref(input_embeddings, router_w, w1, b1, w2, b2):
        import jax, jax.numpy as jnp
        import numpy as np
        NUM_EXPERTS = 8
        TOP_K = 2
        B, S, D = (8, 1024, 256)

        def _moe(tokens, router_w, w1, b1, w2, b2):
            N = tokens.shape[0]
            E = router_w.shape[0]
            logits = tokens.astype(jnp.float32) @ router_w.astype(jnp.float32).T
            probs = jax.nn.softmax(logits, axis=-1)
            rw, re = jax.lax.top_k(probs, TOP_K)
            if TOP_K > 1:
                rw = rw / jnp.maximum(rw.sum(-1, keepdims=True), 1e-12)
            rw = rw.astype(tokens.dtype)
            combine = jnp.zeros((N, E), tokens.dtype).at[jnp.arange(N)[:, None], re].set(rw)
            out = tokens
            for e in range(E):
                h = jax.nn.gelu(tokens @ w1[e] + b1[e], approximate=False)
                y = h @ w2[e] + b2[e]
                out = out + combine[:, e:e + 1] * y
            return out
        b, s, d = input_embeddings.shape
        tokens = input_embeddings.reshape(b * s, d)
        return _moe(tokens, router_w, w1, b1, w2, b2).reshape(b, s, d)

    def _L1_gnn_ref(x, edge_index, W, a_src, a_dst, bias_gat, W_res, b_res, gamma, beta):
        import jax, jax.numpy as jnp
        import numpy as np
        N, DIM, H, C, E = (6250, 256, 4, 64, 100000)
        NEG_SLOPE = 0.2
        LN_EPS = 1e-05
        n = x.shape[0]
        loops = jnp.arange(n, dtype=edge_index.dtype)
        src = jnp.concatenate([edge_index[0], loops])
        dst = jnp.concatenate([edge_index[1], loops])
        h = (x @ W).reshape(n, H, C)
        al_src = jnp.einsum('nhc,hc->nh', h, a_src)
        al_dst = jnp.einsum('nhc,hc->nh', h, a_dst)
        e = jax.nn.leaky_relu(al_src[src] + al_dst[dst], NEG_SLOPE)
        emax = jax.ops.segment_max(e, dst, num_segments=n)
        ee = jnp.exp(e - emax[dst])
        denom = jax.ops.segment_sum(ee, dst, num_segments=n)
        alpha = ee / (denom[dst] + 1e-16)
        msg = h[src] * alpha[:, :, None]
        out = jax.ops.segment_sum(msg, dst, num_segments=n)
        out = out.reshape(n, H * C) + bias_gat
        y = out + x @ W_res + b_res
        mu = jnp.mean(y, axis=-1, keepdims=True)
        var = jnp.mean((y - mu) ** 2, axis=-1, keepdims=True)
        return gamma * (y - mu) * jax.lax.rsqrt(var + LN_EPS) + beta

    def _L1_ffn_ref(h, gate_w, gate_b, w1, b1, w2, b2):
        import math
        import jax, jax.numpy as jnp
        import numpy as np
        CAPACITY_FACTOR = 1.25
        B, L, D = h.shape
        E = gate_w.shape[1]
        T = B * L
        C = max(1, math.ceil(CAPACITY_FACTOR * T / E))
        x = h.reshape(T, D)
        logits = x @ gate_w + gate_b
        probs = jax.nn.softmax(logits, axis=-1)
        idx = jnp.argmax(probs, axis=-1)
        prb = jnp.take_along_axis(probs, idx[:, None], axis=1)[:, 0]
        one_hot = jax.nn.one_hot(idx, E, dtype=jnp.float32)
        pos = (jnp.cumsum(one_hot, axis=0) * one_hot).sum(-1).astype(jnp.int32) - 1
        kept = pos < C
        pos_safe = jnp.where(kept, pos, C)
        buf = jnp.zeros((E, C, D), dtype=h.dtype).at[idx, pos_safe].set(x, mode='drop')
        hmid = jax.nn.relu(jnp.einsum('ecd,edf->ecf', buf, w1) + b1[:, None, :])
        ybuf = jnp.einsum('ecf,efd->ecd', hmid, w2) + b2[:, None, :]
        pos_g = jnp.minimum(pos, C - 1)
        y_tok = ybuf[idx, pos_g] * (prb * kept)[:, None]
        y = y_tok.reshape(B, L, D)
        y = jnp.nan_to_num(y, nan=0.0, posinf=10000.0, neginf=-10000.0)
        return y
    edge_index = jnp.stack([src, dst])
    x = x + _L0_gnn_ref(_layernorm(x, axis=-1), edge_index, L0_gnn_W, L0_gnn_b, L0_gnn_gamma, L0_gnn_beta)
    x = x + _L0_ffn_ref(_layernorm(x, axis=-1)[None], L0_ffn_router_w, L0_ffn_w1, L0_ffn_b1, L0_ffn_w2, L0_ffn_b2)[0]
    x = x + _L1_gnn_ref(_layernorm(x, axis=-1), edge_index, L1_gnn_W, L1_gnn_a_src, L1_gnn_a_dst, L1_gnn_bias_gat, L1_gnn_W_res, L1_gnn_b_res, L1_gnn_gamma, L1_gnn_beta)
    x = x + _L1_ffn_ref(_layernorm(x, axis=-1)[None], L1_ffn_gate_w, L1_ffn_gate_b, L1_ffn_w1, L1_ffn_b1, L1_ffn_w2, L1_ffn_b2)[0]
    return x

_drawn_inputs = setup_inputs


def setup_inputs(seed=0):
    import zlib

    import numpy as np

    out = dict(_drawn_inputs(seed))
    spreads = {'L0_gnn_gamma': (1.0, 0.2),
     'L0_gnn_beta': (0.0, 0.1),
     'L0_ffn_b1': (0.0, 0.338),
     'L0_ffn_b2': (0.0, 0.1),
     'L1_gnn_bias_gat': (0.0, 0.1),
     'L1_gnn_b_res': (0.0, 0.1),
     'L1_gnn_gamma': (1.0, 0.2),
     'L1_gnn_beta': (0.0, 0.1),
     'L1_ffn_gate_b': (0.0, 0.268),
     'L1_ffn_b1': (0.0, 0.8),
     'L1_ffn_b2': (0.0, 0.8)}
    factors = {}
    for name, (base, spread) in spreads.items():
        noise = np.random.default_rng([zlib.crc32(name.encode()), seed]).standard_normal(out[name].shape)
        drawn = base * np.exp(spread * noise) if base else spread * noise
        out[name] = jnp.asarray(drawn.astype(out[name].dtype))
    for name, factor in factors.items():
        out[name] = (out[name] * factor).astype(out[name].dtype)
    return out
```

```python
from contextlib import ExitStack

import concourse.bass as bass
from concourse import mybir

ALU = mybir.AluOpType
ACT = mybir.ActivationFunctionType
AX_X = mybir.AxisListType.X
F32 = mybir.dt.float32
BF16 = mybir.dt.bfloat16
I32 = mybir.dt.int32
U32 = mybir.dt.uint32

P = 128
NODES = 6250
D = 256
KC = D // P
NB = -(-NODES // P)
TAIL = NODES - (NB - 1) * P
EDGES = 206250
T = 4
GROUP = T * P
NG = -(-EDGES // GROUP)
NGP = NG + 1
ECOLS = NGP * GROUP // P
PAD_DST = 8191
STEPS = NG - 1 + NB - 1 + 1
STEPS4 = -(-STEPS // 4) * 4
SQ = -(-STEPS4 // P)
H = 4
C = D // H
HW_ = C + 1
RW = H * HW_
LN_EPS = 1e-5
E = 8
NEG = -3.0e38
F = 1024
CAP = -(-5 * NODES // (4 * E))
PITCH = -(-CAP // P) * P
HCH = 16


class Chain:

    def __init__(self, eng, sem):
        self.eng, self.sem, self.base = eng, sem, 0
        self.i, self.per, self.k = 0, None, 0

    def begin(self, i=0, per=None):
        assert self.k == 0
        self.i, self.per, self.k = i, per, 0

    def link(self, ins):
        self.k += 1
        ins.then_inc(self.sem, 1)
        self.eng.wait_ge(self.sem, self.i * (self.per or 0) + (self.base + self.k))

    def end(self, trips=1):
        assert self.per is None or self.k == self.per, (self.k, self.per)
        self.base += self.k * trips
        self.i, self.per, self.k = 0, None, 0


def tile_at(t, i, width):
    return t[:, bass.ds(i * width, width)]


def in_pairs(eng, n, body):
    with eng.Fori(0, n // 2) as k:
        body(k * 2, 0)
        body(k * 2 + 1, 1)
    if n % 2:
        body(n - 1, 0)


def memory(nc, ctx, phase):

    def sb(name, shape, dt=F32):
        return ctx.enter_context(nc.sbuf_tensor(f"{phase}_{name}", shape, dt))

    def ps(name, width):
        return ctx.enter_context(nc.psum_tensor(f"{phase}_{name}", [P, 512], F32))[:, 0:width]

    def sem(name):
        return ctx.enter_context(nc.semaphore(f"{phase}_{name}"))

    return sb, ps, sem


def setup_phase(nc, a, g):
    with ExitStack() as ctx:
        sb, ps, sem = memory(nc, ctx, "setup")

        iota_i = sb("iota_i", [P, SQ * P], I32)
        iota_f = sb("iota_f", [P, SQ * P])
        pidx_i = sb("pidx_i", [P, 1], I32)
        pidx = sb("pidx", [P, 1])
        spos_i = sb("spos_i", [P, SQ], I32)
        spos = sb("spos", [P, SQ])
        last_i = sb("last_i", [1, NG - 1], I32)
        last_f = sb("last_f", [1, NG - 1])
        ones_row = sb("ones_row", [1, P])
        limit = sb("limit", [P, 1])
        below = sb("below", [P, NG - 1])
        nbelow = sb("nbelow", [P, 1])
        rank = sb("rank", [P, 1])
        far = sb("far", [P, 1])
        passed = sb("passed", [P, SQ * P])
        blk = sb("blk", [P, SQ])
        grp = sb("grp", [P, SQ])
        grp_i = sb("grp_i", [P, SQ], I32)
        dst_s = sb("dst_s", [P, SQ * GROUP], I32)
        src_s = sb("src_s", [P, SQ * GROUP], I32)
        work = sb("work", [P, 4, GROUP])
        dflat = sb("dflat", [P, ECOLS], I32)
        dlo_i = sb("dlo_i", [P, ECOLS], I32)
        dhi_i = sb("dhi_i", [P, ECOLS], I32)
        dlo = sb("dlo", [P, ECOLS])
        dhi = sb("dhi", [P, ECOLS])
        iota_b = sb("iota_b", [P, P], BF16)
        oh_lo = [sb(f"oh_lo{k}", [P, HCH, P], BF16) for k in range(2)]
        oh_hi = [sb(f"oh_hi{k}", [P, HCH, NB], BF16) for k in range(2)]
        zero_b = sb("zero_b", [P, P], BF16)

        last_ps = ps("last_ps", NG - 1)
        blk_ps = ps("blk_ps", SQ)
        row_ps = ps("row_ps", SQ * P)[0:1, :]
        hist_ps = ps("hist_ps", NB)
        turn_ps = [ps(f"turn_ps{k}", T * P).rearrange("p (t e) -> p t e", t=T) for k in range(2)]

        zeros = sb("zeros", [P, RW])
        zeros_ready = sem("zeros_ready")
        zeroed = sem("zeroed")
        iotas = sem("iotas")
        x_in = sem("x_in")
        last_in = sem("last_in")
        dflat_in = sem("dflat_in")
        own = sem("own")
        consts = sem("consts")
        last_wide = sem("last_wide")
        passed_ready = sem("passed_ready")
        blocks_counted = sem("blocks_counted")
        groups_known = sem("groups_known")
        edges_in = [sem(f"edges_in{q}") for q in range(SQ)]
        work_ready = sem("work_ready")
        turned = sem("turned")
        turn_free = sem("turn_free")
        onehots = sem("onehots")
        onehots_used = sem("onehots_used")
        split_ready = sem("split_ready")
        hist_done = sem("hist_done")
        gated = sem("gated")
        block = ctx.enter_context(nc.Block())
        NTURN = SQ * 4
        CHUNKS = ECOLS // HCH
        assert ECOLS % HCH == 0

        @block.gpsimd
        def _(pool):
            nc.gpsimd.iota(iota_i[:, :], [[1, SQ * P]], base=0, channel_multiplier=0).then_inc(iotas, 1)
            nc.gpsimd.iota(pidx_i[:, :], [[1, 1]], base=0, channel_multiplier=1).then_inc(iotas, 1)
            nc.gpsimd.iota(spos_i[:, :], [[P, SQ]], base=0, channel_multiplier=1).then_inc(iotas, 1)
            pool.wait_ge(groups_known, 1)
            for q in range(SQ):
                for t, arr in ((dst_s, a["dst"]), (src_s, a["src"])):
                    nc.gpsimd.indirect_dma_start(
                        out=t[:, q * GROUP:(q + 1) * GROUP], out_offset=None, in_=arr[:, :],
                        in_offset=bass.IndirectOffsetOnAxis(ap=grp_i[:, q:q + 1], axis=0)).then_inc(edges_in[q], 16)

        @block.sync
        def _(sp):
            with nc.allow_non_contiguous_dma(reason="the last destination of each group"):
                sp.dma_start(last_i[:, :], a["dst"][0:NG - 1, GROUP - 1:GROUP].rearrange("g one -> one g")).then_inc(last_in, 16)
            sp.dma_start(dflat[:, :], a["dst"].rearrange("g e -> (g e)").rearrange("(p c) -> p c", p=P)).then_inc(dflat_in, 16)
            sp.dma_start(g["x"][:, :, :], a["x"].rearrange("(b p) d -> p b d", p=P)).then_inc(x_in, 16)
            sp.wait_ge(zeros_ready, 1)
            for e in range(E):
                sp.dma_start(g["sent"][e * PITCH:(e + 1) * PITCH, :].rearrange("(t p) w -> p t w", p=P),
                             zeros[:, :].unsqueeze(1).broadcast_to([P, PITCH // P, RW])).then_inc(zeroed, 16)
            sp.wait_ge(x_in, 16)
            sp.wait_ge(zeroed, 16 * E)

        @block.vector
        def _(dve):
            v = nc.vector
            ch = Chain(dve, own)
            v.memset(zeros[:, :], 0.0).then_inc(zeros_ready, 1)
            v.memset(ones_row[:, :], 1.0).then_inc(consts, 1)
            v.memset(g["ones"][:, :], 1.0).then_inc(consts, 1)
            v.memset(zero_b[:, :], 0.0).then_inc(consts, 1)
            ch.link(v.memset(g["eps"][:, :], LN_EPS))
            dve.wait_ge(iotas, 3)
            v.tensor_copy(iota_f[:, :], iota_i[:, :])
            v.tensor_copy(spos[:, :], spos_i[:, :])
            ch.link(v.tensor_copy(pidx[:, :], pidx_i[:, :]))
            v.tensor_copy(g["iota"][:, :], iota_f[:, 0:P])
            v.tensor_copy(iota_b[:, :], iota_f[:, 0:P])
            v.tensor_scalar(g["ident"][:, :], iota_f[:, 0:P], pidx[:, 0:1], None, ALU.is_equal).then_inc(consts, 1)
            v.tensor_scalar(g["upper"][:, :], iota_f[:, 0:P], pidx[:, 0:1], None, ALU.is_ge)
            v.tensor_scalar(limit[:, :], pidx[:, :], float(P), float(P), ALU.mult, ALU.add)
            v.tensor_scalar(far[:, :], pidx[:, :], float(NB - 1), 1.0e6, ALU.is_ge, ALU.mult)
            dve.wait_ge(last_in, 16)
            ch.link(v.tensor_copy(last_f[:, :], last_i[:, :]))
            v.tensor_copy(g["pidx"][:, :], pidx[:, :]).then_inc(last_wide, 1)
            dve.wait_ge(last_wide, 2)
            ch.link(v.tensor_scalar(below[:, :], last_ps[:, :], limit[:, 0:1], None, ALU.is_lt))
            ch.link(v.reduce_sum(nbelow[:, :], below[:, :], AX_X))
            ch.link(v.scalar_tensor_tensor(rank[:, :], nbelow[:, :], pidx[:, 0:1], far[:, :], ALU.add, ALU.add))
            v.tensor_scalar(passed[:, :], iota_f[:, :], rank[:, 0:1], None, ALU.is_gt).then_inc(passed_ready, 1)
            dve.wait_ge(blocks_counted, 1)
            ch.link(v.tensor_copy(blk[:, :], blk_ps[:, :]))
            v.tensor_copy(g["block_of_step"][:, :], row_ps[:, :])
            ch.link(v.tensor_tensor(grp[:, :], spos[:, :], blk[:, :], ALU.subtract))
            v.tensor_scalar(grp_i[:, :], grp[:, :], float(NG), None, ALU.min).then_inc(groups_known, 1)
            ch.link(v.tensor_scalar(blk[:, :], blk[:, :], float(P), None, ALU.mult))
            for q in range(SQ):
                dve.wait_ge(edges_in[q], 32)
                if q:
                    dve.wait_ge(turned, 4 * q)
                ds_ = dst_s[:, q * GROUP:(q + 1) * GROUP]
                d3 = ds_.rearrange("p (t e) -> p t e", t=T)
                w = [work[:, n, :].rearrange("p (t e) -> p t e", t=T) for n in range(4)]
                v.tensor_copy(work[:, 0, :], src_s[:, q * GROUP:(q + 1) * GROUP])
                v.tensor_scalar(work[:, 1, :], ds_, blk[:, q:q + 1], None, ALU.subtract)
                v.memset(w[2][:, :, 0:1], NEG)
                v.memset(w[3][:, :, P - 1:P], 1.0)
                ch.link(v.tensor_tensor(w[3][:, :, 0:P - 1], d3[:, :, 1:P], d3[:, :, 0:P - 1], ALU.not_equal))
                v.tensor_scalar(w[2][:, :, 1:P], w[3][:, :, 0:P - 1], NEG, None, ALU.mult).then_inc(work_ready, 1)
            dve.wait_ge(dflat_in, 16)
            v.tensor_scalar(dlo_i[:, :], dflat[:, :], P - 1, None, ALU.bitwise_and)
            ch.link(v.tensor_scalar(dhi_i[:, :], dflat[:, :], 7, None, ALU.logical_shift_right))
            v.tensor_copy(dlo[:, :], dlo_i[:, :])
            ch.link(v.tensor_copy(dhi[:, :], dhi_i[:, :]))

            def count(i, k):
                dve.wait_ge(onehots_used, i + 1)
                lo = tile_at(dlo, i, HCH).unsqueeze(2).broadcast_to([P, HCH, P])
                hi = tile_at(dhi, i, HCH).unsqueeze(2).broadcast_to([P, HCH, NB])
                v.tensor_tensor(oh_lo[k][:, :, :], iota_b[:, :].unsqueeze(1).broadcast_to([P, HCH, P]), lo, ALU.is_equal)
                v.tensor_tensor(oh_hi[k][:, :, :], iota_b[:, 0:NB].unsqueeze(1).broadcast_to([P, HCH, NB]), hi,
                                ALU.is_equal).then_inc(onehots, 1)

            in_pairs(dve, CHUNKS, count)
            dve.wait_ge(hist_done, 1)
            ch.link(v.tensor_scalar(g["dinv"][:, :], hist_ps[:, :], 1.0, None, ALU.add))
            dve.drain().then_inc(gated, 1)
            dve.wait_ge(gated, 2)
            v.reciprocal(g["dinv"][:, :], g["dinv"][:, :]).then_inc(gated, 1)
            dve.wait_ge(gated, 3)

        @block.scalar
        def _(act):
            for n in range(NTURN):
                q, arr = divmod(n, 4)
                act.wait_ge(turned, n + 1)
                out = g["edges"][arr][:, q * P * T:(q + 1) * P * T].rearrange("e (s t) -> e t s", t=T)
                nc.scalar.copy(out, turn_ps[n % 2][:, :, :]).then_inc(turn_free, 1)
            act.wait_ge(gated, 1)
            nc.scalar.activation(g["dinv"][:, :], g["dinv"][:, :], ACT.Sqrt).then_inc(gated, 1)

        @block.tensor
        def _(pe):
            t = nc.tensor
            pe.wait_ge(last_wide, 1)
            pe.wait_ge(consts, 4)
            t.matmul(last_ps[:, :], ones_row[:, :], last_f[:, :], start=True, stop=True).then_inc(last_wide, 1)
            pe.wait_ge(passed_ready, 1)
            for q in range(SQ):
                t.matmul(blk_ps[:, q:q + 1], passed[:, q * P:(q + 1) * P], g["ones"][:, 0:1], start=True, stop=True)
            t.matmul(row_ps[:, :], g["ones"][:, 0:1], passed[:, :], start=True, stop=True).then_inc(blocks_counted, 1)
            for n in range(NTURN):
                q, arr = divmod(n, 4)
                pe.wait_ge(work_ready, q + 1)
                if n >= 2:
                    pe.wait_ge(turn_free, n - 1)
                for tt in range(T):
                    ins = t.transpose(turn_ps[n % 2][:, tt, :], work[:, arr, tt * P:(tt + 1) * P], g["ident"][:, :])
                ins.then_inc(turned, 1)
            pe.sem_inc(onehots_used, 2)
            t.matmul(hist_ps[:, :], zero_b[:, :], zero_b[:, 0:NB], start=True, stop=False)

            def count(i, k):
                pe.wait_ge(onehots, i + 1)
                for j in range(HCH):
                    ins = t.matmul(hist_ps[:, :], oh_lo[k][:, j, :], oh_hi[k][:, j, :], start=False, stop=False)
                ins.then_inc(onehots_used, 1)

            in_pairs(pe, CHUNKS, count)
            t.matmul(hist_ps[:, :], zero_b[:, :], zero_b[:, 0:NB], start=False, stop=True).then_inc(hist_done, 1)


def gcn_table_phase(nc, a, g):
    with ExitStack() as ctx:
        sb, ps, sem = memory(nc, ctx, "gcn_table")

        stats = sb("stats", [P, NB * 6])
        mean = sb("mean", [P, NB])
        var = sb("var", [P, NB])
        half = sb("half", [P, NB])
        w_in = sb("w_in", [P, KC, D])
        w_t = sb("w_t", [P, KC, D])
        xn = [sb(f"xn{k}", [P, D]) for k in range(2)]
        xn_t = [sb(f"xn_t{k}", [P, KC, P]) for k in range(2)]
        xt_ps = [ps(f"xt_ps{k}", D).rearrange("p (c n) -> p c n", c=KC) for k in range(2)]
        row_ps = [ps(f"row_ps{k}", D) for k in range(2)]
        w_ps = ps("w_ps", KC * D).rearrange("p (c n) -> p c n", c=KC)

        own = sem("own")
        w_loaded = sem("w_loaded")
        w_turned = sem("w_turned")
        w_ready = sem("w_ready")
        var_ready = sem("var_ready")
        root_ready = sem("root_ready")
        xn_ready = sem("xn_ready")
        xn_turned = sem("xn_turned")
        xn_t_ready = sem("xn_t_ready")
        rows_ready = sem("rows_ready")
        rows_scaled = sem("rows_scaled")
        rows_out = sem("rows_out")
        block = ctx.enter_context(nc.Block())

        @block.sync
        def _(sp):
            sp.dma_start(w_in[:, :, :], a["L0_gnn_W"].rearrange("(o p) k -> p o k", p=P)).then_inc(w_loaded, 16)
            with sp.Fori(0, NB) as i:
                sp.wait_ge(rows_scaled, i + 1)
                sp.dma_start(g["table0"][bass.ds(i * P, P), :], tile_at(g["acc"], i, D)).then_inc(rows_out, 16)
            sp.wait_ge(rows_out, 16 * NB)

        @block.vector
        def _(dve):
            v = nc.vector
            ch = Chain(dve, own)
            emit_stats(nc, dve, ch, g["x"], stats, mean, var, half, var_ready)
            dve.wait_ge(root_ready, 1)
            ch.link(v.reciprocal(var[:, :], var[:, :]))
            dve.sem_inc(xn_turned, 2)
            dve.sem_inc(rows_ready, 2)

            def norm(i, k):
                dve.wait_ge(xn_turned, i + 1)
                v.tensor_scalar(xn[k][:, :], tile_at(g["xf"], i, D), mean[:, bass.ds(i, 1)], var[:, bass.ds(i, 1)],
                                ALU.subtract, ALU.mult).then_inc(xn_ready, 1)

            def scale(i, k):
                dve.wait_ge(rows_ready, i + 3)
                v.tensor_scalar(tile_at(g["acc"], i, D), row_ps[k][:, :], g["dinv"][:, bass.ds(i, 1)], None,
                                ALU.mult).then_inc(rows_scaled, 1)

            norm(0, 0)
            with dve.Fori(0, NB // 2) as j:
                norm(j * 2 + 1, 1)
                scale(j * 2, 0)
                norm(j * 2 + 2, 0)
                scale(j * 2 + 1, 1)
            scale(NB - 1, 0)

        @block.scalar
        def _(act):
            act.wait_ge(w_turned, 1)
            nc.scalar.copy(w_t[:, :, :], w_ps[:, :, :]).then_inc(w_ready, 1)
            act.wait_ge(var_ready, 1)
            nc.scalar.activation(var[:, :], var[:, :], ACT.Sqrt, bias=g["eps"][:, 0:1]).then_inc(root_ready, 1)

            def move(i, k):
                act.wait_ge(xn_turned, i + 3)
                act.wait_ge(rows_ready, i + 1)
                nc.scalar.copy(xn_t[k][:, :, :], xt_ps[k][:, :, :]).then_inc(xn_t_ready, 1)

            in_pairs(act, NB, move)

        @block.tensor
        def _(pe):
            t = nc.tensor
            pe.wait_ge(w_loaded, 16)
            for kc in range(KC):
                for o in range(KC):
                    ins = t.transpose(w_ps[:, kc, o * P:(o + 1) * P], w_in[:, o, kc * P:(kc + 1) * P], g["ident"][:, :])
            ins.then_inc(w_turned, 1)
            pe.wait_ge(w_ready, 1)

            def turn(i, k):
                pe.wait_ge(xn_ready, i + 1)
                for kc in range(KC):
                    ins = t.transpose(xt_ps[k][:, kc, :], xn[k][:, kc * P:(kc + 1) * P], g["ident"][:, :])
                ins.then_inc(xn_turned, 1)

            def rows(i, k, first=False):
                pe.wait_ge(xn_t_ready, i + 1)
                if not first:
                    pe.wait_ge(rows_scaled, i - 1)
                for kc in range(KC):
                    ins = t.matmul(row_ps[k][:, :], xn_t[k][:, kc, :], w_t[:, kc, :], start=(kc == 0), stop=(kc == KC - 1))
                ins.then_inc(rows_ready, 1)

            turn(0, 0)
            turn(1, 1)
            rows(0, 0, True)
            turn(2, 0)
            rows(1, 1, True)
            with pe.Fori(1, NB // 2) as j:
                turn(j * 2 + 1, 1)
                rows(j * 2, 0)
                turn(j * 2 + 2, 0)
                rows(j * 2 + 1, 1)
            rows(NB - 1, 0)


def emit_stats(nc, dve, ch, x3, stats, mean, var, half, var_ready):
    v = nc.vector
    xf = x3[:, :, :].rearrange("p b d -> p (b d)")
    with dve.Fori(0, NB) as i:
        v.bn_stats(stats[:, bass.ds(i * 6, 6)], xf[:, bass.ds(i * D, D)])
    st = stats[:, :].rearrange("p (b s) -> p b s", s=6)
    dve.drain()
    ch.link(v.tensor_tensor(mean[:, :], st[:, :, 1], st[:, :, 4], ALU.add))
    ch.link(v.tensor_tensor(half[:, :], st[:, :, 1], st[:, :, 4], ALU.subtract))
    ch.link(v.tensor_tensor(var[:, :], st[:, :, 2], st[:, :, 5], ALU.add))
    ch.link(v.tensor_scalar(mean[:, :], mean[:, :], 0.5, None, ALU.mult))
    ch.link(v.scalar_tensor_tensor(half[:, :], half[:, :], 0.25, half[:, :], ALU.mult, ALU.mult))
    v.scalar_tensor_tensor(var[:, :], var[:, :], 1.0 / D, half[:, :], ALU.mult, ALU.add).then_inc(var_ready, 1)


def gcn_steps_phase(nc, a, g):
    with ExitStack() as ctx:
        sb, ps, sem = memory(nc, ctx, "gcn_steps")

        R = 4
        TRIPS = STEPS4 // R
        index = [sb(f"index{k}", [P, R * T], I32) for k in range(2)]
        rows = [sb(f"rows{k}", [P, T, D]) for k in range(R)]
        onehot = [sb(f"onehot{k}", [P, T, P]) for k in range(2)]
        sum_ps = [ps(f"sum_ps{k}", D) for k in range(2)]

        own = sem("own")
        index_ready = sem("index_ready")
        index_used = sem("index_used")
        rows_in = [sem(f"rows_in{k}") for k in range(R)]
        onehot_ready = sem("onehot_ready")
        sums_ready = sem("sums_ready")
        sums_added = sem("sums_added")
        slots_taken = sem("slots_taken")
        block = ctx.enter_context(nc.Block())

        @block.scalar
        def _(act):
            act.sem_inc(index_used, 2)

            def indices(j, k):
                act.wait_ge(index_used, j + 1)
                nc.scalar.copy(index[k][:, :], tile_at(g["edges"][0], j, R * T)).then_inc(index_ready, 1)

            in_pairs(act, TRIPS, indices)

        @block.gpsimd
        def _(pool):
            pool.sem_inc(sums_ready, R)

            def gather(j, k):
                pool.wait_ge(index_ready, j + 1)
                for r in range(R):
                    pool.wait_ge(sums_ready, j * R + (r + 1))
                    pool.sem_inc(slots_taken, 1)
                    for t in range(T):
                        n = r * T + t
                        ins = nc.gpsimd.indirect_dma_start(
                            out=rows[r][:, t, :], out_offset=None, in_=g["table0"][:, :],
                            in_offset=bass.IndirectOffsetOnAxis(ap=index[k][:, n:n + 1], axis=0)).then_inc(rows_in[r], 16)
                for r in range(R):
                    pool.wait_ge(rows_in[r], (j + 1) * (16 * T))
                pool.sem_inc(index_used, 1)

            in_pairs(pool, TRIPS, gather)

        @block.vector
        def _(dve):
            v = nc.vector

            def onehots(j, r):
                dve.wait_ge(sums_ready, j * R + (r + R - 1))
                for t in range(T):
                    ins = v.tensor_scalar(onehot[r % 2][:, t, :], g["iota"][:, :],
                                          g["edges"][1][:, bass.ds(j * (R * T) + (r * T + t), 1)], None, ALU.is_equal)
                ins.then_inc(onehot_ready, 1)

            def add(j, r):
                b = dve.value_load(g["block_of_step"][0:1, bass.ds(j * R + r, 1)], min_val=0, max_val=NB - 1)
                dve.wait_ge(sums_ready, j * R + (r + 1 + R))
                into = tile_at(g["acc"], b, D)
                v.tensor_tensor(into, sum_ps[r % 2][:, :], into, ALU.add).then_inc(sums_added, 1)
                dve.wait_ge(sums_added, j * R + (r + 1))

            with dve.Fori(0, TRIPS) as j:
                for r in range(R):
                    onehots(j, r)
                    add(j, r)

        @block.tensor
        def _(pe):
            def product(j, r, first=False):
                pe.wait_ge(rows_in[r], (j + 1) * (16 * T))
                pe.wait_ge(onehot_ready, j * R + (r + 1))
                if not first:
                    pe.wait_ge(sums_added, j * R + (r - 1))
                for t in range(T):
                    ins = nc.tensor.matmul(sum_ps[r % 2][:, :], onehot[r % 2][:, t, :], rows[r][:, t, :],
                                           start=(t == 0), stop=(t == T - 1))
                ins.then_inc(sums_ready, 1)

            for r in range(R):
                product(0, r, first=(r < 2))
            with pe.Fori(1, TRIPS) as j:
                for r in range(R):
                    product(j, r)


def moe_phase(nc, a, g):
    with ExitStack() as ctx:
        sb, ps, sem = memory(nc, ctx, "moe")

        w1 = sb("w1", [P, E, KC, D])
        w2 = sb("w2", [P, E, KC, D])
        b1_in = sb("b1_in", [E * KC, P])
        b1 = sb("b1", [P, E * KC])
        b2 = sb("b2", [E, D])
        router_in = sb("router_in", [E, D])
        router = sb("router", [P, KC, E])
        bias = sb("bias", [P, D])
        gamma = sb("gamma", [P, D])
        beta = sb("beta", [P, D])
        node = sb("node", [P, D])
        stats = sb("stats", [P, 2, 6])
        mv = sb("mv", [P, 2, 2])
        ve = sb("ve", [P, 2])
        rstd = sb("rstd", [P, 2])
        minus_half = sb("minus_half", [P, 1])
        xn = sb("xn", [P, D])
        xn_t = [sb(f"xn_t{k}", [P, KC, P]) for k in range(2)]
        down = sb("down", [P, E])
        lg = sb("lg", [P, E])
        ex = sb("ex", [P, E])
        pr = sb("pr", [P, E])
        first = sb("first", [P, E])
        second = sb("second", [P, E])
        rest = sb("rest", [P, E])
        eq = sb("eq", [P, E])
        s1 = sb("s1", [P, 8])
        comb = [sb(f"comb{k}", [P, E]) for k in range(2)]
        comb_t = sb("comb_t", [E, P])
        hid = [sb(f"hid{k}", [P, KC, P]) for k in range(2)]

        xt_ps = ps("xt_ps", D).rearrange("p (c n) -> p c n", c=KC)
        logit_ps = ps("logit_ps", E)
        combt_ps = ps("combt_ps", P)
        b2_ps = ps("b2_ps", D)
        hid_ps = [ps(f"hid_ps{k}", D).rearrange("p (c n) -> p c n", c=KC) for k in range(2)]
        y_ps = [ps(f"y_ps{k}", D) for k in range(2)]

        own = sem("own")
        loaded = sem("loaded")
        const_ready = sem("const_ready")
        turned_w = sem("turned_w")
        weights_ready = sem("weights_ready")
        var_ready = sem("var_ready")
        rstd_ready = sem("rstd_ready")
        xn_ready = sem("xn_ready")
        xn_turned = sem("xn_turned")
        xn_t_ready = sem("xn_t_ready")
        logits_ready = sem("logits_ready")
        lg_ready = sem("lg_ready")
        exp_ready = sem("exp_ready")
        comb_ready = sem("comb_ready")
        comb_turned = sem("comb_turned")
        comb_t_ready = sem("comb_t_ready")
        b2_ready = sem("b2_ready")
        hid_ready = sem("hid_ready")
        gelu_ready = sem("gelu_ready")
        y_ready = sem("y_ready")
        y_added = sem("y_added")
        block = ctx.enter_context(nc.Block())
        NLOAD = 8

        @block.sync
        def _(sp):
            with nc.allow_non_contiguous_dma(reason="rows broadcast"):
                for t, src in ((b1_in[:, :], a["L0_ffn_b1"].rearrange("e (c p) -> (e c) p", p=P)),
                               (router_in[:, :], a["L0_ffn_router_w"]),
                               (bias[:, :], a["L0_gnn_b"].partition_broadcast(P)),
                               (gamma[:, :], a["L0_gnn_gamma"].partition_broadcast(P)),
                               (beta[:, :], a["L0_gnn_beta"].partition_broadcast(P)),
                               (b2[:, :], a["L0_ffn_b2"]),
                               (w1[:, :, :, :], a["L0_ffn_w1"].rearrange("e (c p) f -> p e c f", p=P)),
                               (w2[:, :, :, :], a["L0_ffn_w2"].rearrange("e (c p) f -> p e c f", p=P))):
                    sp.dma_start(t, src).then_inc(loaded, 16)
            sp.wait_ge(loaded, 16 * NLOAD)

        @block.gpsimd
        def _(pool):
            pool.wait_ge(const_ready, 1)

            def roots(i):
                for c in range(2):
                    pool.wait_ge(var_ready, i * 2 + (c + 1))
                    nc.gpsimd.tensor_tensor(rstd[:, c:c + 1], ve[:, c:c + 1], minus_half[:, :], ALU.pow).then_inc(rstd_ready, 1)

            with pool.Fori(0, NB) as i:
                roots(i)

        @block.vector
        def _(dve):
            v = nc.vector
            ch = Chain(dve, own)
            v.tensor_scalar(down[:, :], g["iota"][:, 0:E], -1.0, float(E), ALU.mult, ALU.add)
            v.memset(minus_half[:, :], -0.5).then_inc(const_ready, 1)
            dve.wait_ge(loaded, 16 * NLOAD)

            def norm_stats(c, i, src):
                v.bn_stats(stats[:, c, :], src)
                dve.drain()
                ch.link(v.bn_aggr(mv[:, c, :], stats[:, c, :]))
                v.tensor_scalar(ve[:, c:c + 1], mv[:, c, 1:2], LN_EPS, None, ALU.add).then_inc(var_ready, 1)

            def pieces(i, k):
                xb = tile_at(g["xf"], i, D)

                def p0():
                    ch.link(v.scalar_tensor_tensor(node[:, :], tile_at(g["acc"], i, D), g["dinv"][:, bass.ds(i, 1)],
                                                   bias[:, :], ALU.mult, ALU.add))
                    norm_stats(0, i, node[:, :])

                def p1():
                    dve.wait_ge(rstd_ready, i * 2 + 1)
                    ch.link(v.tensor_scalar(node[:, :], node[:, :], mv[:, 0, 0:1], rstd[:, 0:1], ALU.subtract, ALU.mult))
                    ch.link(v.tensor_tensor(node[:, :], node[:, :], gamma[:, :], ALU.mult))

                def p2():
                    ch.link(v.tensor_tensor(node[:, :], node[:, :], beta[:, :], ALU.add))

                def p3():
                    ch.link(v.scalar_tensor_tensor(node[:, :], node[:, :], 0.0, xb, ALU.max, ALU.add))
                    norm_stats(1, i, node[:, :])

                def p4():
                    dve.wait_ge(rstd_ready, i * 2 + 2)
                    v.tensor_scalar(xn[:, :], node[:, :], mv[:, 1, 0:1], rstd[:, 1:2], ALU.subtract,
                                    ALU.mult).then_inc(xn_ready, 1)
                    dve.wait_ge(xn_ready, i + 1)
                    ch.link(v.tensor_tensor(xb, node[:, :], xn[:, :], ALU.add))

                def p5():
                    dve.wait_ge(logits_ready, i + 1)
                    ch.link(v.reduce_max(s1[:, 0:1], logit_ps[:, :], AX_X))
                    v.tensor_scalar(lg[:, :], logit_ps[:, :], s1[:, 0:1], None, ALU.subtract).then_inc(lg_ready, 1)

                def p6():
                    dve.wait_ge(exp_ready, i + 1)
                    ch.link(v.reduce_sum(s1[:, 1:2], ex[:, :], AX_X))
                    ch.link(v.reciprocal(s1[:, 2:3], s1[:, 1:2]))
                    ch.link(v.tensor_scalar(pr[:, :], ex[:, :], s1[:, 2:3], None, ALU.mult))
                    ch.link(v.reduce_max(s1[:, 3:4], pr[:, :], AX_X))
                    ch.link(v.scalar_tensor_tensor(eq[:, :], pr[:, :], s1[:, 3:4], down[:, :], ALU.is_equal, ALU.mult))
                    ch.link(v.reduce_max(s1[:, 5:6], eq[:, :], AX_X))
                    ch.link(v.tensor_scalar(first[:, :], eq[:, :], s1[:, 5:6], None, ALU.is_equal))
                    ch.link(v.scalar_tensor_tensor(rest[:, :], first[:, :], -2.0, pr[:, :], ALU.mult, ALU.add))

                def p7():
                    ch.link(v.reduce_max(s1[:, 4:5], rest[:, :], AX_X))
                    ch.link(v.scalar_tensor_tensor(eq[:, :], rest[:, :], s1[:, 4:5], down[:, :], ALU.is_equal, ALU.mult))
                    ch.link(v.reduce_max(s1[:, 5:6], eq[:, :], AX_X))
                    v.tensor_scalar(second[:, :], eq[:, :], s1[:, 5:6], s1[:, 4:5], ALU.is_equal, ALU.mult)
                    ch.link(v.tensor_tensor(s1[:, 6:7], s1[:, 3:4], s1[:, 4:5], ALU.add))
                    ch.link(v.tensor_scalar(s1[:, 6:7], s1[:, 6:7], 1e-12, None, ALU.max))
                    ch.link(v.reciprocal(s1[:, 7:8], s1[:, 6:7]))
                    ch.link(v.scalar_tensor_tensor(first[:, :], first[:, :], s1[:, 3:4], second[:, :], ALU.mult, ALU.add))
                    v.tensor_scalar(comb[k][:, :], first[:, :], s1[:, 7:8], None, ALU.mult).then_inc(comb_ready, 1)
                    dve.wait_ge(comb_ready, i + 1)

                return [p0, p1, p2, p3, p4, p5, p6, p7]

            def block_of(i, k, ahead):
                xb = tile_at(g["xf"], i, D)
                dve.wait_ge(b2_ready, i + 1)
                ch.link(v.tensor_tensor(xb, b2_ps[:, :], xb, ALU.add))
                for e in range(E):
                    if ahead:
                        ahead[e]()
                    dve.wait_ge(y_ready, i * E + (e + 1))
                    ins = v.scalar_tensor_tensor(xb, y_ps[e % 2][:, :], comb[k][:, e:e + 1], xb, ALU.mult, ALU.add)
                    ins.then_inc(y_added, 1)
                    dve.wait_ge(y_added, i * E + (e + 1))

            PREP, ADD = 24, 1
            ch.begin()
            for p in pieces(0, 0):
                p()
            ch.end()
            with dve.Fori(0, (NB - 1) // 2) as j:
                ch.begin(j, 2 * (PREP + ADD))
                block_of(j * 2, 0, pieces(j * 2 + 1, 1))
                block_of(j * 2 + 1, 1, pieces(j * 2 + 2, 0))
            ch.end((NB - 1) // 2)
            block_of(NB - 1, 0, None)

        @block.scalar
        def _(act):
            s = nc.scalar
            act.wait_ge(turned_w, 1)
            s.copy(b1[:, :], xt_ps[:, 0, 0:E * KC])
            s.copy(router[:, :, :], xt_ps[:, 1, 0:KC * E].rearrange("p (c e) -> p c e", c=KC)).then_inc(weights_ready, 1)
            act.wait_ge(weights_ready, 1)

            def turned(i, k):
                act.wait_ge(xn_turned, i + 1)
                s.copy(xn_t[k][:, :, :], xt_ps[:, :, :]).then_inc(xn_t_ready, 1)

            def exps(i):
                act.wait_ge(lg_ready, i + 1)
                s.activation(ex[:, :], lg[:, :], ACT.Exp).then_inc(exp_ready, 1)

            def comb_copy(i):
                act.wait_ge(comb_turned, i + 1)
                s.copy(comb_t[:, :], combt_ps[0:E, :]).then_inc(comb_t_ready, 1)

            def gelu(i, e):
                act.wait_ge(hid_ready, i * E + (e + 1))
                for c in range(KC):
                    n = e * KC + c
                    ins = s.activation(hid[e % 2][:, c, :], hid_ps[e % 2][:, c, :], ACT.Gelu, bias=b1[:, n:n + 1])
                ins.then_inc(gelu_ready, 1)

            def block_of(i, k, more):
                for e in range(E):
                    gelu(i, e)
                    if more and e == 5:
                        turned(i + 1, 1 - k)
                if more:
                    exps(i + 1)
                    comb_copy(i + 1)

            turned(0, 0)
            exps(0)
            comb_copy(0)
            with act.Fori(0, (NB - 1) // 2) as j:
                block_of(j * 2, 0, True)
                block_of(j * 2 + 1, 1, True)
            block_of(NB - 1, 0, False)

        @block.tensor
        def _(pe):
            t = nc.tensor
            pe.wait_ge(loaded, 16 * NLOAD)
            t.transpose(xt_ps[:, 0, 0:E * KC], b1_in[:, :], g["ident"][0:E * KC, 0:E * KC])
            for c in range(KC):
                ins = t.transpose(xt_ps[:, 1, c * E:(c + 1) * E], router_in[:, c * P:(c + 1) * P], g["ident"][0:E, 0:E])
            ins.then_inc(turned_w, 1)
            pe.wait_ge(weights_ready, 1)

            def turn(i, k):
                pe.wait_ge(xn_ready, i + 1)
                for c in range(KC):
                    ins = t.transpose(xt_ps[:, c, :], xn[:, c * P:(c + 1) * P], g["ident"][:, :])
                ins.then_inc(xn_turned, 1)

            def logits(i, k):
                pe.wait_ge(xn_t_ready, i + 1)
                for c in range(KC):
                    ins = t.matmul(logit_ps[:, :], xn_t[k][:, c, :], router[:, c, :], start=(c == 0), stop=(c == KC - 1))
                ins.then_inc(logits_ready, 1)

            def comb_turn(i, k):
                pe.wait_ge(comb_ready, i + 1)
                t.transpose(combt_ps[0:E, :], comb[k][:, :], g["ident"][:, :]).then_inc(comb_turned, 1)
                pe.wait_ge(comb_t_ready, i + 1)
                t.matmul(b2_ps[:, :], comb_t[:, :], b2[:, :], start=True, stop=True).then_inc(b2_ready, 1)

            def up(i, k, e):
                for f in range(KC):
                    for c in range(KC):
                        ins = t.matmul(hid_ps[e % 2][:, f, :], w1[:, e, c, f * P:(f + 1) * P], xn_t[k][:, c, :],
                                       start=(c == 0), stop=(c == KC - 1))
                ins.then_inc(hid_ready, 1)

            def down_(i, e, wait):
                pe.wait_ge(gelu_ready, i * E + (e + 1))
                if wait:
                    pe.wait_ge(y_added, i * E + (e - 1))
                for f in range(KC):
                    ins = t.matmul(y_ps[e % 2][:, :], hid[e % 2][:, f, :], w2[:, e, f, :], start=(f == 0), stop=(f == KC - 1))
                ins.then_inc(y_ready, 1)

            def block_of(i, k, more, start=False):
                for e in range(E + 1):
                    if e < E:
                        up(i, k, e)
                    if e > 0:
                        down_(i, e - 1, not (start and e - 1 < 2))
                    if more and e == 5:
                        turn(i + 1, 1 - k)
                    if more and e == 6:
                        logits(i + 1, 1 - k)
                if more:
                    comb_turn(i + 1, 1 - k)

            turn(0, 0)
            logits(0, 0)
            comb_turn(0, 0)
            block_of(0, 0, True, True)
            block_of(1, 1, True)
            with pe.Fori(1, (NB - 1) // 2) as j:
                block_of(j * 2, 0, True)
                block_of(j * 2 + 1, 1, True)
            block_of(NB - 1, 0, False)


def gat_table_phase(nc, a, g):
    with ExitStack() as ctx:
        sb, ps, sem = memory(nc, ctx, "gat_table")
        NA = RW + H
        stats = sb("stats", [P, NB * 6])
        mean = sb("mean", [P, NB])
        var = sb("var", [P, NB])
        half = sb("half", [P, NB])
        w_in = sb("w_in", [P, KC, D])
        w_res = sb("w_res", [P, KC, D])
        w_aug = sb("w_aug", [P, KC, NA])
        a_src = sb("a_src", [P, D])
        a_dst = sb("a_dst", [P, D])
        prod = sb("prod", [P, KC, D])
        bias = sb("bias", [P, D])
        bias2 = sb("bias2", [P, D])
        xn = [sb(f"xn{k}", [P, D]) for k in range(2)]
        xn_t = [sb(f"xn_t{k}", [P, KC, P]) for k in range(2)]
        row = [sb(f"row{k}", [P, RW]) for k in range(2)]
        res = [sb(f"res{k}", [P, D]) for k in range(2)]
        xt_ps = [ps(f"xt_ps{k}", D).rearrange("p (c n) -> p c n", c=KC) for k in range(2)]
        row_ps = [ps(f"row_ps{k}", NA) for k in range(2)]
        res_ps = [ps(f"res_ps{k}", D) for k in range(2)]

        own = sem("own")
        loaded = sem("loaded")
        weights_ready = sem("weights_ready")
        var_ready = sem("var_ready")
        root_ready = sem("root_ready")
        xn_ready = sem("xn_ready")
        xn_turned = sem("xn_turned")
        xn_t_ready = sem("xn_t_ready")
        products_ready = sem("products_ready")
        rows_ready = sem("rows_ready")
        res_ready = sem("res_ready")
        rows_out = [sem(f"rows_out{k}") for k in range(2)]
        NLOAD = 6
        block = ctx.enter_context(nc.Block())

        @block.sync
        def _(sp):
            for t, src in ((w_in[:, :, :], a["L1_gnn_W"].rearrange("(c p) o -> p c o", p=P)),
                           (w_res[:, :, :], a["L1_gnn_W_res"].rearrange("(c p) o -> p c o", p=P)),
                           (a_src[:, :], a["L1_gnn_a_src"].rearrange("h c -> (h c)").partition_broadcast(P)),
                           (a_dst[:, :], a["L1_gnn_a_dst"].rearrange("h c -> (h c)").partition_broadcast(P)),
                           (bias[:, :], a["L1_gnn_bias_gat"].partition_broadcast(P)),
                           (bias2[:, :], a["L1_gnn_b_res"].partition_broadcast(P))):
                sp.dma_start(t, src).then_inc(loaded, 16)

            def store(i, k):
                sp.wait_ge(rows_ready, i + 1)
                sp.dma_start(g["table1"][bass.ds(i * P, P), :], row[k][:, :]).then_inc(rows_out[k], 16)
                sp.wait_ge(res_ready, i + 1)
                sp.dma_start(g["residual"][bass.ds(i * P, P), :], res[k][:, :]).then_inc(rows_out[k], 16)

            in_pairs(sp, NB, store)
            sp.wait_ge(rows_out[0], 32 * ((NB + 1) // 2))
            sp.wait_ge(rows_out[1], 32 * (NB // 2))

        @block.vector
        def _(dve):
            v = nc.vector
            ch = Chain(dve, own)
            dve.wait_ge(loaded, 16 * NLOAD)
            heads = w_aug[:, :, 0:RW].rearrange("p c (h n) -> p c h n", n=HW_)
            for c in range(KC):
                v.tensor_copy(heads[:, c, :, 0:C], w_in[:, c, :].rearrange("p (h n) -> p h n", h=H))
                v.tensor_tensor(prod[:, c, :], w_in[:, c, :], a_src[:, :], ALU.mult)
            dve.drain()
            for c in range(KC):
                v.reduce_sum(heads[:, c, :, C:HW_], prod[:, c, :].rearrange("p (h n) -> p h n", h=H), AX_X)
            dve.drain()
            for c in range(KC):
                v.tensor_tensor(prod[:, c, :], w_in[:, c, :], a_dst[:, :], ALU.mult)
            v.tensor_tensor(bias[:, :], bias[:, :], bias2[:, :], ALU.add)
            dve.drain()
            for c in range(KC):
                ins = v.reduce_sum(w_aug[:, c, RW:NA], prod[:, c, :].rearrange("p (h n) -> p h n", h=H), AX_X)
            ins.then_inc(weights_ready, 1)
            emit_stats(nc, dve, ch, g["x"], stats, mean, var, half, var_ready)
            dve.wait_ge(root_ready, 1)
            ch.link(v.reciprocal(var[:, :], var[:, :]))
            dve.sem_inc(xn_turned, 2)

            def norm(i, k):
                dve.wait_ge(xn_turned, i + 1)
                v.tensor_scalar(xn[k][:, :], tile_at(g["xf"], i, D), mean[:, bass.ds(i, 1)], var[:, bass.ds(i, 1)],
                                ALU.subtract, ALU.mult).then_inc(xn_ready, 1)

            def finish(i, k, first=False):
                dve.wait_ge(products_ready, i + 1)
                if not first:
                    dve.wait_ge(rows_out[k], (i - k) * 16)
                v.tensor_tensor(res[k][:, :], res_ps[k][:, :], bias[:, :], ALU.add).then_inc(res_ready, 1)

            norm(0, 0)
            norm(1, 1)
            finish(0, 0, True)
            norm(2, 0)
            finish(1, 1, True)
            with dve.Fori(1, NB // 2) as j:
                norm(j * 2 + 1, 1)
                finish(j * 2, 0)
                norm(j * 2 + 2, 0)
                finish(j * 2 + 1, 1)
            finish(NB - 1, 0)
            v.memset(g["acc"][:, :].rearrange("p (n w) -> p n w", w=HW_)[:, :, C:HW_], 1.0)
            dve.wait_ge(rows_ready, NB)
            state = g["state"][:, :].rearrange("p (b two h) -> p b two h", two=2, h=H)
            top, dst = state[:, :, 1, :], state[:, :, 0, :]
            ch.link(v.tensor_tensor(top, top, dst, ALU.add))
            ch.link(v.scalar_tensor_tensor(top, top, 0.2, top, ALU.mult, ALU.max))

        @block.scalar
        def _(act):
            s = nc.scalar
            act.wait_ge(var_ready, 1)
            s.activation(var[:, :], var[:, :], ACT.Sqrt, bias=g["eps"][:, 0:1]).then_inc(root_ready, 1)

            def move(i, k):
                act.wait_ge(xn_turned, i + 3)
                s.copy(xn_t[k][:, :, :], xt_ps[k][:, :, :]).then_inc(xn_t_ready, 1)

            def rows(i, k, first=False):
                act.wait_ge(products_ready, i + 1)
                if not first:
                    act.wait_ge(rows_out[k], (i - k) * 16)
                heads = row_ps[k][:, 0:RW].rearrange("p (h n) -> p h n", n=HW_)
                s.copy(tile_at(g["acc"], i, RW).rearrange("p (h n) -> p h n", n=HW_)[:, :, 0:C], heads[:, :, 0:C])
                st = tile_at(g["state"], i, 2 * H)
                s.copy(st[:, 0:H], row_ps[k][:, RW:NA])
                s.copy(st[:, H:2 * H].unsqueeze(2), heads[:, :, C:HW_])
                s.copy(row[k][:, :], row_ps[k][:, 0:RW]).then_inc(rows_ready, 1)

            move(0, 0)
            move(1, 1)
            rows(0, 0, True)
            move(2, 0)
            rows(1, 1, True)
            with act.Fori(1, NB // 2) as j:
                move(j * 2 + 1, 1)
                rows(j * 2, 0)
                move(j * 2 + 2, 0)
                rows(j * 2 + 1, 1)
            rows(NB - 1, 0)

        @block.tensor
        def _(pe):
            t = nc.tensor
            pe.wait_ge(weights_ready, 1)

            def turn(i, k):
                pe.wait_ge(xn_ready, i + 1)
                for c in range(KC):
                    ins = t.transpose(xt_ps[k][:, c, :], xn[k][:, c * P:(c + 1) * P], g["ident"][:, :])
                ins.then_inc(xn_turned, 1)

            def rows(i, k, first=False):
                pe.wait_ge(xn_t_ready, i + 1)
                if not first:
                    pe.wait_ge(rows_ready, i - 1)
                    pe.wait_ge(res_ready, i - 1)
                for c in range(KC):
                    t.matmul(row_ps[k][:, :], xn_t[k][:, c, :], w_aug[:, c, :], start=(c == 0), stop=(c == KC - 1))
                for c in range(KC):
                    ins = t.matmul(res_ps[k][:, :], xn_t[k][:, c, :], w_res[:, c, :], start=(c == 0), stop=(c == KC - 1))
                ins.then_inc(products_ready, 1)

            turn(0, 0)
            turn(1, 1)
            rows(0, 0, True)
            turn(2, 0)
            rows(1, 1, True)
            with pe.Fori(1, NB // 2) as j:
                turn(j * 2 + 1, 1)
                rows(j * 2, 0)
                turn(j * 2 + 2, 0)
                rows(j * 2 + 1, 1)
            rows(NB - 1, 0)


def gat_steps_phase(nc, a, g):
    with ExitStack() as ctx:
        sb, ps, sem = memory(nc, ctx, "gat_steps")
        R = 4
        TRIPS = STEPS4 // R
        TH = T * H
        index = [sb(f"index{k}", [P, R * T], I32) for k in range(2)]
        rows = [sb(f"rows{k}", [P, T, RW]) for k in range(R)]
        onehot = [sb(f"onehot{k}", [P, T, P]) for k in range(2)]
        onehot_t = [sb(f"onehot_t{k}", [P, T, P]) for k in range(2)]
        score_t = sb("score_t", [TH, P])
        run_max = sb("run_max", [TH, P])
        begin = sb("begin", [P, T, H])
        cand = sb("cand", [P, T, H + 1])
        absent = sb("absent", [P, T])
        cand_m = sb("cand_m", [P, T, H])
        top = sb("top", [P, H])
        top2 = sb("top2", [P, H])
        dst_max = [sb(f"dst_max{k}", [P, 2 * H]) for k in range(2)]
        drop = [sb(f"drop{k}", [P, H]) for k in range(2)]
        fade = [sb(f"fade{k}", [P, H]) for k in range(2)]
        z = sb("z", [P, T, H])
        z2 = sb("z2", [P, T, H])
        arg = [sb(f"arg{k}", [P, T, H]) for k in range(2)]

        turn_ps = ps("turn_ps", 2 * P)
        onehot_ps = ps("onehot_ps", T * P).rearrange("p (t e) -> p t e", t=T)
        back_ps = ps("back_ps", TH).rearrange("p (t h) -> p t h", t=T)
        cand_ps = ps("cand_ps", T * (H + 1)).rearrange("p (t h) -> p t h", t=T)
        edge_ps = ps("edge_ps", T * 2 * H).rearrange("p (t h) -> p t h", t=T)
        weight_ps = ps("weight_ps", TH).rearrange("p (t h) -> p t h", t=T)
        sum_ps = [ps(f"sum_ps{k}", RW) for k in range(2)]

        own = sem("own")
        index_ready = sem("index_ready")
        slots_taken = sem("slots_taken")
        slots_free = sem("slots_free")
        rows_in = [sem(f"rows_in{k}") for k in range(R)]
        onehot_ready = sem("onehot_ready")
        begin_ready = sem("begin_ready")
        scores_turned = sem("scores_turned")
        score_t_ready = sem("score_t_ready")
        onehot_turned = sem("onehot_turned")
        onehot_t_ready = sem("onehot_t_ready")
        scanned = sem("scanned")
        back_ready = sem("back_ready")
        cand_ready = sem("cand_ready")
        cand_spread = sem("cand_spread")
        dst_max_ready = sem("dst_max_ready")
        fade_ready = sem("fade_ready")
        edge_ready = sem("edge_ready")
        arg_ready = sem("arg_ready")
        weights_ready = sem("weights_ready")
        rows_weighed = sem("rows_weighed")
        sums_added = sem("sums_added")
        block = ctx.enter_context(nc.Block())

        def headed(ap):
            return ap.rearrange("p t (h n) -> p (t h) n", n=HW_)

        @block.gpsimd
        def _(pool):
            pool.sem_inc(slots_free, R)

            def gather(j, k):
                pool.wait_ge(index_ready, j + 1)
                for r in range(R):
                    pool.wait_ge(slots_free, j * R + (r + 1))
                    pool.sem_inc(slots_taken, 1)
                    for t in range(T):
                        n = r * T + t
                        nc.gpsimd.indirect_dma_start(
                            out=rows[r][:, t, :], out_offset=None, in_=g["table1"][:, :],
                            in_offset=bass.IndirectOffsetOnAxis(ap=index[k][:, n:n + 1], axis=0)).then_inc(rows_in[r], 16)

            in_pairs(pool, TRIPS, gather)

        def run(eng, step):
            for r in range(R):
                step(0, r, r == 0, False)
            with eng.Fori(1, TRIPS - 1) as j:
                for r in range(R):
                    step(j, r, False, False)
            for r in range(R):
                step(TRIPS - 1, r, False, r == R - 1)

        def after(j, r):
            return (j, r + 1) if r < R - 1 else (j + 1, 0)

        @block.vector
        def _(dve):
            v = nc.vector
            ch = Chain(dve, own)

            def onehots(j, r):
                for t in range(T):
                    ins = v.tensor_scalar(onehot[r % 2][:, t, :], g["iota"][:, :],
                                          g["edges"][1][:, bass.ds(j * (R * T) + (r * T + t), 1)], None, ALU.is_equal)
                ins.then_inc(onehot_ready, 1)

            def scan(j, r):
                dve.wait_ge(score_t_ready, j * R + (r + 1))
                v.tensor_tensor_scan(run_max[:, :], turn_ps[0:TH, P:2 * P], score_t[:, :], NEG, ALU.add,
                                     ALU.max).then_inc(scanned, 1)

            def candidates(j, r):
                last = tile_at(g["edges"][3], j * R + r, T)
                dve.wait_ge(back_ready, j * R + (r + 1))
                v.tensor_scalar(cand[:, :, H], last, 1.0, None, ALU.mult)
                v.tensor_tensor(cand[:, :, 0:H], back_ps[:, :, :], last.unsqueeze(2).broadcast_to([P, T, H]),
                                ALU.mult).then_inc(cand_ready, 1)

            def block_at(j, r):
                return dve.value_load(g["block_of_step"][0:1, bass.ds(j * R + r, 1)], min_val=0, max_val=NB - 1)

            def maxima(j, r, b):
                st = tile_at(g["state"], b, 2 * H)
                new = dst_max[r % 2]
                v.tensor_scalar(new[:, 0:H], st[:, 0:H], 1.0, None, ALU.mult)
                dve.wait_ge(cand_spread, j * R + (r + 1))
                ch.link(v.tensor_scalar(absent[:, :], cand_ps[:, :, H], -NEG, NEG, ALU.mult, ALU.add))
                ch.link(v.tensor_tensor(cand_m[:, :, :], cand_ps[:, :, 0:H], absent[:, :].unsqueeze(2).broadcast_to([P, T, H]),
                                        ALU.add))
                ch.link(v.tensor_reduce(top[:, :], cand_m[:, :, :].rearrange("p t h -> p h t"), AX_X, ALU.max))
                ch.link(v.tensor_tensor(top2[:, :], top[:, :], st[:, 0:H], ALU.add))
                ch.link(v.scalar_tensor_tensor(top[:, :], top2[:, :], 0.2, top2[:, :], ALU.mult, ALU.max))
                ch.link(v.tensor_tensor(new[:, H:2 * H], top[:, :], st[:, H:2 * H], ALU.max))
                ch.link(v.tensor_tensor(drop[r % 2][:, :], st[:, H:2 * H], new[:, H:2 * H], ALU.subtract))
                v.tensor_scalar(st[:, H:2 * H], new[:, H:2 * H], 1.0, None, ALU.mult).then_inc(dst_max_ready, 1)

            def arguments(j, r):
                dve.wait_ge(edge_ready, j * R + (r + 1))
                z_, z2_ = z[:, :, :], z2[:, :, :]
                src = rows[r][:, :, :].rearrange("p t (h n) -> p t h n", n=HW_)[:, :, :, C]
                ch.link(v.tensor_tensor(z_, edge_ps[:, :, 0:H], src, ALU.add))
                ch.link(v.scalar_tensor_tensor(z2_, z_, 0.2, z_, ALU.mult, ALU.max))
                ch.link(v.tensor_tensor(z_, edge_ps[:, :, H:2 * H], z2_, ALU.subtract))
                v.tensor_scalar(arg[r % 2][:, :, :], z_, -1.0, 0.0, ALU.mult, ALU.min).then_inc(arg_ready, 1)

            def weigh(j, r):
                dve.wait_ge(weights_ready, j * R + (r + 1))
                msg = headed(rows[r][:, :, :])[:, :, 0:C]
                w = weight_ps[:, :, :].rearrange("p t h -> p (t h)").unsqueeze(2).broadcast_to([P, TH, C])
                v.tensor_tensor(msg, msg, w, ALU.mult).then_inc(rows_weighed, 1)

            def fold(j, r):
                b = block_at(j, r)
                acc = tile_at(g["acc"], b, RW)
                acc3 = acc.rearrange("p (h n) -> p h n", n=HW_)
                dve.wait_ge(fade_ready, j * R + (r + 1))
                ch.link(v.tensor_tensor(acc3, acc3, fade[r % 2][:, :].unsqueeze(2).broadcast_to([P, H, HW_]), ALU.mult))
                dve.wait_ge(slots_free, j * R + (r + 1 + R))
                v.tensor_tensor(acc, sum_ps[r % 2][:, :], acc, ALU.add).then_inc(sums_added, 1)
                dve.wait_ge(sums_added, j * R + (r + 1))

            def step(j, r, first, last):
                maxima(j, r, block_at(j, r))
                if not first:
                    fold(*((j, r - 1) if r else (j - 1, R - 1)))
                if not last:
                    onehots(*after(j, r))
                arguments(j, r)
                if not last:
                    scan(*after(j, r))
                weigh(j, r)
                if not last:
                    candidates(*after(j, r))

            LINKS = 7 + 1 + 3
            onehots(0, 0)
            scan(0, 0)
            candidates(0, 0)
            for r in range(R):
                step(0, r, r == 0, False)
            ch.end()
            with dve.Fori(1, TRIPS - 1) as j:
                ch.begin(j - 1, LINKS * R)
                for r in range(R):
                    step(j, r, False, False)
            ch.end(TRIPS - 2)
            for r in range(R):
                step(TRIPS - 1, r, False, r == R - 1)
            fold(TRIPS - 1, R - 1)

        @block.scalar
        def _(act):
            s = nc.scalar

            def indices(j, k):
                s.copy(index[k][:, :], tile_at(g["edges"][0], j, R * T)).then_inc(index_ready, 1)

            def begins(j, r):
                s.copy(begin[:, :, :], tile_at(g["edges"][2], j * R + r, T).unsqueeze(2).broadcast_to([P, T, H])
                       ).then_inc(begin_ready, 1)

            def scores(j, r):
                act.wait_ge(scores_turned, j * R + (r + 1))
                s.copy(score_t[:, :], turn_ps[0:TH, 0:P]).then_inc(score_t_ready, 1)

            def onehots(j, r):
                act.wait_ge(onehot_turned, j * R + (r + 1))
                s.copy(onehot_t[r % 2][:, :, :], onehot_ps[:, :, :]).then_inc(onehot_t_ready, 1)

            def fades(j, r):
                act.wait_ge(dst_max_ready, j * R + (r + 1))
                s.activation(fade[r % 2][:, :], drop[r % 2][:, :], ACT.Exp).then_inc(fade_ready, 1)

            def weights(j, r):
                act.wait_ge(arg_ready, j * R + (r + 1))
                x = arg[r % 2][:, :, :]
                s.activation(weight_ps[:, :, :], x, ACT.Exp)
                s.activation(headed(rows[r][:, :, :])[:, :, C:HW_].rearrange("p n one -> p (n one)"),
                             x.rearrange("p t h -> p (t h)"), ACT.Exp).then_inc(weights_ready, 1)

            def step(j, r, k, last, ahead):
                if not last:
                    begins(*after(j, r))
                fades(j, r)
                if not last:
                    scores(*after(j, r))
                    onehots(*after(j, r))
                weights(j, r)
                if ahead and r == 0:
                    indices(j + 1, 1 - k)

            indices(0, 0)
            begins(0, 0)
            scores(0, 0)
            onehots(0, 0)
            for r in range(R):
                step(0, r, 0, False, True)
            assert TRIPS % 2 == 1
            with act.Fori(0, (TRIPS - 3) // 2) as m:
                for r in range(R):
                    step(m * 2 + 1, r, 1, False, True)
                for r in range(R):
                    step(m * 2 + 2, r, 0, False, True)
            for r in range(R):
                step(TRIPS - 2, r, 1, False, True)
            for r in range(R):
                step(TRIPS - 1, r, 0, r == R - 1, False)

        @block.tensor
        def _(pe):
            t = nc.tensor

            def scores(j, r):
                pe.wait_ge(rows_in[r], (j + 1) * (16 * T))
                src = headed(rows[r][:, :, :])[:, :, C:HW_].rearrange("p n one -> p (n one)")
                t.transpose(turn_ps[0:TH, 0:P], src, g["ident"][:, :])
                pe.wait_ge(begin_ready, j * R + (r + 1))
                t.transpose(turn_ps[0:TH, P:2 * P], begin[:, :, :].rearrange("p t h -> p (t h)"),
                            g["ident"][:, :]).then_inc(scores_turned, 1)

            def onehots(j, r):
                pe.wait_ge(onehot_ready, j * R + (r + 1))
                for n in range(T):
                    ins = t.transpose(onehot_ps[:, n, :], onehot[r % 2][:, n, :], g["ident"][:, :])
                ins.then_inc(onehot_turned, 1)

            def back(j, r):
                pe.wait_ge(scanned, j * R + (r + 1))
                t.matmul(back_ps[:, :, :].rearrange("p t h -> p (t h)"), run_max[:, :], g["ident"][0:TH, 0:TH],
                         start=True, stop=True).then_inc(back_ready, 1)

            def spread(j, r):
                pe.wait_ge(cand_ready, j * R + (r + 1))
                for n in range(T):
                    ins = t.matmul(cand_ps[:, n, :], onehot[r % 2][:, n, :], cand[:, n, :], start=True, stop=True)
                ins.then_inc(cand_spread, 1)

            def to_edges(j, r):
                pe.wait_ge(dst_max_ready, j * R + (r + 1))
                pe.wait_ge(onehot_t_ready, j * R + (r + 1))
                for n in range(T):
                    ins = t.matmul(edge_ps[:, n, :], onehot_t[r % 2][:, n, :], dst_max[r % 2][:, :], start=True, stop=True)
                ins.then_inc(edge_ready, 1)

            def sums(j, r):
                pe.wait_ge(rows_weighed, j * R + (r + 1))
                for n in range(T):
                    ins = t.matmul(sum_ps[r % 2][:, :], onehot[r % 2][:, n, :], rows[r][:, n, :],
                                   start=(n == 0), stop=(n == T - 1))
                ins.then_inc(slots_free, 1)

            def step(j, r, first, last):
                to_edges(j, r)
                if not last:
                    scores(*after(j, r))
                    onehots(*after(j, r))
                    back(*after(j, r))
                sums(j, r)
                if not last:
                    spread(*after(j, r))

            scores(0, 0)
            onehots(0, 0)
            back(0, 0)
            spread(0, 0)
            run(pe, step)


def route_phase(nc, a, g):
    with ExitStack() as ctx:
        sb, ps, sem = memory(nc, ctx, "route")
        rden = sb("rden", [P, NB * H])
        res = [sb(f"res{k}", [P, D]) for k in range(2)]
        gamma = sb("gamma", [P, D])
        beta = sb("beta", [P, D])
        gate = sb("gate", [P, KC, E])
        gate_b = sb("gate_b", [P, E])
        node = sb("node", [P, D])
        stats = sb("stats", [P, 2, 6])
        mv = sb("mv", [P, 2, 2])
        ve = sb("ve", [P, 2])
        rstd = sb("rstd", [P, 2])
        minus_half = sb("minus_half", [P, 1])
        xn = [sb(f"xn{k}", [P, D]) for k in range(2)]
        xn_t = sb("xn_t", [P, KC, P])
        down = sb("down", [P, E])
        valid = sb("valid", [P, 1])
        lane = sb("lane", [P, E])
        logit = sb("logit", [P, NB, E])
        ex = sb("ex", [P, NB, E])
        pr = sb("pr", [P, NB, E])
        score = sb("score", [P, NB, E])
        pick = sb("pick", [P, NB, E])
        totals = sb("totals", [P, NB, E])
        before = sb("before", [P, NB, E])
        one = sb("one", [P, NB])
        big = sb("big", [P, NB])
        inv = sb("inv", [P, NB])
        place = sb("place", [P, NB])
        home = sb("home", [P, NB])
        slot = sb("slot", [P, NB])
        send = sb("send", [P, NB])
        index = [sb(f"index{k}", [P, 1], I32) for k in range(2)]

        xt_ps = ps("xt_ps", D).rearrange("p (c n) -> p c n", c=KC)
        logit_ps = ps("logit_ps", E)
        upto_ps = ps("upto_ps", NB * E).rearrange("p (b e) -> p b e", e=E)
        total_ps = ps("total_ps", NB * E).rearrange("p (b e) -> p b e", e=E)

        own = sem("own")
        loaded = sem("loaded")
        const_ready = sem("const_ready")
        res_in = [sem(f"res_in{k}") for k in range(2)]
        res_used = sem("res_used")
        var_ready = sem("var_ready")
        rstd_ready = sem("rstd_ready")
        xn_ready = sem("xn_ready")
        xn_turned = sem("xn_turned")
        xn_t_ready = sem("xn_t_ready")
        logits_ready = sem("logits_ready")
        logits_kept = sem("logits_kept")
        shifted = sem("shifted")
        exp_ready = sem("exp_ready")
        picked = sem("picked")
        counted = sem("counted")
        placed = sem("placed")
        index_ready = sem("index_ready")
        rows_out = [sem(f"rows_out{k}") for k in range(2)]
        index_free = sem("index_free")
        block = ctx.enter_context(nc.Block())
        NLOAD = 4

        @block.sync
        def _(sp):
            with nc.allow_non_contiguous_dma(reason="the gate's 8 columns"):
                for t, src in ((gamma[:, :], a["L1_gnn_gamma"].partition_broadcast(P)),
                               (beta[:, :], a["L1_gnn_beta"].partition_broadcast(P)),
                               (gate[:, :, :], a["L1_ffn_gate_w"].rearrange("(c p) e -> p c e", p=P)),
                               (gate_b[:, :], a["L1_ffn_gate_b"].partition_broadcast(P))):
                    sp.dma_start(t, src).then_inc(loaded, 16)

            def load(i, k):
                sp.wait_ge(res_used, i + 1)
                sp.dma_start(res[k][:, :], g["residual"][bass.ds(i * P, P), :]).then_inc(res_in[k], 16)

            in_pairs(sp, NB, load)

        @block.vector
        def _(dve):
            v = nc.vector
            ch = Chain(dve, own)
            dve.sem_inc(res_used, 2)
            v.tensor_scalar(down[:, :], g["iota"][:, 0:E], -1.0, float(E), ALU.mult, ALU.add)
            v.tensor_scalar(lane[:, :], g["iota"][:, 0:E], float(PITCH), None, ALU.mult)
            v.tensor_scalar(valid[:, :], g["pidx"][:, :], float(TAIL), None, ALU.is_lt)
            v.memset(minus_half[:, :], -0.5).then_inc(const_ready, 1)
            den = g["acc"][:, :].rearrange("p (n w) -> p n w", w=HW_)[:, :, C]
            ch.link(v.tensor_scalar(rden[:, :], den, 1e-16, None, ALU.add))
            ch.link(v.reciprocal(rden[:, :], rden[:, :]))
            dve.wait_ge(loaded, 16 * NLOAD)

            def norm_stats(c, src):
                v.bn_stats(stats[:, c, :], src)
                dve.drain()
                ch.link(v.bn_aggr(mv[:, c, :], stats[:, c, :]))
                v.tensor_scalar(ve[:, c:c + 1], mv[:, c, 1:2], LN_EPS, None, ALU.add).then_inc(var_ready, 1)

            def finish(i, k):
                xb = tile_at(g["xf"], i, D)
                row = tile_at(g["acc"], i, RW)
                msg = row.rearrange("p (h n) -> p h n", n=HW_)[:, :, 0:C]
                r = tile_at(rden, i, H).unsqueeze(2).broadcast_to([P, H, C])
                ch.link(v.tensor_tensor(node[:, :].rearrange("p (h n) -> p h n", h=H), msg, r, ALU.mult))
                dve.wait_ge(res_in[k], ((i - k) * 8) + 16)
                ch.link(v.tensor_tensor(node[:, :], node[:, :], res[k][:, :], ALU.add))
                norm_stats(0, node[:, :])
                dve.sem_inc(res_used, 1)
                dve.wait_ge(rstd_ready, i * 2 + 1)
                ch.link(v.tensor_scalar(node[:, :], node[:, :], mv[:, 0, 0:1], rstd[:, 0:1], ALU.subtract, ALU.mult))
                ch.link(v.tensor_tensor(node[:, :], node[:, :], gamma[:, :], ALU.mult))
                ch.link(v.tensor_tensor(node[:, :], node[:, :], beta[:, :], ALU.add))
                ch.link(v.tensor_tensor(node[:, :], node[:, :], xb, ALU.add))
                norm_stats(1, node[:, :])
                dve.wait_ge(rstd_ready, i * 2 + 2)
                v.tensor_scalar(xn[k][:, :], node[:, :], mv[:, 1, 0:1], rstd[:, 1:2], ALU.subtract, ALU.mult).then_inc(xn_ready, 1)
                dve.wait_ge(logits_ready, i + 1)
                v.tensor_tensor(logit[:, bass.ds(i, 1), :].rearrange("p one e -> p (one e)"), logit_ps[:, :], gate_b[:, :],
                                ALU.add).then_inc(logits_kept, 1)

            LINKS = 8
            ch.end()
            with dve.Fori(0, NB // 2) as j:
                ch.begin(j, 2 * LINKS)
                finish(j * 2, 0)
                finish(j * 2 + 1, 1)
            ch.end(NB // 2)
            finish(NB - 1, 0)

            def wide(t):
                return t[:, :].unsqueeze(2).broadcast_to([P, NB, E])

            def over_blocks(t):
                return t[:, :].unsqueeze(1).broadcast_to([P, NB, E])

            dve.wait_ge(logits_kept, NB)
            ch.link(v.reduce_max(big[:, :], logit[:, :, :], AX_X))
            v.tensor_tensor(logit[:, :, :], logit[:, :, :], wide(big), ALU.subtract).then_inc(shifted, 1)
            dve.wait_ge(exp_ready, 1)
            ch.link(v.reduce_sum(inv[:, :], ex[:, :, :], AX_X))
            ch.link(v.reciprocal(inv[:, :], inv[:, :]))
            ch.link(v.tensor_tensor(pr[:, :, :], ex[:, :, :], wide(inv), ALU.mult))
            ch.link(v.reduce_max(big[:, :], pr[:, :, :], AX_X))
            v.tensor_copy(g["acc"][:, :].rearrange("p (b w) -> p b w", w=RW)[:, :, D], big[:, :])
            ch.link(v.tensor_tensor(score[:, :, :], pr[:, :, :], wide(big), ALU.is_equal))
            ch.link(v.tensor_tensor(score[:, :, :], score[:, :, :], over_blocks(down), ALU.mult))
            ch.link(v.reduce_max(one[:, :], score[:, :, :], AX_X))
            ch.link(v.tensor_tensor(pick[:, :, :], score[:, :, :], wide(one), ALU.is_equal))
            v.tensor_scalar(pick[:, NB - 1, :], pick[:, NB - 1, :], valid[:, 0:1], None, ALU.mult).then_inc(picked, 1)
            dve.wait_ge(counted, 1)
            ch.link(v.tensor_copy(totals[:, :, :], total_ps[:, :, :]))
            for e in range(E):
                ins = v.tensor_tensor_scan(before[:, :, e], totals[:, :, e], totals[:, :, e], 0.0, ALU.add, ALU.bypass)
            ch.link(ins)
            ch.link(v.tensor_tensor(before[:, :, :], before[:, :, :], totals[:, :, :], ALU.subtract))
            ch.link(v.tensor_tensor(before[:, :, :], upto_ps[:, :, :], before[:, :, :], ALU.add))
            ch.link(v.tensor_tensor(before[:, :, :], before[:, :, :], pick[:, :, :], ALU.mult))
            ch.link(v.reduce_sum(place[:, :], before[:, :, :], AX_X))
            ch.link(v.tensor_tensor(score[:, :, :], pick[:, :, :], over_blocks(lane), ALU.mult))
            ch.link(v.reduce_sum(home[:, :], score[:, :, :], AX_X))
            ch.link(v.tensor_scalar(g["kept"][:, :], place[:, :], float(CAP), None, ALU.is_le))
            ch.link(v.tensor_scalar(place[:, :], place[:, :], -1.0, None, ALU.add))
            ch.link(v.tensor_scalar(slot[:, :], place[:, :], float(CAP - 1), 0.0, ALU.min, ALU.max))
            ch.link(v.tensor_tensor(slot[:, :], slot[:, :], home[:, :], ALU.add))
            v.tensor_copy(g["slot"][:, :], slot[:, :])
            ch.link(v.tensor_scalar(send[:, :], g["kept"][:, :], -float(E * PITCH), float(E * PITCH), ALU.mult, ALU.add))
            ch.link(v.tensor_tensor(send[:, :], send[:, :], slot[:, :], ALU.add))
            v.tensor_scalar(valid[:, :], valid[:, :], -float(E * PITCH), float(E * PITCH), ALU.mult, ALU.add)
            dve.drain()
            v.tensor_tensor(send[:, NB - 1:NB], send[:, NB - 1:NB], valid[:, :], ALU.add).then_inc(placed, 1)

        @block.scalar
        def _(act):
            s = nc.scalar

            def turned(i, k):
                act.wait_ge(xn_turned, i + 1)
                s.copy(xn_t[:, :, :], xt_ps[:, :, :])
                s.copy(tile_at(g["acc"], i, RW)[:, 0:D], xn[k][:, :])
                s.copy(tile_at(g["xf"], i, D), node[:, :]).then_inc(xn_t_ready, 1)

            in_pairs(act, NB, turned)
            act.wait_ge(shifted, 1)
            s.activation(ex[:, :, :], logit[:, :, :], ACT.Exp).then_inc(exp_ready, 1)
            act.wait_ge(placed, 1)

            def indices(i, k):
                act.wait_ge(index_free, i + 1)
                s.copy(index[k][:, :], send[:, bass.ds(i, 1)]).then_inc(index_ready, 1)

            in_pairs(act, NB, indices)

        @block.tensor
        def _(pe):
            t = nc.tensor
            pe.wait_ge(loaded, 16 * NLOAD)

            def gates(i, k):
                pe.wait_ge(xn_ready, i + 1)
                for c in range(KC):
                    ins = t.transpose(xt_ps[:, c, :], xn[k][:, c * P:(c + 1) * P], g["ident"][:, :])
                ins.then_inc(xn_turned, 1)
                pe.wait_ge(xn_t_ready, i + 1)
                for c in range(KC):
                    ins = t.matmul(logit_ps[:, :], xn_t[:, c, :], gate[:, c, :], start=(c == 0), stop=(c == KC - 1))
                ins.then_inc(logits_ready, 1)

            in_pairs(pe, NB, gates)
            pe.wait_ge(picked, 1)
            pk = pick[:, :, :].rearrange("p b e -> p (b e)")
            t.matmul(upto_ps.rearrange("p b e -> p (b e)"), g["upper"][:, :], pk, start=True, stop=True)
            t.matmul(total_ps.rearrange("p b e -> p (b e)"), g["ones"][:, :], pk, start=True, stop=True).then_inc(counted, 1)

        @block.gpsimd
        def _(pool):
            pool.wait_ge(const_ready, 1)
            with pool.Fori(0, NB) as i:
                for c in range(2):
                    pool.wait_ge(var_ready, i * 2 + (c + 1))
                    nc.gpsimd.tensor_tensor(rstd[:, c:c + 1], ve[:, c:c + 1], minus_half[:, :], ALU.pow).then_inc(rstd_ready, 1)
            pool.sem_inc(index_free, 2)
            pool.wait_ge(placed, 1)
            for i in range(NB):
                k = i % 2
                pool.wait_ge(index_ready, i + 1)
                nc.gpsimd.indirect_dma_start(
                    out=g["sent"][:, :], in_=g["acc"][:, i * RW:(i + 1) * RW], in_offset=None,
                    out_offset=bass.IndirectOffsetOnAxis(ap=index[k][:, 0:1], axis=0),
                    bounds_check=E * PITCH - 1, oob_is_err=False).then_inc(rows_out[k], 16)
                pool.wait_ge(rows_out[k], 16 * (i // 2 + 1))
                pool.sem_inc(index_free, 1)


def expert_phase(nc, a, g):
    with ExitStack() as ctx:
        sb, ps, sem = memory(nc, ctx, "expert")
        NT = -(-CAP // P)
        CP = NT * P
        HALF = CP // 2
        FC = F // P
        w1 = [sb(f"w1_{k}", [P, KC, F]) for k in range(2)]
        w2 = [sb(f"w2_{k}", [P, FC, D]) for k in range(2)]
        xe = [sb(f"xe{k}", [P, NT, RW]) for k in range(2)]
        xe_t = sb("xe_t", [P, KC, CP])
        hid = sb("hid", [P, FC, CP])
        b1_in = sb("b1_in", [E * FC, P])
        b1 = sb("b1", [P, E * FC])
        b1_e = [sb(f"b1_e{k}", [P, FC]) for k in range(2)]
        b2 = sb("b2", [P, E * D])
        y = [sb(f"y{k}", [P, D]) for k in range(2)]
        flag = [sb(f"flag{n}", [P, D], I32) for n in range(3)]
        fill = [sb(f"fill{n}", [P, D]) for n in range(3)]
        xt_ps = [ps(f"xt_ps{k}", 512).rearrange("p (t n) -> p t n", n=P) for k in range(2)]
        hid_ps = [ps(f"hid_ps{k}", HALF) for k in range(2)]
        y_ps = [ps(f"y_ps{k}", D) for k in range(2)]

        own = sem("own")
        bias_in = sem("bias_in")
        b1_turned = sem("b1_turned")
        b1_ready = sem("b1_ready")
        b1_picked = sem("b1_picked")
        loaded = [sem(f"loaded{k}") for k in range(2)]
        rows_turned = sem("rows_turned")
        rows_t_ready = sem("rows_t_ready")
        up_ready = sem("up_ready")
        hid_ready = sem("hid_ready")
        down_ready = sem("down_ready")
        y_read = sem("y_read")
        y_ready = sem("y_ready")
        y_out = [sem(f"y_out{k}") for k in range(2)]
        block = ctx.enter_context(nc.Block())
        NX = KC * NT // 4
        NU = FC * 2
        fill_values = (1.0e4, -1.0e4, 0.0)
        FMAX = 3.4028234663852886e38

        @block.sync
        def _(sp):
            sp.dma_start(b1_in[:, :], a["L1_ffn_b1"].rearrange("e (c p) -> (e c) p", p=P)).then_inc(bias_in, 16)
            sp.dma_start(b2[:, :], a["L1_ffn_b2"].rearrange("e d -> (e d)").partition_broadcast(P)).then_inc(bias_in, 16)

            def load(e, k, wait=True):
                if wait:
                    sp.wait_ge(down_ready, (e - 1) * NT)
                sp.dma_start(xe[k][:, :, :], g["sent"][bass.ds(e * PITCH, PITCH), :].rearrange("(t p) w -> p t w", p=P)
                             ).then_inc(loaded[k], 16)
                sp.dma_start(w1[k][:, :, :], a["L1_ffn_w1"][bass.ds(e * D, D), :].rearrange("(c p) f -> p c f", p=P)
                             ).then_inc(loaded[k], 16)
                sp.dma_start(w2[k][:, :, :], a["L1_ffn_w2"][bass.ds(e * F, F), :].rearrange("(c p) d -> p c d", p=P)
                             ).then_inc(loaded[k], 16)

            def store(e):
                for t in range(NT):
                    sp.wait_ge(y_ready, e * NT + (t + 1))
                    sp.dma_start(g["answers"][bass.ds(e * PITCH + t * P, P), :], y[t % 2][:, :]).then_inc(y_out[t % 2], 16)

            load(0, 0, False)
            load(1, 1, False)
            with sp.Fori(0, E // 2 - 1) as j:
                store(j * 2)
                load(j * 2 + 2, 0)
                store(j * 2 + 1)
                load(j * 2 + 3, 1)
            store(E - 2)
            store(E - 1)
            for k in range(2):
                sp.wait_ge(y_out[k], 16 * E * NT // 2)

        @block.vector
        def _(dve):
            v = nc.vector
            ch = Chain(dve, own)
            for n in range(3):
                ch.link(v.memset(fill[n][:, :], fill_values[n]))
            dve.wait_ge(bias_in, 32)

            def outs(e, k, first):
                for t in range(NT):
                    y_, yp = y[t % 2][:, :], y_ps[t % 2][:, :]
                    dve.wait_ge(down_ready, e * NT + (t + 1))
                    if not (first and t < 2):
                        dve.wait_ge(y_out[t % 2], e * (8 * NT) + (t // 2) * 16)
                    v.tensor_tensor(y_, yp, b2[:, bass.ds(e * D, D)], ALU.add).then_inc(y_read, 1)
                    dve.wait_ge(y_read, e * NT + (t + 1))
                    ch.link(v.tensor_scalar(y_, y_, xe[k][:, t, D:D + 1], None, ALU.mult))
                    v.tensor_scalar(flag[0][:, :], y_, FMAX, None, ALU.is_gt)
                    v.tensor_scalar(flag[1][:, :], y_, -FMAX, None, ALU.is_lt)
                    v.tensor_tensor(flag[2][:, :], y_, y_, ALU.not_equal)
                    for n in range(3):
                        dve.drain()
                        ins = v.copy_predicated(y_, flag[n][:, :], fill[n][:, :])
                    ins.then_inc(y_ready, 1)

            outs(0, 0, True)
            outs(1, 1, False)
            ch.end()
            with dve.Fori(1, E // 2) as j:
                ch.begin(j - 1, 2 * NT)
                outs(j * 2, 0, False)
                outs(j * 2 + 1, 1, False)
            ch.end(E // 2 - 1)

        @block.scalar
        def _(act):
            s = nc.scalar
            act.wait_ge(b1_turned, 1)
            s.copy(b1[:, :], xt_ps[0][:, 0, 0:E * FC]).then_inc(b1_ready, 1)
            act.wait_ge(b1_ready, 1)

            def rows(e, n):
                c, q = divmod(n, NT // 4)
                act.wait_ge(rows_turned, e * NX + (n + 1))
                s.copy(xe_t[:, c, q * 512:(q + 1) * 512].rearrange("p (t n) -> p t n", n=P), xt_ps[n % 2][:, :, :]
                       ).then_inc(rows_t_ready, 1)

            def expert(e, k):
                s.copy(b1_e[k][:, :], b1[:, bass.ds(e * FC, FC)]).then_inc(b1_picked, 1)
                for n in range(NX):
                    rows(e, n)
                act.wait_ge(b1_picked, e + 1)
                for u in range(NU):
                    f, half = divmod(u, 2)
                    act.wait_ge(up_ready, e * NU + (u + 1))
                    s.activation(hid[:, f, half * HALF:(half + 1) * HALF], hid_ps[u % 2][:, :], ACT.Relu,
                                 bias=b1_e[k][:, f:f + 1]).then_inc(hid_ready, 1)

            in_pairs(act, E, expert)

        @block.tensor
        def _(pe):
            t = nc.tensor
            pe.wait_ge(bias_in, 32)
            t.transpose(xt_ps[0][:, 0, 0:E * FC], b1_in[:, :], g["ident"][0:E * FC, 0:E * FC]).then_inc(b1_turned, 1)
            pe.wait_ge(b1_ready, 1)

            def expert(e, k, first):
                pe.wait_ge(loaded[k], (e - k) * 24 + 48)
                for n in range(NX):
                    c, q = divmod(n, NT // 4)
                    if n >= 2:
                        pe.wait_ge(rows_t_ready, e * NX + (n - 1))
                    for i in range(4):
                        ins = t.transpose(xt_ps[n % 2][:, i, :], xe[k][:, q * 4 + i, c * P:(c + 1) * P], g["ident"][:, :])
                    ins.then_inc(rows_turned, 1)
                pe.wait_ge(rows_t_ready, e * NX + NX)
                for u in range(NU):
                    f, half = divmod(u, 2)
                    if u >= 2:
                        pe.wait_ge(hid_ready, e * NU + (u - 1))
                    for c in range(KC):
                        ins = t.matmul(hid_ps[u % 2][:, :], w1[k][:, c, f * P:(f + 1) * P],
                                       xe_t[:, c, half * HALF:(half + 1) * HALF], start=(c == 0), stop=(c == KC - 1))
                    ins.then_inc(up_ready, 1)
                pe.wait_ge(hid_ready, e * NU + NU)
                for n in range(NT):
                    if not (first and n < 2):
                        pe.wait_ge(y_read, e * NT + (n - 1))
                    for f in range(FC):
                        ins = t.matmul(y_ps[n % 2][:, :], hid[:, f, n * P:(n + 1) * P], w2[k][:, f, :],
                                       start=(f == 0), stop=(f == FC - 1))
                    ins.then_inc(down_ready, 1)

            expert(0, 0, True)
            expert(1, 1, False)
            with pe.Fori(1, E // 2) as j:
                expert(j * 2, 0, False)
                expert(j * 2 + 1, 1, False)


def combine_phase(nc, a, g, out):
    with ExitStack() as ctx:
        sb, ps, sem = memory(nc, ctx, "combine")
        R = 4
        index = [sb(f"index{k}", [P, 1], I32) for k in range(R)]
        rows = [sb(f"rows{k}", [P, D]) for k in range(R)]
        index_ready = sem("index_ready")
        rows_in = [sem(f"rows_in{k}") for k in range(R)]
        rows_added = sem("rows_added")
        stored = sem("stored")
        block = ctx.enter_context(nc.Block())

        @block.scalar
        def _(act):
            for i in range(NB):
                if i >= R:
                    act.wait_ge(rows_added, i - R + 1)
                nc.scalar.copy(index[i % R][:, :], g["slot"][:, i:i + 1]).then_inc(index_ready, 1)

        @block.gpsimd
        def _(pool):
            for i in range(NB):
                pool.wait_ge(index_ready, i + 1)
                if i >= R:
                    pool.wait_ge(rows_added, i - R + 1)
                nc.gpsimd.indirect_dma_start(
                    out=rows[i % R][:, :], out_offset=None, in_=g["answers"][:, :],
                    in_offset=bass.IndirectOffsetOnAxis(ap=index[i % R][:, 0:1], axis=0)).then_inc(rows_in[i % R], 16)

        @block.vector
        def _(dve):
            for i in range(NB):
                dve.wait_ge(rows_in[i % R], 16 * (i // R + 1))
                xb = g["x"][:, i, :]
                nc.vector.scalar_tensor_tensor(xb, rows[i % R][:, :], g["kept"][:, i:i + 1], xb, ALU.mult,
                                               ALU.add).then_inc(rows_added, 1)

        @block.sync
        def _(sp):
            for i in range(NB):
                n = P if i < NB - 1 else TAIL
                sp.wait_ge(rows_added, i + 1)
                sp.dma_start(out[i * P:i * P + n, :], g["x"][0:n, i, :]).then_inc(stored, 16)
            sp.wait_ge(stored, 16 * NB)


def program(nc, a, out):
    with ExitStack() as whole:
        def sb(name, shape, dt=F32, ctx=whole):
            return ctx.enter_context(nc.sbuf_tensor(name, shape, dt))

        g = {"table0": nc.dram_tensor("table0", [NB * P, D], F32).ap(),
             "table1": nc.dram_tensor("table1", [NB * P, RW], F32).ap(),
             "residual": nc.dram_tensor("residual", [NB * P, D], F32).ap(),
             "sent": nc.dram_tensor("sent", [E * PITCH, RW], F32).ap(),
             "answers": nc.dram_tensor("answers", [E * PITCH, D], F32).ap(),
             "x": sb("x_all", [P, NB, D]),
             "iota": sb("iota", [P, P]), "pidx": sb("pidx", [P, 1]), "ident": sb("ident", [P, P]),
             "upper": sb("upper", [P, P]), "ones": sb("ones", [P, P]), "eps": sb("eps", [P, 1]),
             "kept": sb("kept", [P, NB]), "slot": sb("slot", [P, NB])}
        g["xf"] = g["x"][:, :, :].rearrange("p b d -> p (b d)")
        with ExitStack() as graph:
            g["edges"] = [sb(f"edges{n}", [P, SQ * P * T], F32, graph) for n in range(4)]
            g["block_of_step"] = sb("block_of_step", [1, SQ * P], I32, graph)
            g["dinv"] = sb("dinv", [P, NB], F32, graph)
            g["state"] = sb("state", [P, NB * 2 * H], F32, graph)
            setup_phase(nc, a, g)
            g["acc"] = sb("acc", [P, NB * RW], F32, graph)
            gcn_table_phase(nc, a, g)
            gcn_steps_phase(nc, a, g)
            moe_phase(nc, a, g)
            gat_table_phase(nc, a, g)
            gat_steps_phase(nc, a, g)
            route_phase(nc, a, g)
        expert_phase(nc, a, g)
        combine_phase(nc, a, g, out)


INS = ["x", "src", "dst",
       "L0_gnn_W", "L0_gnn_b", "L0_gnn_gamma", "L0_gnn_beta",
       "L0_ffn_router_w", "L0_ffn_w1", "L0_ffn_b1", "L0_ffn_w2", "L0_ffn_b2",
       "L1_gnn_W", "L1_gnn_a_src", "L1_gnn_a_dst", "L1_gnn_bias_gat", "L1_gnn_W_res", "L1_gnn_b_res",
       "L1_gnn_gamma", "L1_gnn_beta",
       "L1_ffn_gate_w", "L1_ffn_gate_b", "L1_ffn_w1", "L1_ffn_b1", "L1_ffn_w2", "L1_ffn_b2"]


def kernel(**inputs):
    import numpy as _np
    import concourse.bacc as _bacc
    from concourse.bass_utils import run_bass_kernel_spmd as _run

    nc = _bacc.Bacc("TRN2", target_bir_lowering=False, num_devices=1)
    arrays, aps = {}, {}
    for name in INS:
        v = _np.ascontiguousarray(inputs[name])
        if name == "x":
            v = _np.concatenate([v, _np.zeros((NB * P - NODES, D), v.dtype)])
        if name in ("src", "dst"):
            pad = _np.full(NGP * GROUP - EDGES, PAD_DST if name == "dst" else 0, v.dtype)
            v = _np.concatenate([v, pad]).reshape(NGP, GROUP)
        if name in ("L1_ffn_w1", "L1_ffn_w2"):
            v = v.reshape(-1, v.shape[-1])
        arrays[f"in_{name}"] = v
        aps[name] = nc.dram_tensor(f"in_{name}", v.shape, mybir.dt.from_np(v.dtype), kind="ExternalInput").ap()
    out = nc.dram_tensor("out_0", (NODES, D), F32, kind="ExternalOutput").ap()
    program(nc, aps, out)
    r = _run(nc, [arrays], core_ids=[0])
    return r.results[0]["out_0"]
```

```python
from contextlib import ExitStack

import concourse.bass as bass
from concourse import mybir

ALU = mybir.AluOpType
ACT = mybir.ActivationFunctionType
AX_X = mybir.AxisListType.X
F32 = mybir.dt.float32
BF16 = mybir.dt.bfloat16
I32 = mybir.dt.int32
U32 = mybir.dt.uint32

P = 128
NODES = 6250
D = 256
KC = D // P
NB = -(-NODES // P)
TAIL = NODES - (NB - 1) * P
EDGES = 206250
T = 4
GROUP = T * P
NG = -(-EDGES // GROUP)
NGP = NG + 1
ECOLS = NGP * GROUP // P
PAD_DST = 8191
STEPS = NG - 1 + NB - 1 + 1
STEPS4 = -(-STEPS // 4) * 4
SQ = -(-STEPS4 // P)
H = 4
C = D // H
HW_ = C + 1
RW = H * HW_
LN_EPS = 1e-5
E = 8
NEG = -3.0e38
F = 1024
CAP = -(-5 * NODES // (4 * E))
PITCH = -(-CAP // P) * P
HCH = 16


class Chain:

    def __init__(self, eng, sem):
        self.eng, self.sem, self.base = eng, sem, 0
        self.i, self.per, self.k = 0, None, 0

    def begin(self, i=0, per=None):
        assert self.k == 0
        self.i, self.per, self.k = i, per, 0

    def link(self, ins):
        self.k += 1
        ins.then_inc(self.sem, 1)
        self.eng.wait_ge(self.sem, self.i * (self.per or 0) + (self.base + self.k))

    def link_after(self, ins, between):
        self.k += 1
        ins.then_inc(self.sem, 1)
        if between is not None:
            between()
        self.eng.wait_ge(self.sem, self.i * (self.per or 0) + (self.base + self.k))

    def note(self, ins):
        self.k += 1
        ins.then_inc(self.sem, 1)

    def settle(self):
        self.eng.wait_ge(self.sem, self.i * (self.per or 0) + (self.base + self.k))

    def end(self, trips=1):
        assert self.per is None or self.k == self.per, (self.k, self.per)
        self.base += self.k * trips
        self.i, self.per, self.k = 0, None, 0


def tile_at(t, i, width):
    return t[:, bass.ds(i * width, width)]


def in_pairs(eng, n, body):
    with eng.Fori(0, n // 2) as k:
        body(k * 2, 0)
        body(k * 2 + 1, 1)
    if n % 2:
        body(n - 1, 0)


def memory(nc, ctx, phase):

    def sb(name, shape, dt=F32):
        return ctx.enter_context(nc.sbuf_tensor(f"{phase}_{name}", shape, dt))

    def ps(name, width):
        return ctx.enter_context(nc.psum_tensor(f"{phase}_{name}", [P, 512], F32))[:, 0:width]

    def sem(name):
        return ctx.enter_context(nc.semaphore(f"{phase}_{name}"))

    return sb, ps, sem


def setup_phase(nc, a, g):
    with ExitStack() as ctx:
        sb, ps, sem = memory(nc, ctx, "setup")

        iota_i = sb("iota_i", [P, SQ * P], I32)
        iota_f = sb("iota_f", [P, SQ * P])
        pidx_i = sb("pidx_i", [P, 1], I32)
        pidx = sb("pidx", [P, 1])
        spos_i = sb("spos_i", [P, SQ], I32)
        spos = sb("spos", [P, SQ])
        last_i = sb("last_i", [1, NG - 1], I32)
        last_f = sb("last_f", [1, NG - 1])
        ones_row = sb("ones_row", [1, P])
        limit = sb("limit", [P, 1])
        below = sb("below", [P, NG - 1])
        nbelow = sb("nbelow", [P, 1])
        rank = sb("rank", [P, 1])
        far = sb("far", [P, 1])
        passed = sb("passed", [P, SQ * P])
        blk = sb("blk", [P, SQ])
        grp = sb("grp", [P, SQ])
        grp_i = sb("grp_i", [P, SQ], I32)
        dst_s = sb("dst_s", [P, SQ * GROUP], I32)
        src_s = sb("src_s", [P, SQ * GROUP], I32)
        work = sb("work", [P, 4, GROUP])
        dflat = sb("dflat", [P, ECOLS], I32)
        dlo_i = sb("dlo_i", [P, ECOLS], I32)
        dhi_i = sb("dhi_i", [P, ECOLS], I32)
        dlo = sb("dlo", [P, ECOLS])
        dhi = sb("dhi", [P, ECOLS])
        iota_b = sb("iota_b", [P, P], BF16)
        oh_lo = [sb(f"oh_lo{k}", [P, HCH, P], BF16) for k in range(2)]
        oh_hi = [sb(f"oh_hi{k}", [P, HCH, NB], BF16) for k in range(2)]
        zero_b = sb("zero_b", [P, P], BF16)

        last_ps = ps("last_ps", NG - 1)
        blk_ps = ps("blk_ps", SQ)
        row_ps = ps("row_ps", SQ * P)[0:1, :]
        hist_ps = ps("hist_ps", NB)
        turn_ps = [ps(f"turn_ps{k}", T * P).rearrange("p (t e) -> p t e", t=T) for k in range(2)]

        zeros = sb("zeros", [P, RW])
        zeros_ready = sem("zeros_ready")
        zeroed = sem("zeroed")
        iotas = sem("iotas")
        x_in = sem("x_in")
        last_in = sem("last_in")
        dflat_in = sem("dflat_in")
        own = sem("own")
        consts = sem("consts")
        last_wide = sem("last_wide")
        passed_ready = sem("passed_ready")
        blocks_counted = sem("blocks_counted")
        groups_known = sem("groups_known")
        edges_in = [sem(f"edges_in{q}") for q in range(SQ)]
        work_ready = sem("work_ready")
        turned = sem("turned")
        turn_free = sem("turn_free")
        onehots = sem("onehots")
        onehots_used = sem("onehots_used")
        split_ready = sem("split_ready")
        hist_done = sem("hist_done")
        gated = sem("gated")
        block = ctx.enter_context(nc.Block())
        NTURN = SQ * 4
        CHUNKS = ECOLS // HCH
        assert ECOLS % HCH == 0

        @block.gpsimd
        def _(pool):
            nc.gpsimd.iota(iota_i[:, :], [[1, SQ * P]], base=0, channel_multiplier=0).then_inc(iotas, 1)
            nc.gpsimd.iota(pidx_i[:, :], [[1, 1]], base=0, channel_multiplier=1).then_inc(iotas, 1)
            nc.gpsimd.iota(spos_i[:, :], [[P, SQ]], base=0, channel_multiplier=1).then_inc(iotas, 1)
            pool.wait_ge(groups_known, 1)
            for q in range(SQ):
                for t, arr in ((dst_s, a["dst"]), (src_s, a["src"])):
                    nc.gpsimd.indirect_dma_start(
                        out=t[:, q * GROUP:(q + 1) * GROUP], out_offset=None, in_=arr[:, :],
                        in_offset=bass.IndirectOffsetOnAxis(ap=grp_i[:, q:q + 1], axis=0)).then_inc(edges_in[q], 16)

        @block.sync
        def _(sp):
            with nc.allow_non_contiguous_dma(reason="the last destination of each group"):
                sp.dma_start(last_i[:, :], a["dst"][0:NG - 1, GROUP - 1:GROUP].rearrange("g one -> one g")).then_inc(last_in, 16)
            sp.dma_start(dflat[:, :], a["dst"].rearrange("g e -> (g e)").rearrange("(p c) -> p c", p=P)).then_inc(dflat_in, 16)
            sp.dma_start(g["x"][:, :, :], a["x"].rearrange("(b p) d -> p b d", p=P)).then_inc(x_in, 16)
            sp.wait_ge(zeros_ready, 1)
            for e in range(E):
                sp.dma_start(g["sent"][e * PITCH:(e + 1) * PITCH, :].rearrange("(t p) w -> p t w", p=P),
                             zeros[:, :].unsqueeze(1).broadcast_to([P, PITCH // P, RW])).then_inc(zeroed, 16)
            sp.wait_ge(x_in, 16)
            sp.wait_ge(zeroed, 16 * E)

        @block.vector
        def _(dve):
            v = nc.vector
            ch = Chain(dve, own)
            v.memset(zeros[:, :], 0.0).then_inc(zeros_ready, 1)
            v.memset(ones_row[:, :], 1.0).then_inc(consts, 1)
            v.memset(g["ones"][:, :], 1.0).then_inc(consts, 1)
            v.memset(zero_b[:, :], 0.0).then_inc(consts, 1)
            ch.link(v.memset(g["eps"][:, :], LN_EPS))
            dve.wait_ge(iotas, 3)
            v.tensor_copy(iota_f[:, :], iota_i[:, :])
            v.tensor_copy(spos[:, :], spos_i[:, :])
            ch.link(v.tensor_copy(pidx[:, :], pidx_i[:, :]))
            v.tensor_copy(g["iota"][:, :], iota_f[:, 0:P])
            v.tensor_copy(iota_b[:, :], iota_f[:, 0:P])
            v.tensor_scalar(g["ident"][:, :], iota_f[:, 0:P], pidx[:, 0:1], None, ALU.is_equal).then_inc(consts, 1)
            v.tensor_scalar(g["upper"][:, :], iota_f[:, 0:P], pidx[:, 0:1], None, ALU.is_ge)
            v.tensor_scalar(limit[:, :], pidx[:, :], float(P), float(P), ALU.mult, ALU.add)
            v.tensor_scalar(far[:, :], pidx[:, :], float(NB - 1), 1.0e6, ALU.is_ge, ALU.mult)
            dve.wait_ge(last_in, 16)
            ch.link(v.tensor_copy(last_f[:, :], last_i[:, :]))
            v.tensor_copy(g["pidx"][:, :], pidx[:, :]).then_inc(last_wide, 1)
            dve.wait_ge(last_wide, 2)
            ch.link(v.tensor_scalar(below[:, :], last_ps[:, :], limit[:, 0:1], None, ALU.is_lt))
            ch.link(v.reduce_sum(nbelow[:, :], below[:, :], AX_X))
            ch.link(v.scalar_tensor_tensor(rank[:, :], nbelow[:, :], pidx[:, 0:1], far[:, :], ALU.add, ALU.add))
            v.tensor_scalar(passed[:, :], iota_f[:, :], rank[:, 0:1], None, ALU.is_gt).then_inc(passed_ready, 1)
            dve.wait_ge(blocks_counted, 1)
            ch.link(v.tensor_copy(blk[:, :], blk_ps[:, :]))
            v.tensor_copy(g["block_of_step"][:, :], row_ps[:, :])
            ch.link(v.tensor_tensor(grp[:, :], spos[:, :], blk[:, :], ALU.subtract))
            v.tensor_scalar(grp_i[:, :], grp[:, :], float(NG), None, ALU.min).then_inc(groups_known, 1)
            ch.link(v.tensor_scalar(blk[:, :], blk[:, :], float(P), None, ALU.mult))
            for q in range(SQ):
                dve.wait_ge(edges_in[q], 32)
                if q:
                    dve.wait_ge(turned, 4 * q)
                ds_ = dst_s[:, q * GROUP:(q + 1) * GROUP]
                d3 = ds_.rearrange("p (t e) -> p t e", t=T)
                w = [work[:, n, :].rearrange("p (t e) -> p t e", t=T) for n in range(4)]
                v.tensor_copy(work[:, 0, :], src_s[:, q * GROUP:(q + 1) * GROUP])
                v.tensor_scalar(work[:, 1, :], ds_, blk[:, q:q + 1], None, ALU.subtract)
                v.memset(w[2][:, :, 0:1], NEG)
                v.memset(w[3][:, :, P - 1:P], 1.0)
                ch.link(v.tensor_tensor(w[3][:, :, 0:P - 1], d3[:, :, 1:P], d3[:, :, 0:P - 1], ALU.not_equal))
                v.tensor_scalar(w[2][:, :, 1:P], w[3][:, :, 0:P - 1], NEG, None, ALU.mult).then_inc(work_ready, 1)
            dve.wait_ge(dflat_in, 16)
            v.tensor_scalar(dlo_i[:, :], dflat[:, :], P - 1, None, ALU.bitwise_and)
            ch.link(v.tensor_scalar(dhi_i[:, :], dflat[:, :], 7, None, ALU.logical_shift_right))
            v.tensor_copy(dlo[:, :], dlo_i[:, :])
            ch.link(v.tensor_copy(dhi[:, :], dhi_i[:, :]))

            def count(i, k):
                dve.wait_ge(onehots_used, i + 1)
                lo = tile_at(dlo, i, HCH).unsqueeze(2).broadcast_to([P, HCH, P])
                hi = tile_at(dhi, i, HCH).unsqueeze(2).broadcast_to([P, HCH, NB])
                v.tensor_tensor(oh_lo[k][:, :, :], iota_b[:, :].unsqueeze(1).broadcast_to([P, HCH, P]), lo, ALU.is_equal)
                v.tensor_tensor(oh_hi[k][:, :, :], iota_b[:, 0:NB].unsqueeze(1).broadcast_to([P, HCH, NB]), hi,
                                ALU.is_equal).then_inc(onehots, 1)

            in_pairs(dve, CHUNKS, count)
            dve.wait_ge(hist_done, 1)
            ch.link(v.tensor_scalar(g["dinv"][:, :], hist_ps[:, :], 1.0, None, ALU.add))
            dve.drain().then_inc(gated, 1)
            dve.wait_ge(gated, 2)
            v.reciprocal(g["dinv"][:, :], g["dinv"][:, :]).then_inc(gated, 1)
            dve.wait_ge(gated, 3)

        @block.scalar
        def _(act):
            for n in range(NTURN):
                q, arr = divmod(n, 4)
                act.wait_ge(turned, n + 1)
                out = g["edges"][arr][:, q * P * T:(q + 1) * P * T].rearrange("e (s t) -> e t s", t=T)
                nc.scalar.copy(out, turn_ps[n % 2][:, :, :]).then_inc(turn_free, 1)
            act.wait_ge(gated, 1)
            nc.scalar.activation(g["dinv"][:, :], g["dinv"][:, :], ACT.Sqrt).then_inc(gated, 1)

        @block.tensor
        def _(pe):
            t = nc.tensor
            pe.wait_ge(last_wide, 1)
            pe.wait_ge(consts, 4)
            t.matmul(last_ps[:, :], ones_row[:, :], last_f[:, :], start=True, stop=True).then_inc(last_wide, 1)
            pe.wait_ge(passed_ready, 1)
            for q in range(SQ):
                t.matmul(blk_ps[:, q:q + 1], passed[:, q * P:(q + 1) * P], g["ones"][:, 0:1], start=True, stop=True)
            t.matmul(row_ps[:, :], g["ones"][:, 0:1], passed[:, :], start=True, stop=True).then_inc(blocks_counted, 1)
            for n in range(NTURN):
                q, arr = divmod(n, 4)
                pe.wait_ge(work_ready, q + 1)
                if n >= 2:
                    pe.wait_ge(turn_free, n - 1)
                for tt in range(T):
                    ins = t.transpose(turn_ps[n % 2][:, tt, :], work[:, arr, tt * P:(tt + 1) * P], g["ident"][:, :])
                ins.then_inc(turned, 1)
            pe.sem_inc(onehots_used, 2)
            t.matmul(hist_ps[:, :], zero_b[:, :], zero_b[:, 0:NB], start=True, stop=False)

            def count(i, k):
                pe.wait_ge(onehots, i + 1)
                for j in range(HCH):
                    ins = t.matmul(hist_ps[:, :], oh_lo[k][:, j, :], oh_hi[k][:, j, :], start=False, stop=False)
                ins.then_inc(onehots_used, 1)

            in_pairs(pe, CHUNKS, count)
            t.matmul(hist_ps[:, :], zero_b[:, :], zero_b[:, 0:NB], start=False, stop=True).then_inc(hist_done, 1)


def gcn_table_phase(nc, a, g):
    with ExitStack() as ctx:
        sb, ps, sem = memory(nc, ctx, "gcn_table")

        stats = sb("stats", [P, NB * 6])
        mean = sb("mean", [P, NB])
        var = sb("var", [P, NB])
        half = sb("half", [P, NB])
        w_in = sb("w_in", [P, KC, D])
        w_t = sb("w_t", [P, KC, D])
        xn = [sb(f"xn{k}", [P, D]) for k in range(2)]
        xn_t = [sb(f"xn_t{k}", [P, KC, P]) for k in range(2)]
        xt_ps = [ps(f"xt_ps{k}", D).rearrange("p (c n) -> p c n", c=KC) for k in range(2)]
        row_ps = [ps(f"row_ps{k}", D) for k in range(2)]
        w_ps = ps("w_ps", KC * D).rearrange("p (c n) -> p c n", c=KC)

        own = sem("own")
        w_loaded = sem("w_loaded")
        w_turned = sem("w_turned")
        w_ready = sem("w_ready")
        var_ready = sem("var_ready")
        root_ready = sem("root_ready")
        xn_ready = sem("xn_ready")
        xn_turned = sem("xn_turned")
        xn_t_ready = sem("xn_t_ready")
        rows_ready = sem("rows_ready")
        rows_scaled = sem("rows_scaled")
        rows_out = sem("rows_out")
        block = ctx.enter_context(nc.Block())

        @block.sync
        def _(sp):
            sp.dma_start(w_in[:, :, :], a["L0_gnn_W"].rearrange("(o p) k -> p o k", p=P)).then_inc(w_loaded, 16)
            with sp.Fori(0, NB) as i:
                sp.wait_ge(rows_scaled, i + 1)
                sp.dma_start(g["table0"][bass.ds(i * P, P), :], tile_at(g["acc"], i, D)).then_inc(rows_out, 16)
            sp.wait_ge(rows_out, 16 * NB)

        @block.vector
        def _(dve):
            v = nc.vector
            ch = Chain(dve, own)
            emit_stats(nc, dve, ch, g["xf"], D, stats, mean, var, half, var_ready)
            dve.wait_ge(root_ready, 1)
            ch.link(v.reciprocal(var[:, :], var[:, :]))
            dve.sem_inc(xn_turned, 2)
            dve.sem_inc(rows_ready, 2)

            def norm(i, k):
                dve.wait_ge(xn_turned, i + 1)
                v.tensor_scalar(xn[k][:, :], tile_at(g["xf"], i, D), mean[:, bass.ds(i, 1)], var[:, bass.ds(i, 1)],
                                ALU.subtract, ALU.mult).then_inc(xn_ready, 1)

            def scale(i, k):
                dve.wait_ge(rows_ready, i + 3)
                v.tensor_scalar(tile_at(g["acc"], i, D), row_ps[k][:, :], g["dinv"][:, bass.ds(i, 1)], None,
                                ALU.mult).then_inc(rows_scaled, 1)

            norm(0, 0)
            norm(1, 1)
            with dve.Fori(0, NB // 2 - 1) as j:
                norm(j * 2 + 2, 0)
                scale(j * 2, 0)
                norm(j * 2 + 3, 1)
                scale(j * 2 + 1, 1)
            norm(NB - 1, 0)
            scale(NB - 3, 0)
            scale(NB - 2, 1)
            scale(NB - 1, 0)

        @block.scalar
        def _(act):
            act.wait_ge(w_turned, 1)
            nc.scalar.copy(w_t[:, :, :], w_ps[:, :, :]).then_inc(w_ready, 1)
            act.wait_ge(var_ready, 1)
            nc.scalar.activation(var[:, :], var[:, :], ACT.Sqrt, bias=g["eps"][:, 0:1]).then_inc(root_ready, 1)

            def move(i, k):
                act.wait_ge(xn_turned, i + 3)
                act.wait_ge(rows_ready, i + 1)
                nc.scalar.copy(xn_t[k][:, :, :], xt_ps[k][:, :, :]).then_inc(xn_t_ready, 1)

            in_pairs(act, NB, move)

        @block.tensor
        def _(pe):
            t = nc.tensor
            pe.wait_ge(w_loaded, 16)
            for kc in range(KC):
                for o in range(KC):
                    ins = t.transpose(w_ps[:, kc, o * P:(o + 1) * P], w_in[:, o, kc * P:(kc + 1) * P], g["ident"][:, :])
            ins.then_inc(w_turned, 1)
            pe.wait_ge(w_ready, 1)

            def turn(i, k):
                pe.wait_ge(xn_ready, i + 1)
                for kc in range(KC):
                    ins = t.transpose(xt_ps[k][:, kc, :], xn[k][:, kc * P:(kc + 1) * P], g["ident"][:, :])
                ins.then_inc(xn_turned, 1)

            def rows(i, k, first=False):
                pe.wait_ge(xn_t_ready, i + 1)
                if not first:
                    pe.wait_ge(rows_scaled, i - 1)
                for kc in range(KC):
                    ins = t.matmul(row_ps[k][:, :], xn_t[k][:, kc, :], w_t[:, kc, :], start=(kc == 0), stop=(kc == KC - 1))
                ins.then_inc(rows_ready, 1)

            turn(0, 0)
            turn(1, 1)
            rows(0, 0, True)
            turn(2, 0)
            rows(1, 1, True)
            with pe.Fori(1, NB // 2) as j:
                turn(j * 2 + 1, 1)
                rows(j * 2, 0)
                turn(j * 2 + 2, 0)
                rows(j * 2 + 1, 1)
            rows(NB - 1, 0)


def emit_stats(nc, dve, ch, xf, pitch, stats, mean, var, half, var_ready):
    v = nc.vector
    with dve.Fori(0, NB) as i:
        v.bn_stats(stats[:, bass.ds(i * 6, 6)], xf[:, bass.ds(i * pitch, D)])
    st = stats[:, :].rearrange("p (b s) -> p b s", s=6)
    dve.drain()
    ch.link(v.tensor_tensor(mean[:, :], st[:, :, 1], st[:, :, 4], ALU.add))
    ch.link(v.tensor_tensor(half[:, :], st[:, :, 1], st[:, :, 4], ALU.subtract))
    ch.link(v.tensor_tensor(var[:, :], st[:, :, 2], st[:, :, 5], ALU.add))
    ch.link(v.tensor_scalar(mean[:, :], mean[:, :], 0.5, None, ALU.mult))
    ch.link(v.scalar_tensor_tensor(half[:, :], half[:, :], 0.25, half[:, :], ALU.mult, ALU.mult))
    v.scalar_tensor_tensor(var[:, :], var[:, :], 1.0 / D, half[:, :], ALU.mult, ALU.add).then_inc(var_ready, 1)


def gcn_steps_phase(nc, a, g):
    with ExitStack() as ctx:
        sb, ps, sem = memory(nc, ctx, "gcn_steps")

        R = 4
        TRIPS = STEPS4 // R
        index = [sb(f"index{k}", [P, R * T], I32) for k in range(2)]
        rows = [sb(f"rows{k}", [P, T, D]) for k in range(R)]
        onehot = [sb(f"onehot{k}", [P, T, P]) for k in range(2)]
        sum_ps = [ps(f"sum_ps{k}", D) for k in range(2)]

        own = sem("own")
        index_ready = sem("index_ready")
        index_used = sem("index_used")
        rows_in = [sem(f"rows_in{k}") for k in range(R)]
        onehot_ready = sem("onehot_ready")
        sums_ready = sem("sums_ready")
        sums_added = sem("sums_added")
        slots_taken = sem("slots_taken")
        block = ctx.enter_context(nc.Block())

        @block.scalar
        def _(act):
            act.sem_inc(index_used, 2)

            def indices(j, k):
                act.wait_ge(index_used, j + 1)
                nc.scalar.copy(index[k][:, :], tile_at(g["edges"][0], j, R * T)).then_inc(index_ready, 1)

            in_pairs(act, TRIPS, indices)

        @block.gpsimd
        def _(pool):
            pool.sem_inc(sums_ready, R)

            def gather(j, k):
                pool.wait_ge(index_ready, j + 1)
                for r in range(R):
                    pool.wait_ge(sums_ready, j * R + (r + 1))
                    pool.sem_inc(slots_taken, 1)
                    for t in range(T):
                        n = r * T + t
                        ins = nc.gpsimd.indirect_dma_start(
                            out=rows[r][:, t, :], out_offset=None, in_=g["table0"][:, :],
                            in_offset=bass.IndirectOffsetOnAxis(ap=index[k][:, n:n + 1], axis=0)).then_inc(rows_in[r], 16)
                for r in range(R):
                    pool.wait_ge(rows_in[r], (j + 1) * (16 * T))
                pool.sem_inc(index_used, 1)

            in_pairs(pool, TRIPS, gather)

        @block.vector
        def _(dve):
            v = nc.vector

            def onehots(j, r):
                dve.wait_ge(sums_ready, j * R + (r + R - 1))
                for t in range(T):
                    ins = v.tensor_scalar(onehot[r % 2][:, t, :], g["iota"][:, :],
                                          g["edges"][1][:, bass.ds(j * (R * T) + (r * T + t), 1)], None, ALU.is_equal)
                ins.then_inc(onehot_ready, 1)

            def add(j, r):
                b = dve.value_load(g["block_of_step"][0:1, bass.ds(j * R + r, 1)], min_val=0, max_val=NB - 1)
                dve.wait_ge(sums_ready, j * R + (r + 1 + R))
                into = tile_at(g["acc"], b, D)
                v.tensor_tensor(into, sum_ps[r % 2][:, :], into, ALU.add).then_inc(sums_added, 1)
                dve.wait_ge(sums_added, j * R + (r + 1))

            with dve.Fori(0, TRIPS) as j:
                for r in range(R):
                    onehots(j, r)
                    add(j, r)

        @block.tensor
        def _(pe):
            def product(j, r, first=False):
                pe.wait_ge(rows_in[r], (j + 1) * (16 * T))
                pe.wait_ge(onehot_ready, j * R + (r + 1))
                if not first:
                    pe.wait_ge(sums_added, j * R + (r - 1))
                for t in range(T):
                    ins = nc.tensor.matmul(sum_ps[r % 2][:, :], onehot[r % 2][:, t, :], rows[r][:, t, :],
                                           start=(t == 0), stop=(t == T - 1))
                ins.then_inc(sums_ready, 1)

            for r in range(R):
                product(0, r, first=(r < 2))
            with pe.Fori(1, TRIPS) as j:
                for r in range(R):
                    product(j, r)


def moe_phase(nc, a, g):
    with ExitStack() as ctx:
        sb, ps, sem = memory(nc, ctx, "moe")

        w1 = sb("w1", [P, E, KC, D])
        w2 = sb("w2", [P, E, KC, D])
        b1_in = sb("b1_in", [E * KC, P])
        b1 = sb("b1", [P, E * KC])
        b2 = sb("b2", [E, D])
        router_in = sb("router_in", [E, D])
        router = sb("router", [P, KC, E])
        bias = sb("bias", [P, D])
        gamma = sb("gamma", [P, D])
        beta = sb("beta", [P, D])
        node = sb("node", [P, D])
        stats = sb("stats", [P, 2, 6])
        mv = sb("mv", [P, 2, 2])
        ve = sb("ve", [P, 2])
        rstd = sb("rstd", [P, 2])
        minus_half = sb("minus_half", [P, 1])
        xn = sb("xn", [P, D])
        xn_t = [sb(f"xn_t{k}", [P, KC, P]) for k in range(2)]
        down = sb("down", [P, E])
        lg = sb("lg", [P, E])
        ex = sb("ex", [P, E])
        pr = sb("pr", [P, E])
        first = sb("first", [P, E])
        second = sb("second", [P, E])
        rest = sb("rest", [P, E])
        eq = sb("eq", [P, E])
        s1 = sb("s1", [P, 8])
        comb = [sb(f"comb{k}", [P, E]) for k in range(2)]
        comb_t = sb("comb_t", [E, P])
        hid = [sb(f"hid{k}", [P, KC, P]) for k in range(2)]

        xt_ps = ps("xt_ps", D).rearrange("p (c n) -> p c n", c=KC)
        logit_ps = ps("logit_ps", E)
        combt_ps = ps("combt_ps", P)
        b2_ps = ps("b2_ps", D)
        hid_ps = [ps(f"hid_ps{k}", D).rearrange("p (c n) -> p c n", c=KC) for k in range(2)]
        y_ps = [ps(f"y_ps{k}", D) for k in range(2)]

        own = sem("own")
        loaded = sem("loaded")
        const_ready = sem("const_ready")
        turned_w = sem("turned_w")
        weights_ready = sem("weights_ready")
        var_ready = sem("var_ready")
        rstd_ready = sem("rstd_ready")
        xn_ready = sem("xn_ready")
        xn_turned = sem("xn_turned")
        xn_t_ready = sem("xn_t_ready")
        logits_ready = sem("logits_ready")
        lg_ready = sem("lg_ready")
        exp_ready = sem("exp_ready")
        comb_ready = sem("comb_ready")
        comb_turned = sem("comb_turned")
        comb_t_ready = sem("comb_t_ready")
        b2_ready = sem("b2_ready")
        hid_ready = sem("hid_ready")
        gelu_ready = sem("gelu_ready")
        y_ready = sem("y_ready")
        y_added = sem("y_added")
        block = ctx.enter_context(nc.Block())
        NLOAD = 8

        @block.sync
        def _(sp):
            with nc.allow_non_contiguous_dma(reason="rows broadcast"):
                for t, src in ((b1_in[:, :], a["L0_ffn_b1"].rearrange("e (c p) -> (e c) p", p=P)),
                               (router_in[:, :], a["L0_ffn_router_w"]),
                               (bias[:, :], a["L0_gnn_b"].partition_broadcast(P)),
                               (gamma[:, :], a["L0_gnn_gamma"].partition_broadcast(P)),
                               (beta[:, :], a["L0_gnn_beta"].partition_broadcast(P)),
                               (b2[:, :], a["L0_ffn_b2"]),
                               (w1[:, :, :, :], a["L0_ffn_w1"].rearrange("e (c p) f -> p e c f", p=P)),
                               (w2[:, :, :, :], a["L0_ffn_w2"].rearrange("e (c p) f -> p e c f", p=P))):
                    sp.dma_start(t, src).then_inc(loaded, 16)
            sp.wait_ge(loaded, 16 * NLOAD)

        @block.gpsimd
        def _(pool):
            pool.wait_ge(const_ready, 1)

            def roots(i):
                for c in range(2):
                    pool.wait_ge(var_ready, i * 2 + (c + 1))
                    nc.gpsimd.tensor_tensor(rstd[:, c:c + 1], ve[:, c:c + 1], minus_half[:, :], ALU.pow).then_inc(rstd_ready, 1)

            with pool.Fori(0, NB) as i:
                roots(i)

        @block.vector
        def _(dve):
            v = nc.vector
            ch = Chain(dve, own)
            v.tensor_scalar(down[:, :], g["iota"][:, 0:E], -1.0, float(E), ALU.mult, ALU.add)
            v.memset(minus_half[:, :], -0.5).then_inc(const_ready, 1)
            dve.wait_ge(loaded, 16 * NLOAD)

            def norm_stats(c, i, src):
                v.bn_stats(stats[:, c, :], src)
                dve.drain()
                ch.link(v.bn_aggr(mv[:, c, :], stats[:, c, :]))
                v.tensor_scalar(ve[:, c:c + 1], mv[:, c, 1:2], LN_EPS, None, ALU.add).then_inc(var_ready, 1)

            def pieces(i, k):
                xb = tile_at(g["xf"], i, D)

                def p0():
                    ch.link(v.scalar_tensor_tensor(node[:, :], tile_at(g["acc"], i, D), g["dinv"][:, bass.ds(i, 1)],
                                                   bias[:, :], ALU.mult, ALU.add))
                    norm_stats(0, i, node[:, :])

                def p1():
                    dve.wait_ge(rstd_ready, i * 2 + 1)
                    ch.link(v.tensor_scalar(node[:, :], node[:, :], mv[:, 0, 0:1], rstd[:, 0:1], ALU.subtract, ALU.mult))
                    ch.link(v.tensor_tensor(node[:, :], node[:, :], gamma[:, :], ALU.mult))

                def p2():
                    ch.link(v.tensor_tensor(node[:, :], node[:, :], beta[:, :], ALU.add))

                def p3():
                    ch.link(v.scalar_tensor_tensor(node[:, :], node[:, :], 0.0, xb, ALU.max, ALU.add))
                    norm_stats(1, i, node[:, :])

                def p4():
                    dve.wait_ge(rstd_ready, i * 2 + 2)
                    v.tensor_scalar(xn[:, :], node[:, :], mv[:, 1, 0:1], rstd[:, 1:2], ALU.subtract,
                                    ALU.mult).then_inc(xn_ready, 1)
                    dve.wait_ge(xn_ready, i + 1)
                    ch.link(v.tensor_tensor(xb, node[:, :], xn[:, :], ALU.add))

                def p5():
                    dve.wait_ge(logits_ready, i + 1)
                    ch.link(v.reduce_max(s1[:, 0:1], logit_ps[:, :], AX_X))
                    v.tensor_scalar(lg[:, :], logit_ps[:, :], s1[:, 0:1], None, ALU.subtract).then_inc(lg_ready, 1)

                def p6():
                    dve.wait_ge(exp_ready, i + 1)
                    ch.link(v.reduce_sum(s1[:, 1:2], ex[:, :], AX_X))
                    ch.link(v.reciprocal(s1[:, 2:3], s1[:, 1:2]))
                    ch.link(v.tensor_scalar(pr[:, :], ex[:, :], s1[:, 2:3], None, ALU.mult))
                    ch.link(v.reduce_max(s1[:, 3:4], pr[:, :], AX_X))
                    ch.link(v.scalar_tensor_tensor(eq[:, :], pr[:, :], s1[:, 3:4], down[:, :], ALU.is_equal, ALU.mult))
                    ch.link(v.reduce_max(s1[:, 5:6], eq[:, :], AX_X))
                    ch.link(v.tensor_scalar(first[:, :], eq[:, :], s1[:, 5:6], None, ALU.is_equal))
                    ch.link(v.scalar_tensor_tensor(rest[:, :], first[:, :], -2.0, pr[:, :], ALU.mult, ALU.add))

                def p7():
                    ch.link(v.reduce_max(s1[:, 4:5], rest[:, :], AX_X))
                    ch.link(v.scalar_tensor_tensor(eq[:, :], rest[:, :], s1[:, 4:5], down[:, :], ALU.is_equal, ALU.mult))
                    ch.link(v.reduce_max(s1[:, 5:6], eq[:, :], AX_X))
                    v.tensor_scalar(second[:, :], eq[:, :], s1[:, 5:6], s1[:, 4:5], ALU.is_equal, ALU.mult)
                    ch.link(v.tensor_tensor(s1[:, 6:7], s1[:, 3:4], s1[:, 4:5], ALU.add))
                    ch.link(v.tensor_scalar(s1[:, 6:7], s1[:, 6:7], 1e-12, None, ALU.max))
                    ch.link(v.reciprocal(s1[:, 7:8], s1[:, 6:7]))
                    ch.link(v.scalar_tensor_tensor(first[:, :], first[:, :], s1[:, 3:4], second[:, :], ALU.mult, ALU.add))
                    v.tensor_scalar(comb[k][:, :], first[:, :], s1[:, 7:8], None, ALU.mult).then_inc(comb_ready, 1)
                    dve.wait_ge(comb_ready, i + 1)

                return [p0, p1, p2, p3, p4, p5, p6, p7]

            def block_of(i, k, ahead):
                xb = tile_at(g["xf"], i, D)
                dve.wait_ge(b2_ready, i + 1)
                ch.link(v.tensor_tensor(xb, b2_ps[:, :], xb, ALU.add))
                for e in range(E):
                    if ahead:
                        ahead[e]()
                    dve.wait_ge(y_ready, i * E + (e + 1))
                    ins = v.scalar_tensor_tensor(xb, y_ps[e % 2][:, :], comb[k][:, e:e + 1], xb, ALU.mult, ALU.add)
                    ins.then_inc(y_added, 1)
                    dve.wait_ge(y_added, i * E + (e + 1))

            PREP, ADD = 24, 1
            ch.begin()
            for p in pieces(0, 0):
                p()
            ch.end()
            with dve.Fori(0, (NB - 1) // 2) as j:
                ch.begin(j, 2 * (PREP + ADD))
                block_of(j * 2, 0, pieces(j * 2 + 1, 1))
                block_of(j * 2 + 1, 1, pieces(j * 2 + 2, 0))
            ch.end((NB - 1) // 2)
            block_of(NB - 1, 0, None)

        @block.scalar
        def _(act):
            s = nc.scalar
            act.wait_ge(turned_w, 1)
            s.copy(b1[:, :], xt_ps[:, 0, 0:E * KC])
            s.copy(router[:, :, :], xt_ps[:, 1, 0:KC * E].rearrange("p (c e) -> p c e", c=KC)).then_inc(weights_ready, 1)
            act.wait_ge(weights_ready, 1)

            def turned(i, k):
                act.wait_ge(xn_turned, i + 1)
                s.copy(xn_t[k][:, :, :], xt_ps[:, :, :]).then_inc(xn_t_ready, 1)

            def exps(i):
                act.wait_ge(lg_ready, i + 1)
                s.activation(ex[:, :], lg[:, :], ACT.Exp).then_inc(exp_ready, 1)

            def comb_copy(i):
                act.wait_ge(comb_turned, i + 1)
                s.copy(comb_t[:, :], combt_ps[0:E, :]).then_inc(comb_t_ready, 1)

            def gelu(i, e):
                act.wait_ge(hid_ready, i * E + (e + 1))
                for c in range(KC):
                    n = e * KC + c
                    ins = s.activation(hid[e % 2][:, c, :], hid_ps[e % 2][:, c, :], ACT.Gelu, bias=b1[:, n:n + 1])
                ins.then_inc(gelu_ready, 1)

            def block_of(i, k, more):
                for e in range(E):
                    gelu(i, e)
                    if more and e == 5:
                        turned(i + 1, 1 - k)
                if more:
                    exps(i + 1)
                    comb_copy(i + 1)

            turned(0, 0)
            exps(0)
            comb_copy(0)
            with act.Fori(0, (NB - 1) // 2) as j:
                block_of(j * 2, 0, True)
                block_of(j * 2 + 1, 1, True)
            block_of(NB - 1, 0, False)

        @block.tensor
        def _(pe):
            t = nc.tensor
            pe.wait_ge(loaded, 16 * NLOAD)
            t.transpose(xt_ps[:, 0, 0:E * KC], b1_in[:, :], g["ident"][0:E * KC, 0:E * KC])
            for c in range(KC):
                ins = t.transpose(xt_ps[:, 1, c * E:(c + 1) * E], router_in[:, c * P:(c + 1) * P], g["ident"][0:E, 0:E])
            ins.then_inc(turned_w, 1)
            pe.wait_ge(weights_ready, 1)

            def turn(i, k):
                pe.wait_ge(xn_ready, i + 1)
                for c in range(KC):
                    ins = t.transpose(xt_ps[:, c, :], xn[:, c * P:(c + 1) * P], g["ident"][:, :])
                ins.then_inc(xn_turned, 1)

            def logits(i, k):
                pe.wait_ge(xn_t_ready, i + 1)
                for c in range(KC):
                    ins = t.matmul(logit_ps[:, :], xn_t[k][:, c, :], router[:, c, :], start=(c == 0), stop=(c == KC - 1))
                ins.then_inc(logits_ready, 1)

            def comb_turn(i, k):
                pe.wait_ge(comb_ready, i + 1)
                t.transpose(combt_ps[0:E, :], comb[k][:, :], g["ident"][:, :]).then_inc(comb_turned, 1)
                pe.wait_ge(comb_t_ready, i + 1)
                t.matmul(b2_ps[:, :], comb_t[:, :], b2[:, :], start=True, stop=True).then_inc(b2_ready, 1)

            def up(i, k, e):
                for f in range(KC):
                    for c in range(KC):
                        ins = t.matmul(hid_ps[e % 2][:, f, :], w1[:, e, c, f * P:(f + 1) * P], xn_t[k][:, c, :],
                                       start=(c == 0), stop=(c == KC - 1))
                ins.then_inc(hid_ready, 1)

            def down_(i, e, wait):
                pe.wait_ge(gelu_ready, i * E + (e + 1))
                if wait:
                    pe.wait_ge(y_added, i * E + (e - 1))
                for f in range(KC):
                    ins = t.matmul(y_ps[e % 2][:, :], hid[e % 2][:, f, :], w2[:, e, f, :], start=(f == 0), stop=(f == KC - 1))
                ins.then_inc(y_ready, 1)

            def block_of(i, k, more, start=False):
                for e in range(E + 1):
                    if e < E:
                        up(i, k, e)
                    if e > 0:
                        down_(i, e - 1, not (start and e - 1 < 2))
                    if more and e == 5:
                        turn(i + 1, 1 - k)
                    if more and e == 6:
                        logits(i + 1, 1 - k)
                if more:
                    comb_turn(i + 1, 1 - k)

            turn(0, 0)
            logits(0, 0)
            comb_turn(0, 0)
            block_of(0, 0, True, True)
            block_of(1, 1, True)
            with pe.Fori(1, (NB - 1) // 2) as j:
                block_of(j * 2, 0, True)
                block_of(j * 2 + 1, 1, True)
            block_of(NB - 1, 0, False)


def gat_table_phase(nc, a, g):
    with ExitStack() as ctx:
        sb, ps, sem = memory(nc, ctx, "gat_table")
        NA = RW + H
        stats = sb("stats", [P, NB * 6])
        mean = sb("mean", [P, NB])
        var = sb("var", [P, NB])
        half = sb("half", [P, NB])
        w_in = sb("w_in", [P, KC, D])
        w_res = sb("w_res", [P, KC, D])
        w_aug = sb("w_aug", [P, KC, NA])
        a_src = sb("a_src", [P, D])
        a_dst = sb("a_dst", [P, D])
        prod = sb("prod", [P, KC, D])
        bias = sb("bias", [P, D])
        bias2 = sb("bias2", [P, D])
        xn = [sb(f"xn{k}", [P, D]) for k in range(2)]
        xn_t = [sb(f"xn_t{k}", [P, KC, P]) for k in range(2)]
        row = [sb(f"row{k}", [P, RW]) for k in range(2)]
        res = [sb(f"res{k}", [P, D]) for k in range(2)]
        xt_ps = [ps(f"xt_ps{k}", D).rearrange("p (c n) -> p c n", c=KC) for k in range(2)]
        row_ps = [ps(f"row_ps{k}", NA) for k in range(2)]
        res_ps = [ps(f"res_ps{k}", D) for k in range(2)]

        own = sem("own")
        loaded = sem("loaded")
        weights_ready = sem("weights_ready")
        var_ready = sem("var_ready")
        root_ready = sem("root_ready")
        xn_ready = sem("xn_ready")
        xn_turned = sem("xn_turned")
        xn_t_ready = sem("xn_t_ready")
        products_ready = sem("products_ready")
        rows_ready = sem("rows_ready")
        res_ready = sem("res_ready")
        rows_out = [sem(f"rows_out{k}") for k in range(2)]
        NLOAD = 6
        block = ctx.enter_context(nc.Block())

        @block.sync
        def _(sp):
            for t, src in ((w_in[:, :, :], a["L1_gnn_W"].rearrange("(c p) o -> p c o", p=P)),
                           (w_res[:, :, :], a["L1_gnn_W_res"].rearrange("(c p) o -> p c o", p=P)),
                           (a_src[:, :], a["L1_gnn_a_src"].rearrange("h c -> (h c)").partition_broadcast(P)),
                           (a_dst[:, :], a["L1_gnn_a_dst"].rearrange("h c -> (h c)").partition_broadcast(P)),
                           (bias[:, :], a["L1_gnn_bias_gat"].partition_broadcast(P)),
                           (bias2[:, :], a["L1_gnn_b_res"].partition_broadcast(P))):
                sp.dma_start(t, src).then_inc(loaded, 16)

            def store(i, k):
                sp.wait_ge(rows_ready, i + 1)
                sp.dma_start(g["table1"][bass.ds(i * P, P), :], row[k][:, :]).then_inc(rows_out[k], 16)
                sp.wait_ge(res_ready, i + 1)
                sp.dma_start(g["residual"][bass.ds(i * P, P), :], res[k][:, :]).then_inc(rows_out[k], 16)

            in_pairs(sp, NB, store)
            sp.wait_ge(rows_out[0], 32 * ((NB + 1) // 2))
            sp.wait_ge(rows_out[1], 32 * (NB // 2))

        @block.vector
        def _(dve):
            v = nc.vector
            ch = Chain(dve, own)
            dve.wait_ge(loaded, 16 * NLOAD)
            heads = w_aug[:, :, 0:RW].rearrange("p c (h n) -> p c h n", n=HW_)
            for c in range(KC):
                v.tensor_copy(heads[:, c, :, 0:C], w_in[:, c, :].rearrange("p (h n) -> p h n", h=H))
                v.tensor_tensor(prod[:, c, :], w_in[:, c, :], a_src[:, :], ALU.mult)
            dve.drain()
            for c in range(KC):
                v.reduce_sum(heads[:, c, :, C:HW_], prod[:, c, :].rearrange("p (h n) -> p h n", h=H), AX_X)
            dve.drain()
            for c in range(KC):
                v.tensor_tensor(prod[:, c, :], w_in[:, c, :], a_dst[:, :], ALU.mult)
            v.tensor_tensor(bias[:, :], bias[:, :], bias2[:, :], ALU.add)
            dve.drain()
            for c in range(KC):
                ins = v.reduce_sum(w_aug[:, c, RW:NA], prod[:, c, :].rearrange("p (h n) -> p h n", h=H), AX_X)
            ins.then_inc(weights_ready, 1)
            emit_stats(nc, dve, ch, g["xf"], D, stats, mean, var, half, var_ready)
            dve.wait_ge(root_ready, 1)
            ch.link(v.reciprocal(var[:, :], var[:, :]))
            dve.sem_inc(xn_turned, 2)

            def norm(i, k):
                dve.wait_ge(xn_turned, i + 1)
                v.tensor_scalar(xn[k][:, :], tile_at(g["xf"], i, D), mean[:, bass.ds(i, 1)], var[:, bass.ds(i, 1)],
                                ALU.subtract, ALU.mult).then_inc(xn_ready, 1)

            def finish(i, k, first=False):
                dve.wait_ge(products_ready, i + 1)
                if not first:
                    dve.wait_ge(rows_out[k], (i - k) * 16)
                v.tensor_tensor(res[k][:, :], res_ps[k][:, :], bias[:, :], ALU.add).then_inc(res_ready, 1)

            norm(0, 0)
            norm(1, 1)
            norm(2, 0)
            finish(0, 0, True)
            norm(3, 1)
            finish(1, 1, True)
            with dve.Fori(1, NB // 2 - 1) as j:
                norm(j * 2 + 2, 0)
                finish(j * 2, 0)
                norm(j * 2 + 3, 1)
                finish(j * 2 + 1, 1)
            norm(NB - 1, 0)
            finish(NB - 3, 0)
            finish(NB - 2, 1)
            finish(NB - 1, 0)
            v.memset(g["acc"][:, :].rearrange("p (n w) -> p n w", w=HW_)[:, :, C:HW_], 1.0)
            dve.wait_ge(rows_ready, NB)
            state = g["state"][:, :].rearrange("p (b two h) -> p b two h", two=2, h=H)
            top, dst = state[:, :, 1, :], state[:, :, 0, :]
            ch.link(v.tensor_tensor(top, top, dst, ALU.add))
            ch.link(v.scalar_tensor_tensor(top, top, 0.2, top, ALU.mult, ALU.max))

        @block.scalar
        def _(act):
            s = nc.scalar
            act.wait_ge(var_ready, 1)
            s.activation(var[:, :], var[:, :], ACT.Sqrt, bias=g["eps"][:, 0:1]).then_inc(root_ready, 1)

            def move(i, k):
                act.wait_ge(xn_turned, i + 3)
                s.copy(xn_t[k][:, :, :], xt_ps[k][:, :, :]).then_inc(xn_t_ready, 1)

            def rows(i, k, first=False):
                act.wait_ge(products_ready, i + 1)
                if not first:
                    act.wait_ge(rows_out[k], (i - k) * 16)
                heads = row_ps[k][:, 0:RW].rearrange("p (h n) -> p h n", n=HW_)
                s.copy(tile_at(g["acc"], i, RW).rearrange("p (h n) -> p h n", n=HW_)[:, :, 0:C], heads[:, :, 0:C])
                st = tile_at(g["state"], i, 2 * H)
                s.copy(st[:, 0:H], row_ps[k][:, RW:NA])
                s.copy(st[:, H:2 * H].unsqueeze(2), heads[:, :, C:HW_])
                s.copy(row[k][:, :], row_ps[k][:, 0:RW]).then_inc(rows_ready, 1)

            move(0, 0)
            move(1, 1)
            rows(0, 0, True)
            move(2, 0)
            rows(1, 1, True)
            with act.Fori(1, NB // 2) as j:
                move(j * 2 + 1, 1)
                rows(j * 2, 0)
                move(j * 2 + 2, 0)
                rows(j * 2 + 1, 1)
            rows(NB - 1, 0)

        @block.tensor
        def _(pe):
            t = nc.tensor
            pe.wait_ge(weights_ready, 1)

            def turn(i, k):
                pe.wait_ge(xn_ready, i + 1)
                for c in range(KC):
                    ins = t.transpose(xt_ps[k][:, c, :], xn[k][:, c * P:(c + 1) * P], g["ident"][:, :])
                ins.then_inc(xn_turned, 1)

            def rows(i, k, first=False):
                pe.wait_ge(xn_t_ready, i + 1)
                if not first:
                    pe.wait_ge(rows_ready, i - 1)
                    pe.wait_ge(res_ready, i - 1)
                for c in range(KC):
                    t.matmul(row_ps[k][:, :], xn_t[k][:, c, :], w_aug[:, c, :], start=(c == 0), stop=(c == KC - 1))
                for c in range(KC):
                    ins = t.matmul(res_ps[k][:, :], xn_t[k][:, c, :], w_res[:, c, :], start=(c == 0), stop=(c == KC - 1))
                ins.then_inc(products_ready, 1)

            turn(0, 0)
            turn(1, 1)
            rows(0, 0, True)
            turn(2, 0)
            rows(1, 1, True)
            with pe.Fori(1, NB // 2) as j:
                turn(j * 2 + 1, 1)
                rows(j * 2, 0)
                turn(j * 2 + 2, 0)
                rows(j * 2 + 1, 1)
            rows(NB - 1, 0)


def gat_steps_phase(nc, a, g):
    with ExitStack() as ctx:
        sb, ps, sem = memory(nc, ctx, "gat_steps")
        R = 4
        TRIPS = STEPS4 // R
        TH = T * H
        index = [sb(f"index{k}", [P, R * T], I32) for k in range(2)]
        rows = [sb(f"rows{k}", [P, T, RW]) for k in range(R)]
        onehot = [sb(f"onehot{k}", [P, T, P]) for k in range(R)]
        onehot_t = [sb(f"onehot_t{k}", [P, T, P]) for k in range(2)]
        score_t = sb("score_t", [TH, P])
        run_max = sb("run_max", [TH, P])
        begin = sb("begin", [P, T, H])
        cand = sb("cand", [P, T, H + 1])
        absent = sb("absent", [P, T])
        cand_m = sb("cand_m", [P, T, H])
        top = sb("top", [P, H])
        top2 = sb("top2", [P, H])
        dst_max = [sb(f"dst_max{k}", [P, 2 * H]) for k in range(2)]
        drop = [sb(f"drop{k}", [P, H]) for k in range(2)]
        fade = [sb(f"fade{k}", [P, H]) for k in range(R)]
        z = sb("z", [P, T, H])
        z2 = sb("z2", [P, T, H])
        arg = [sb(f"arg{k}", [P, T, H]) for k in range(2)]

        turn_ps = ps("turn_ps", 2 * P)
        onehot_ps = ps("onehot_ps", T * P).rearrange("p (t e) -> p t e", t=T)
        back_ps = ps("back_ps", TH).rearrange("p (t h) -> p t h", t=T)
        cand_ps = ps("cand_ps", T * (H + 1)).rearrange("p (t h) -> p t h", t=T)
        edge_ps = ps("edge_ps", T * 2 * H).rearrange("p (t h) -> p t h", t=T)
        weight_ps = ps("weight_ps", TH).rearrange("p (t h) -> p t h", t=T)
        sum_ps = [ps(f"sum_ps{k}", RW) for k in range(2)]

        own = sem("own")
        index_ready = sem("index_ready")
        slots_taken = sem("slots_taken")
        slots_free = sem("slots_free")
        rows_in = [sem(f"rows_in{k}") for k in range(R)]
        onehot_ready = sem("onehot_ready")
        begin_ready = sem("begin_ready")
        scores_turned = sem("scores_turned")
        score_t_ready = sem("score_t_ready")
        onehot_turned = sem("onehot_turned")
        onehot_t_ready = sem("onehot_t_ready")
        scanned = sem("scanned")
        back_ready = sem("back_ready")
        cand_ready = sem("cand_ready")
        cand_spread = sem("cand_spread")
        dst_max_ready = sem("dst_max_ready")
        drop_ready = sem("drop_ready")
        fade_ready = sem("fade_ready")
        edge_ready = sem("edge_ready")
        arg_ready = sem("arg_ready")
        weights_ready = sem("weights_ready")
        rows_weighed = sem("rows_weighed")
        sums_added = sem("sums_added")
        sums_faded = sem("sums_faded")
        block = ctx.enter_context(nc.Block())

        def headed(ap):
            return ap.rearrange("p t (h n) -> p (t h) n", n=HW_)

        @block.gpsimd
        def _(pool):
            pool.sem_inc(slots_free, R)

            def gather(j, k):
                pool.wait_ge(index_ready, j + 1)
                for r in range(R):
                    pool.wait_ge(slots_free, j * R + (r + 1))
                    pool.sem_inc(slots_taken, 1)
                    for t in range(T):
                        n = r * T + t
                        nc.gpsimd.indirect_dma_start(
                            out=rows[r][:, t, :], out_offset=None, in_=g["table1"][:, :],
                            in_offset=bass.IndirectOffsetOnAxis(ap=index[k][:, n:n + 1], axis=0)).then_inc(rows_in[r], 16)

            in_pairs(pool, TRIPS, gather)

        def run(eng, step):
            for r in range(R):
                step(0, r, r == 0, False)
            with eng.Fori(1, TRIPS - 1) as j:
                for r in range(R):
                    step(j, r, False, False)
            for r in range(R):
                step(TRIPS - 1, r, False, r == R - 1)

        def after(j, r):
            return (j, r + 1) if r < R - 1 else (j + 1, 0)

        @block.vector
        def _(dve):
            v = nc.vector
            ch = Chain(dve, own)

            def onehot_tile(j, r, t):
                ins = v.tensor_scalar(onehot[r][:, t, :], g["iota"][:, :],
                                      g["edges"][1][:, bass.ds(j * (R * T) + (r * T + t), 1)], None, ALU.is_equal)
                if t == T - 1:
                    ins.then_inc(onehot_ready, 1)

            def scan(j, r):
                dve.wait_ge(score_t_ready, j * R + (r + 1))
                v.tensor_tensor_scan(run_max[:, :], turn_ps[0:TH, P:2 * P], score_t[:, :], NEG, ALU.add,
                                     ALU.max).then_inc(scanned, 1)

            def candidates(j, r):
                last = tile_at(g["edges"][3], j * R + r, T)
                dve.wait_ge(back_ready, j * R + (r + 1))
                v.tensor_scalar(cand[:, :, H], last, 1.0, None, ALU.mult)
                v.tensor_tensor(cand[:, :, 0:H], back_ps[:, :, :], last.unsqueeze(2).broadcast_to([P, T, H]),
                                ALU.mult).then_inc(cand_ready, 1)

            def block_at(j, r):
                return dve.value_load(g["block_of_step"][0:1, bass.ds(j * R + r, 1)], min_val=0, max_val=NB - 1)

            def step(j, r, first, last, b_fold):
                n = j * R + (r + 1)
                b = block_at(j, r)
                if not first and r < 2:
                    b_fold = block_at(j - 1, R - 2 + r)
                nj, nr = after(j, r)
                st = tile_at(g["state"], b, 2 * H)
                new = dst_max[r % 2]
                v.tensor_scalar(new[:, 0:H], st[:, 0:H], 1.0, None, ALU.mult)
                dve.wait_ge(cand_spread, n)
                fill = [] if last else [lambda t=t: onehot_tile(nj, nr, t) for t in range(T)]

                def linked(ins):
                    ch.link_after(ins, fill.pop(0) if fill else None)

                linked(v.tensor_scalar(absent[:, :], cand_ps[:, :, H], -NEG, NEG, ALU.mult, ALU.add))
                linked(v.tensor_tensor(cand_m[:, :, :], cand_ps[:, :, 0:H],
                                       absent[:, :].unsqueeze(2).broadcast_to([P, T, H]), ALU.add))
                linked(v.tensor_reduce(top[:, :], cand_m[:, :, :].rearrange("p t h -> p h t"), AX_X, ALU.max))
                linked(v.tensor_tensor(top2[:, :], top[:, :], st[:, 0:H], ALU.add))
                linked(v.scalar_tensor_tensor(top[:, :], top2[:, :], 0.2, top2[:, :], ALU.mult, ALU.max))
                v.tensor_tensor(new[:, H:2 * H], top[:, :], st[:, H:2 * H], ALU.max).then_inc(dst_max_ready, 1)
                if not first:
                    acc = tile_at(g["acc"], b_fold, RW)
                    acc3 = acc.rearrange("p (h n) -> p h n", n=HW_)
                    dve.wait_ge(fade_ready, n - 2)
                    ins = v.tensor_tensor(acc3, acc3, fade[(r - 2) % R][:, :].unsqueeze(2).broadcast_to([P, H, HW_]),
                                          ALU.mult)
                    ins.then_inc(sums_faded, 1)
                dve.wait_ge(dst_max_ready, n)
                ch.link(v.tensor_tensor(drop[r % 2][:, :], st[:, H:2 * H], new[:, H:2 * H], ALU.subtract))
                v.tensor_scalar(st[:, H:2 * H], new[:, H:2 * H], 1.0, None, ALU.mult).then_inc(drop_ready, 1)
                if not first:
                    dve.wait_ge(sums_faded, n - 2)
                    dve.wait_ge(slots_free, n - 2 + R)
                    v.tensor_tensor(acc, sum_ps[r % 2][:, :], acc, ALU.add).then_inc(sums_added, 1)
                dve.wait_ge(edge_ready, n)
                z_, z2_ = z[:, :, :], z2[:, :, :]
                src = rows[r][:, :, :].rearrange("p t (h n) -> p t h n", n=HW_)[:, :, :, C]
                ch.link_after(v.tensor_tensor(z_, edge_ps[:, :, 0:H], src, ALU.add),
                              None if last else lambda: scan(nj, nr))
                ch.link(v.scalar_tensor_tensor(z2_, z_, 0.2, z_, ALU.mult, ALU.max))
                ch.link(v.tensor_tensor(z_, edge_ps[:, :, H:2 * H], z2_, ALU.subtract))
                v.tensor_scalar(arg[r % 2][:, :, :], z_, -1.0, 0.0, ALU.mult, ALU.min).then_inc(arg_ready, 1)
                if not last:
                    candidates(nj, nr)
                dve.wait_ge(weights_ready, n)
                msg = headed(rows[r][:, :, :])[:, :, 0:C]
                w = weight_ps[:, :, :].rearrange("p t h -> p (t h)").unsqueeze(2).broadcast_to([P, TH, C])
                v.tensor_tensor(msg, msg, w, ALU.mult).then_inc(rows_weighed, 1)
                return b

            def trip(j, first, last):
                b = []
                for r in range(R):
                    b.append(step(j, r, first and r < 2, last and r == R - 1, b[r - 2] if r >= 2 else None))
                return b

            LINKS = 5 + 1 + 3
            for t in range(T):
                onehot_tile(0, 0, t)
            scan(0, 0)
            candidates(0, 0)
            trip(0, True, False)
            ch.end()
            with dve.Fori(1, TRIPS - 1) as j:
                ch.begin(j - 1, LINKS * R)
                trip(j, False, False)
            ch.end(TRIPS - 2)
            for n, b in enumerate(trip(TRIPS - 1, False, True)[R - 2:]):
                acc = tile_at(g["acc"], b, RW)
                acc3 = acc.rearrange("p (h n) -> p h n", n=HW_)
                dve.wait_ge(fade_ready, STEPS4 - 1 + n)
                if n:
                    dve.wait_ge(sums_added, STEPS4 - 1)
                ch.link(v.tensor_tensor(acc3, acc3, fade[R - 2 + n][:, :].unsqueeze(2).broadcast_to([P, H, HW_]), ALU.mult))
                dve.wait_ge(slots_free, STEPS4 - 1 + n + R)
                v.tensor_tensor(acc, sum_ps[n][:, :], acc, ALU.add).then_inc(sums_added, 1)

        @block.scalar
        def _(act):
            s = nc.scalar

            def indices(j, k):
                s.copy(index[k][:, :], tile_at(g["edges"][0], j, R * T)).then_inc(index_ready, 1)

            def begins(j, r):
                s.copy(begin[:, :, :], tile_at(g["edges"][2], j * R + r, T).unsqueeze(2).broadcast_to([P, T, H])
                       ).then_inc(begin_ready, 1)

            def scores(j, r):
                act.wait_ge(scores_turned, j * R + (r + 1))
                s.copy(score_t[:, :], turn_ps[0:TH, 0:P]).then_inc(score_t_ready, 1)

            def onehots(j, r):
                act.wait_ge(onehot_turned, j * R + (r + 1))
                s.copy(onehot_t[r % 2][:, :, :], onehot_ps[:, :, :]).then_inc(onehot_t_ready, 1)

            def fades(j, r):
                act.wait_ge(drop_ready, j * R + (r + 1))
                s.activation(fade[r][:, :], drop[r % 2][:, :], ACT.Exp).then_inc(fade_ready, 1)

            def weights(j, r):
                act.wait_ge(arg_ready, j * R + (r + 1))
                x = arg[r % 2][:, :, :]
                s.activation(weight_ps[:, :, :], x, ACT.Exp)
                s.activation(headed(rows[r][:, :, :])[:, :, C:HW_].rearrange("p n one -> p (n one)"),
                             x.rearrange("p t h -> p (t h)"), ACT.Exp).then_inc(weights_ready, 1)

            def step(j, r, k, last, ahead):
                if not last:
                    begins(*after(j, r))
                    scores(*after(j, r))
                    onehots(*after(j, r))
                fades(j, r)
                weights(j, r)
                if ahead and r == 0:
                    indices(j + 1, 1 - k)

            indices(0, 0)
            begins(0, 0)
            scores(0, 0)
            onehots(0, 0)
            for r in range(R):
                step(0, r, 0, False, True)
            assert TRIPS % 2 == 1
            with act.Fori(0, (TRIPS - 3) // 2) as m:
                for r in range(R):
                    step(m * 2 + 1, r, 1, False, True)
                for r in range(R):
                    step(m * 2 + 2, r, 0, False, True)
            for r in range(R):
                step(TRIPS - 2, r, 1, False, True)
            for r in range(R):
                step(TRIPS - 1, r, 0, r == R - 1, False)

        @block.tensor
        def _(pe):
            t = nc.tensor

            def scores(j, r):
                pe.wait_ge(rows_in[r], (j + 1) * (16 * T))
                src = headed(rows[r][:, :, :])[:, :, C:HW_].rearrange("p n one -> p (n one)")
                t.transpose(turn_ps[0:TH, 0:P], src, g["ident"][:, :])
                pe.wait_ge(begin_ready, j * R + (r + 1))
                t.transpose(turn_ps[0:TH, P:2 * P], begin[:, :, :].rearrange("p t h -> p (t h)"),
                            g["ident"][:, :]).then_inc(scores_turned, 1)

            def onehots(j, r):
                pe.wait_ge(onehot_ready, j * R + (r + 1))
                for n in range(T):
                    ins = t.transpose(onehot_ps[:, n, :], onehot[r][:, n, :], g["ident"][:, :])
                ins.then_inc(onehot_turned, 1)

            def back(j, r):
                pe.wait_ge(scanned, j * R + (r + 1))
                t.matmul(back_ps[:, :, :].rearrange("p t h -> p (t h)"), run_max[:, :], g["ident"][0:TH, 0:TH],
                         start=True, stop=True).then_inc(back_ready, 1)

            def spread(j, r):
                pe.wait_ge(cand_ready, j * R + (r + 1))
                for n in range(T):
                    ins = t.matmul(cand_ps[:, n, :], onehot[r][:, n, :], cand[:, n, :], start=True, stop=True)
                ins.then_inc(cand_spread, 1)

            def to_edges(j, r):
                pe.wait_ge(dst_max_ready, j * R + (r + 1))
                pe.wait_ge(onehot_t_ready, j * R + (r + 1))
                for n in range(T):
                    ins = t.matmul(edge_ps[:, n, :], onehot_t[r % 2][:, n, :], dst_max[r % 2][:, :], start=True, stop=True)
                ins.then_inc(edge_ready, 1)

            def sums(j, r, tiles):
                if 0 in tiles:
                    pe.wait_ge(rows_weighed, j * R + (r + 1))
                for n in tiles:
                    ins = t.matmul(sum_ps[r % 2][:, :], onehot[r][:, n, :], rows[r][:, n, :],
                                   start=(n == 0), stop=(n == T - 1))
                if T - 1 in tiles:
                    ins.then_inc(slots_free, 1)

            def step(j, r, first, last):
                if not last:
                    scores(*after(j, r))
                    pe.wait_ge(onehot_t_ready, j * R + (r + 1))
                    onehots(*after(j, r))
                to_edges(j, r)
                prev = (j, r - 1) if r else (j - 1, R - 1)
                if not first:
                    sums(*prev, [0])
                if not last:
                    back(*after(j, r))
                if not first:
                    sums(*prev, [1])
                if not last:
                    spread(*after(j, r))
                if not first:
                    sums(*prev, [2, 3])

            scores(0, 0)
            onehots(0, 0)
            back(0, 0)
            spread(0, 0)
            run(pe, step)
            sums(TRIPS - 1, R - 1, range(T))


def route_phase(nc, a, g):
    with ExitStack() as ctx:
        sb, ps, sem = memory(nc, ctx, "route")
        rden = sb("rden", [P, NB * H])
        res = [sb(f"res{k}", [P, D]) for k in range(2)]
        gamma = sb("gamma", [P, D])
        beta = sb("beta", [P, D])
        gate = sb("gate", [P, KC, E])
        gate_b = sb("gate_b", [P, E])
        node = [sb(f"node{k}", [P, D]) for k in range(2)]
        stats = sb("stats", [P, NB * 6])
        mean = sb("mean", [P, NB])
        var = sb("var", [P, NB])
        half = sb("half", [P, NB])
        xn = [sb(f"xn{k}", [P, D]) for k in range(2)]
        xn_t = [sb(f"xn_t{k}", [P, KC, P]) for k in range(2)]
        down = sb("down", [P, E])
        valid = sb("valid", [P, 1])
        lane = sb("lane", [P, E])
        logit = sb("logit", [P, NB, E])
        ex = sb("ex", [P, NB, E])
        pr = sb("pr", [P, NB, E])
        score = sb("score", [P, NB, E])
        pick = sb("pick", [P, NB, E])
        totals = sb("totals", [P, NB, E])
        before = sb("before", [P, NB, E])
        one = sb("one", [P, NB])
        big = sb("big", [P, NB])
        inv = sb("inv", [P, NB])
        place = sb("place", [P, NB])
        home = sb("home", [P, NB])
        slot = sb("slot", [P, NB])
        send = sb("send", [P, NB])
        index = sb("index", [P, NB], I32)

        xt_ps = [ps(f"xt_ps{k}", D).rearrange("p (c n) -> p c n", c=KC) for k in range(2)]
        logit_ps = [ps(f"logit_ps{k}", E) for k in range(2)]
        upto_ps = ps("upto_ps", NB * E).rearrange("p (b e) -> p b e", e=E)
        total_ps = ps("total_ps", NB * E).rearrange("p (b e) -> p b e", e=E)

        own = sem("own")
        loaded = sem("loaded")
        res_in = [sem(f"res_in{k}") for k in range(2)]
        res_used = sem("res_used")
        var_ready = sem("var_ready")
        root_ready = sem("root_ready")
        xn_ready = sem("xn_ready")
        xn_turned = sem("xn_turned")
        xn_t_ready = sem("xn_t_ready")
        logits_ready = sem("logits_ready")
        logits_kept = sem("logits_kept")
        shifted = sem("shifted")
        exp_ready = sem("exp_ready")
        picked = sem("picked")
        counted = sem("counted")
        placed = sem("placed")
        rows_out = sem("rows_out")
        block = ctx.enter_context(nc.Block())
        NLOAD = 4

        @block.sync
        def _(sp):
            with nc.allow_non_contiguous_dma(reason="the gate's 8 columns"):
                for t, src in ((gamma[:, :], a["L1_gnn_gamma"].partition_broadcast(P)),
                               (beta[:, :], a["L1_gnn_beta"].partition_broadcast(P)),
                               (gate[:, :, :], a["L1_ffn_gate_w"].rearrange("(c p) e -> p c e", p=P)),
                               (gate_b[:, :], a["L1_ffn_gate_b"].partition_broadcast(P))):
                    sp.dma_start(t, src).then_inc(loaded, 16)

            def load(i, k):
                sp.wait_ge(res_used, i + 1)
                sp.dma_start(res[k][:, :], g["residual"][bass.ds(i * P, P), :]).then_inc(res_in[k], 16)

            in_pairs(sp, NB, load)

        @block.vector
        def _(dve):
            v = nc.vector
            ch = Chain(dve, own)
            dve.sem_inc(res_used, 2)
            v.tensor_scalar(down[:, :], g["iota"][:, 0:E], -1.0, float(E), ALU.mult, ALU.add)
            v.tensor_scalar(lane[:, :], g["iota"][:, 0:E], float(PITCH), None, ALU.mult)
            v.tensor_scalar(valid[:, :], g["pidx"][:, :], float(TAIL), None, ALU.is_lt)
            den = g["acc"][:, :].rearrange("p (n w) -> p n w", w=HW_)[:, :, C]
            ch.link(v.tensor_scalar(rden[:, :], den, 1e-16, None, ALU.add))
            ch.link(v.reciprocal(rden[:, :], rden[:, :]))
            dve.wait_ge(loaded, 16 * NLOAD)

            def attended(i, k):
                dve.wait_ge(res_used, i + 1)
                msg = tile_at(g["acc"], i, RW).rearrange("p (h n) -> p h n", n=HW_)[:, :, 0:C]
                r = tile_at(rden, i, H).unsqueeze(2).broadcast_to([P, H, C])
                return v.tensor_tensor(node[k][:, :].rearrange("p (h n) -> p h n", h=H), msg, r, ALU.mult)

            def with_residual(i, k):
                dve.wait_ge(res_in[k], ((i - k) * 8) + 16)
                v.tensor_tensor(tile_at(g["acc"], i, RW)[:, 0:D], node[k][:, :], res[k][:, :], ALU.add).then_inc(res_used, 1)

            def layer_norm_steps(i, k):
                n = node[k][:, :]
                xb = tile_at(g["xf"], i, D)
                return (lambda: v.tensor_scalar(n, tile_at(g["acc"], i, RW)[:, 0:D], mean[:, bass.ds(i, 1)],
                                                var[:, bass.ds(i, 1)], ALU.subtract, ALU.mult),
                        lambda: v.tensor_tensor(n, n, gamma[:, :], ALU.mult),
                        lambda: v.tensor_tensor(n, n, beta[:, :], ALU.add),
                        lambda: v.tensor_tensor(xb, n, xb, ALU.add))

            ch.end()
            with dve.Fori(0, NB // 2) as j:
                ch.begin(j, 2)
                ch.link_after(attended(j * 2, 0), lambda: ch.link(attended(j * 2 + 1, 1)))
                with_residual(j * 2, 0)
                with_residual(j * 2 + 1, 1)
            ch.end(NB // 2)
            ch.link(attended(NB - 1, 0))
            with_residual(NB - 1, 0)
            dve.wait_ge(res_used, NB + 2)
            emit_stats(nc, dve, ch, g["acc"], RW, stats, mean, var, half, var_ready)
            dve.wait_ge(root_ready, 1)
            ch.link(v.reciprocal(var[:, :], var[:, :]))
            ch.end()
            with dve.Fori(0, NB // 2) as j:
                ch.begin(j, 8)
                for first, second in zip(layer_norm_steps(j * 2, 0), layer_norm_steps(j * 2 + 1, 1)):
                    ins = first()
                    ch.link_after(ins, lambda: ch.note(second()))
                    ch.settle()
            ch.end(NB // 2)
            for one_step in layer_norm_steps(NB - 1, 0):
                ch.link(one_step())
            emit_stats(nc, dve, ch, g["xf"], D, stats, mean, var, half, var_ready)
            dve.wait_ge(root_ready, 2)
            ch.link(v.reciprocal(var[:, :], var[:, :]))
            dve.sem_inc(xn_turned, 2)

            def norm(i, k):
                dve.wait_ge(xn_turned, i + 1)
                if not isinstance(i, int) or i >= 2:
                    dve.wait_ge(xn_t_ready, i - 1)
                v.tensor_scalar(xn[k][:, :], tile_at(g["xf"], i, D), mean[:, bass.ds(i, 1)], var[:, bass.ds(i, 1)],
                                ALU.subtract, ALU.mult).then_inc(xn_ready, 1)

            def keep(i, k):
                dve.wait_ge(logits_ready, i + 1)
                v.tensor_tensor(logit[:, bass.ds(i, 1), :].rearrange("p one e -> p (one e)"), logit_ps[k][:, :],
                                gate_b[:, :], ALU.add).then_inc(logits_kept, 1)

            norm(0, 0)
            norm(1, 1)
            with dve.Fori(0, NB // 2 - 1) as j:
                norm(j * 2 + 2, 0)
                keep(j * 2, 0)
                norm(j * 2 + 3, 1)
                keep(j * 2 + 1, 1)
            norm(NB - 1, 0)
            keep(NB - 3, 0)
            keep(NB - 2, 1)
            keep(NB - 1, 0)

            def wide(t):
                return t[:, :].unsqueeze(2).broadcast_to([P, NB, E])

            def over_blocks(t):
                return t[:, :].unsqueeze(1).broadcast_to([P, NB, E])

            dve.wait_ge(logits_kept, NB)
            ch.link(v.reduce_max(big[:, :], logit[:, :, :], AX_X))
            v.tensor_tensor(logit[:, :, :], logit[:, :, :], wide(big), ALU.subtract).then_inc(shifted, 1)
            dve.wait_ge(exp_ready, 1)
            ch.link(v.reduce_sum(inv[:, :], ex[:, :, :], AX_X))
            ch.link(v.reciprocal(inv[:, :], inv[:, :]))
            ch.link(v.tensor_tensor(pr[:, :, :], ex[:, :, :], wide(inv), ALU.mult))
            ch.link(v.reduce_max(big[:, :], pr[:, :, :], AX_X))
            v.tensor_copy(g["acc"][:, :].rearrange("p (b w) -> p b w", w=RW)[:, :, D], big[:, :])
            ch.link(v.tensor_tensor(score[:, :, :], pr[:, :, :], wide(big), ALU.is_equal))
            ch.link(v.tensor_tensor(score[:, :, :], score[:, :, :], over_blocks(down), ALU.mult))
            ch.link(v.reduce_max(one[:, :], score[:, :, :], AX_X))
            ch.link(v.tensor_tensor(pick[:, :, :], score[:, :, :], wide(one), ALU.is_equal))
            v.tensor_scalar(pick[:, NB - 1, :], pick[:, NB - 1, :], valid[:, 0:1], None, ALU.mult).then_inc(picked, 1)
            dve.wait_ge(counted, 1)
            ch.link(v.tensor_copy(totals[:, :, :], total_ps[:, :, :]))
            for e in range(E):
                ins = v.tensor_tensor_scan(before[:, :, e], totals[:, :, e], totals[:, :, e], 0.0, ALU.add, ALU.bypass)
            ch.link(ins)
            ch.link(v.tensor_tensor(before[:, :, :], before[:, :, :], totals[:, :, :], ALU.subtract))
            ch.link(v.tensor_tensor(before[:, :, :], upto_ps[:, :, :], before[:, :, :], ALU.add))
            ch.link(v.tensor_tensor(before[:, :, :], before[:, :, :], pick[:, :, :], ALU.mult))
            ch.link(v.reduce_sum(place[:, :], before[:, :, :], AX_X))
            ch.link(v.tensor_tensor(score[:, :, :], pick[:, :, :], over_blocks(lane), ALU.mult))
            ch.link(v.reduce_sum(home[:, :], score[:, :, :], AX_X))
            ch.link(v.tensor_scalar(g["kept"][:, :], place[:, :], float(CAP), None, ALU.is_le))
            ch.link(v.tensor_scalar(place[:, :], place[:, :], -1.0, None, ALU.add))
            ch.link(v.tensor_scalar(slot[:, :], place[:, :], float(CAP - 1), 0.0, ALU.min, ALU.max))
            ch.link(v.tensor_tensor(slot[:, :], slot[:, :], home[:, :], ALU.add))
            v.tensor_copy(g["slot"][:, :], slot[:, :])
            ch.link(v.tensor_scalar(send[:, :], g["kept"][:, :], -float(E * PITCH), float(E * PITCH), ALU.mult, ALU.add))
            ch.link(v.tensor_tensor(send[:, :], send[:, :], slot[:, :], ALU.add))
            v.tensor_scalar(valid[:, :], valid[:, :], -float(E * PITCH), float(E * PITCH), ALU.mult, ALU.add)
            dve.drain()
            ch.link(v.tensor_tensor(send[:, NB - 1:NB], send[:, NB - 1:NB], valid[:, :], ALU.add))
            v.tensor_copy(index[:, :], send[:, :]).then_inc(placed, 1)

        @block.scalar
        def _(act):
            s = nc.scalar
            for n in range(2):
                act.wait_ge(var_ready, n + 1)
                s.activation(var[:, :], var[:, :], ACT.Sqrt, bias=g["eps"][:, 0:1]).then_inc(root_ready, 1)

            def turned(i, k):
                act.wait_ge(xn_turned, i + 3)
                if not isinstance(i, int) or i >= 2:
                    act.wait_ge(logits_ready, i - 1)
                s.copy(xn_t[k][:, :, :], xt_ps[k][:, :, :])
                s.copy(tile_at(g["acc"], i, RW)[:, 0:D], xn[k][:, :]).then_inc(xn_t_ready, 1)

            turned(0, 0)
            turned(1, 1)
            with act.Fori(1, NB // 2) as j:
                turned(j * 2, 0)
                turned(j * 2 + 1, 1)
            turned(NB - 1, 0)
            act.wait_ge(shifted, 1)
            s.activation(ex[:, :, :], logit[:, :, :], ACT.Exp).then_inc(exp_ready, 1)

        @block.tensor
        def _(pe):
            t = nc.tensor
            pe.wait_ge(loaded, 16 * NLOAD)

            def turn(i, k):
                pe.wait_ge(xn_ready, i + 1)
                for c in range(KC):
                    ins = t.transpose(xt_ps[k][:, c, :], xn[k][:, c * P:(c + 1) * P], g["ident"][:, :])
                ins.then_inc(xn_turned, 1)

            def gates(i, k, first=False):
                pe.wait_ge(xn_t_ready, i + 1)
                if not first:
                    pe.wait_ge(logits_kept, i - 1)
                for c in range(KC):
                    ins = t.matmul(logit_ps[k][:, :], xn_t[k][:, c, :], gate[:, c, :], start=(c == 0), stop=(c == KC - 1))
                ins.then_inc(logits_ready, 1)

            turn(0, 0)
            turn(1, 1)
            gates(0, 0, True)
            turn(2, 0)
            gates(1, 1, True)
            with pe.Fori(1, NB // 2) as j:
                turn(j * 2 + 1, 1)
                gates(j * 2, 0)
                turn(j * 2 + 2, 0)
                gates(j * 2 + 1, 1)
            gates(NB - 1, 0)
            pe.wait_ge(picked, 1)
            pk = pick[:, :, :].rearrange("p b e -> p (b e)")
            t.matmul(upto_ps.rearrange("p b e -> p (b e)"), g["upper"][:, :], pk, start=True, stop=True)
            t.matmul(total_ps.rearrange("p b e -> p (b e)"), g["ones"][:, :], pk, start=True, stop=True).then_inc(counted, 1)

        @block.gpsimd
        def _(pool):
            pool.wait_ge(placed, 1)
            for i in range(NB):
                nc.gpsimd.indirect_dma_start(
                    out=g["sent"][:, :], in_=g["acc"][:, i * RW:(i + 1) * RW], in_offset=None,
                    out_offset=bass.IndirectOffsetOnAxis(ap=index[:, i:i + 1], axis=0),
                    bounds_check=E * PITCH - 1, oob_is_err=False).then_inc(rows_out, 16)
            pool.wait_ge(rows_out, 16 * NB)


def expert_phase(nc, a, g):
    with ExitStack() as ctx:
        sb, ps, sem = memory(nc, ctx, "expert")
        NT = -(-CAP // P)
        CP = NT * P
        HALF = CP // 2
        FC = F // P
        w1 = [sb(f"w1_{k}", [P, KC, F]) for k in range(2)]
        w2 = [sb(f"w2_{k}", [P, FC, D]) for k in range(2)]
        xe = [sb(f"xe{k}", [P, NT, RW]) for k in range(2)]
        xe_t = sb("xe_t", [P, KC, CP])
        hid = sb("hid", [P, FC, CP])
        b1_in = sb("b1_in", [E * FC, P])
        b1 = sb("b1", [P, E * FC])
        b1_e = [sb(f"b1_e{k}", [P, FC]) for k in range(2)]
        b2 = sb("b2", [P, E * D])
        y = [sb(f"y{k}", [P, D]) for k in range(2)]
        flag = [sb(f"flag{n}", [P, D], I32) for n in range(3)]
        fill = [sb(f"fill{n}", [P, D]) for n in range(3)]
        xt_ps = [ps(f"xt_ps{k}", 512).rearrange("p (t n) -> p t n", n=P) for k in range(2)]
        hid_ps = [ps(f"hid_ps{k}", HALF) for k in range(2)]
        y_ps = [ps(f"y_ps{k}", D) for k in range(2)]

        own = sem("own")
        bias_in = sem("bias_in")
        b1_turned = sem("b1_turned")
        b1_ready = sem("b1_ready")
        b1_picked = sem("b1_picked")
        loaded = [sem(f"loaded{k}") for k in range(2)]
        rows_turned = sem("rows_turned")
        rows_t_ready = sem("rows_t_ready")
        up_ready = sem("up_ready")
        hid_ready = sem("hid_ready")
        down_ready = sem("down_ready")
        y_read = sem("y_read")
        y_ready = sem("y_ready")
        y_out = [sem(f"y_out{k}") for k in range(2)]
        block = ctx.enter_context(nc.Block())
        NX = KC * NT // 4
        NU = FC * 2
        fill_values = (1.0e4, -1.0e4, 0.0)
        FMAX = 3.4028234663852886e38

        @block.sync
        def _(sp):
            sp.dma_start(b1_in[:, :], a["L1_ffn_b1"].rearrange("e (c p) -> (e c) p", p=P)).then_inc(bias_in, 16)
            sp.dma_start(b2[:, :], a["L1_ffn_b2"].rearrange("e d -> (e d)").partition_broadcast(P)).then_inc(bias_in, 16)

            def load(e, k, wait=True):
                if wait:
                    sp.wait_ge(down_ready, (e - 1) * NT)
                sp.dma_start(xe[k][:, :, :], g["sent"][bass.ds(e * PITCH, PITCH), :].rearrange("(t p) w -> p t w", p=P)
                             ).then_inc(loaded[k], 16)
                sp.dma_start(w1[k][:, :, :], a["L1_ffn_w1"][bass.ds(e * D, D), :].rearrange("(c p) f -> p c f", p=P)
                             ).then_inc(loaded[k], 16)
                sp.dma_start(w2[k][:, :, :], a["L1_ffn_w2"][bass.ds(e * F, F), :].rearrange("(c p) d -> p c d", p=P)
                             ).then_inc(loaded[k], 16)

            def store(e):
                for t in range(NT):
                    sp.wait_ge(y_ready, e * NT + (t + 1))
                    sp.dma_start(g["answers"][bass.ds(e * PITCH + t * P, P), :], y[t % 2][:, :]).then_inc(y_out[t % 2], 16)

            load(0, 0, False)
            load(1, 1, False)
            with sp.Fori(0, E // 2 - 1) as j:
                store(j * 2)
                load(j * 2 + 2, 0)
                store(j * 2 + 1)
                load(j * 2 + 3, 1)
            store(E - 2)
            store(E - 1)
            for k in range(2):
                sp.wait_ge(y_out[k], 16 * E * NT // 2)

        @block.vector
        def _(dve):
            v = nc.vector
            ch = Chain(dve, own)
            for n in range(3):
                ch.link(v.memset(fill[n][:, :], fill_values[n]))
            dve.wait_ge(bias_in, 32)

            def outs(e, k, first):
                for t in range(NT):
                    y_, yp = y[t % 2][:, :], y_ps[t % 2][:, :]
                    dve.wait_ge(down_ready, e * NT + (t + 1))
                    if not (first and t < 2):
                        dve.wait_ge(y_out[t % 2], e * (8 * NT) + (t // 2) * 16)
                    v.tensor_tensor(y_, yp, b2[:, bass.ds(e * D, D)], ALU.add).then_inc(y_read, 1)
                    dve.wait_ge(y_read, e * NT + (t + 1))
                    ch.link(v.tensor_scalar(y_, y_, xe[k][:, t, D:D + 1], None, ALU.mult))
                    v.tensor_scalar(flag[0][:, :], y_, FMAX, None, ALU.is_gt)
                    v.tensor_scalar(flag[1][:, :], y_, -FMAX, None, ALU.is_lt)
                    v.tensor_tensor(flag[2][:, :], y_, y_, ALU.not_equal)
                    for n in range(3):
                        dve.drain()
                        ins = v.copy_predicated(y_, flag[n][:, :], fill[n][:, :])
                    ins.then_inc(y_ready, 1)

            outs(0, 0, True)
            outs(1, 1, False)
            ch.end()
            with dve.Fori(1, E // 2) as j:
                ch.begin(j - 1, 2 * NT)
                outs(j * 2, 0, False)
                outs(j * 2 + 1, 1, False)
            ch.end(E // 2 - 1)

        @block.scalar
        def _(act):
            s = nc.scalar
            act.wait_ge(b1_turned, 1)
            s.copy(b1[:, :], xt_ps[0][:, 0, 0:E * FC]).then_inc(b1_ready, 1)
            act.wait_ge(b1_ready, 1)

            def rows(e, n):
                c, q = divmod(n, NT // 4)
                act.wait_ge(rows_turned, e * NX + (n + 1))
                s.copy(xe_t[:, c, q * 512:(q + 1) * 512].rearrange("p (t n) -> p t n", n=P), xt_ps[n % 2][:, :, :]
                       ).then_inc(rows_t_ready, 1)

            def expert(e, k):
                s.copy(b1_e[k][:, :], b1[:, bass.ds(e * FC, FC)]).then_inc(b1_picked, 1)
                for n in range(NX):
                    rows(e, n)
                act.wait_ge(b1_picked, e + 1)
                for u in range(NU):
                    f, half = divmod(u, 2)
                    act.wait_ge(up_ready, e * NU + (u + 1))
                    s.activation(hid[:, f, half * HALF:(half + 1) * HALF], hid_ps[u % 2][:, :], ACT.Relu,
                                 bias=b1_e[k][:, f:f + 1]).then_inc(hid_ready, 1)

            in_pairs(act, E, expert)

        @block.tensor
        def _(pe):
            t = nc.tensor
            pe.wait_ge(bias_in, 32)
            t.transpose(xt_ps[0][:, 0, 0:E * FC], b1_in[:, :], g["ident"][0:E * FC, 0:E * FC]).then_inc(b1_turned, 1)
            pe.wait_ge(b1_ready, 1)

            def expert(e, k, first):
                pe.wait_ge(loaded[k], (e - k) * 24 + 48)
                for n in range(NX):
                    c, q = divmod(n, NT // 4)
                    if n >= 2:
                        pe.wait_ge(rows_t_ready, e * NX + (n - 1))
                    for i in range(4):
                        ins = t.transpose(xt_ps[n % 2][:, i, :], xe[k][:, q * 4 + i, c * P:(c + 1) * P], g["ident"][:, :])
                    ins.then_inc(rows_turned, 1)
                pe.wait_ge(rows_t_ready, e * NX + NX)
                for u in range(NU):
                    f, half = divmod(u, 2)
                    if u >= 2:
                        pe.wait_ge(hid_ready, e * NU + (u - 1))
                    for c in range(KC):
                        ins = t.matmul(hid_ps[u % 2][:, :], w1[k][:, c, f * P:(f + 1) * P],
                                       xe_t[:, c, half * HALF:(half + 1) * HALF], start=(c == 0), stop=(c == KC - 1))
                    ins.then_inc(up_ready, 1)
                pe.wait_ge(hid_ready, e * NU + NU)
                for n in range(NT):
                    if not (first and n < 2):
                        pe.wait_ge(y_read, e * NT + (n - 1))
                    for f in range(FC):
                        ins = t.matmul(y_ps[n % 2][:, :], hid[:, f, n * P:(n + 1) * P], w2[k][:, f, :],
                                       start=(f == 0), stop=(f == FC - 1))
                    ins.then_inc(down_ready, 1)

            expert(0, 0, True)
            expert(1, 1, False)
            with pe.Fori(1, E // 2) as j:
                expert(j * 2, 0, False)
                expert(j * 2 + 1, 1, False)


def combine_phase(nc, a, g, out):
    with ExitStack() as ctx:
        sb, ps, sem = memory(nc, ctx, "combine")
        R = 4
        index = sb("index", [P, NB], I32)
        rows = [sb(f"rows{k}", [P, D]) for k in range(R)]
        index_ready = sem("index_ready")
        rows_in = [sem(f"rows_in{k}") for k in range(R)]
        rows_added = sem("rows_added")
        stored = sem("stored")
        block = ctx.enter_context(nc.Block())

        @block.scalar
        def _(act):
            nc.scalar.copy(index[:, :], g["slot"][:, :]).then_inc(index_ready, 1)

        @block.gpsimd
        def _(pool):
            pool.wait_ge(index_ready, 1)
            for i in range(NB):
                if i >= R:
                    pool.wait_ge(rows_added, i - R + 1)
                nc.gpsimd.indirect_dma_start(
                    out=rows[i % R][:, :], out_offset=None, in_=g["answers"][:, :],
                    in_offset=bass.IndirectOffsetOnAxis(ap=index[:, i:i + 1], axis=0)).then_inc(rows_in[i % R], 16)

        @block.vector
        def _(dve):
            for i in range(NB):
                dve.wait_ge(rows_in[i % R], 16 * (i // R + 1))
                xb = g["x"][:, i, :]
                nc.vector.scalar_tensor_tensor(xb, rows[i % R][:, :], g["kept"][:, i:i + 1], xb, ALU.mult,
                                               ALU.add).then_inc(rows_added, 1)

        @block.sync
        def _(sp):
            for i in range(NB):
                n = P if i < NB - 1 else TAIL
                sp.wait_ge(rows_added, i + 1)
                sp.dma_start(out[i * P:i * P + n, :], g["x"][0:n, i, :]).then_inc(stored, 16)
            sp.wait_ge(stored, 16 * NB)


def program(nc, a, out):
    with ExitStack() as whole:
        def sb(name, shape, dt=F32, ctx=whole):
            return ctx.enter_context(nc.sbuf_tensor(name, shape, dt))

        g = {"table0": nc.dram_tensor("table0", [NB * P, D], F32).ap(),
             "table1": nc.dram_tensor("table1", [NB * P, RW], F32).ap(),
             "residual": nc.dram_tensor("residual", [NB * P, D], F32).ap(),
             "sent": nc.dram_tensor("sent", [E * PITCH, RW], F32).ap(),
             "answers": nc.dram_tensor("answers", [E * PITCH, D], F32).ap(),
             "x": sb("x_all", [P, NB, D]),
             "iota": sb("iota", [P, P]), "pidx": sb("pidx", [P, 1]), "ident": sb("ident", [P, P]),
             "upper": sb("upper", [P, P]), "ones": sb("ones", [P, P]), "eps": sb("eps", [P, 1]),
             "kept": sb("kept", [P, NB]), "slot": sb("slot", [P, NB])}
        g["xf"] = g["x"][:, :, :].rearrange("p b d -> p (b d)")
        with ExitStack() as graph:
            g["edges"] = [sb(f"edges{n}", [P, SQ * P * T], F32, graph) for n in range(4)]
            g["block_of_step"] = sb("block_of_step", [1, SQ * P], I32, graph)
            g["dinv"] = sb("dinv", [P, NB], F32, graph)
            g["state"] = sb("state", [P, NB * 2 * H], F32, graph)
            setup_phase(nc, a, g)
            g["acc"] = sb("acc", [P, NB * RW], F32, graph)
            gcn_table_phase(nc, a, g)
            gcn_steps_phase(nc, a, g)
            moe_phase(nc, a, g)
            gat_table_phase(nc, a, g)
            gat_steps_phase(nc, a, g)
            route_phase(nc, a, g)
        expert_phase(nc, a, g)
        combine_phase(nc, a, g, out)


INS = ["x", "src", "dst",
       "L0_gnn_W", "L0_gnn_b", "L0_gnn_gamma", "L0_gnn_beta",
       "L0_ffn_router_w", "L0_ffn_w1", "L0_ffn_b1", "L0_ffn_w2", "L0_ffn_b2",
       "L1_gnn_W", "L1_gnn_a_src", "L1_gnn_a_dst", "L1_gnn_bias_gat", "L1_gnn_W_res", "L1_gnn_b_res",
       "L1_gnn_gamma", "L1_gnn_beta",
       "L1_ffn_gate_w", "L1_ffn_gate_b", "L1_ffn_w1", "L1_ffn_b1", "L1_ffn_w2", "L1_ffn_b2"]


def kernel(**inputs):
    import numpy as _np
    import concourse.bacc as _bacc
    from concourse.bass_utils import run_bass_kernel_spmd as _run

    nc = _bacc.Bacc("TRN2", target_bir_lowering=False, num_devices=1)
    arrays, aps = {}, {}
    for name in INS:
        v = _np.ascontiguousarray(inputs[name])
        if name == "x":
            v = _np.concatenate([v, _np.zeros((NB * P - NODES, D), v.dtype)])
        if name in ("src", "dst"):
            pad = _np.full(NGP * GROUP - EDGES, PAD_DST if name == "dst" else 0, v.dtype)
            v = _np.concatenate([v, pad]).reshape(NGP, GROUP)
        if name in ("L1_ffn_w1", "L1_ffn_w2"):
            v = v.reshape(-1, v.shape[-1])
        arrays[f"in_{name}"] = v
        aps[name] = nc.dram_tensor(f"in_{name}", v.shape, mybir.dt.from_np(v.dtype), kind="ExternalInput").ap()
    out = nc.dram_tensor("out_0", (NODES, D), F32, kind="ExternalOutput").ap()
    program(nc, aps, out)
    r = _run(nc, [arrays], core_ids=[0])
    return r.results[0]["out_0"]
```
